# Optimizing a Trainium2 kernel written in Bass

```python
import numpy as np
import jax
import jax.numpy as jnp

def _softmax(x, axis=-1):
    return jax.nn.softmax(x, axis=axis)

def _gelu(x):
    return jax.nn.gelu(x, approximate=True)

def _silu(x):
    return jax.nn.silu(x)

def _sigmoid(x):
    return jax.nn.sigmoid(x)

def _layernorm(x, axis=-1, eps=1e-05):
    m = jnp.mean(x, axis=axis, keepdims=True)
    v = jnp.var(x, axis=axis, keepdims=True)
    return (x - m) / jnp.sqrt(v + eps)

def _scatter_add(tgt, idx, src, axis=0):
    return tgt.at[idx].add(src)

def _segment_sum(src, seg, n):
    return jax.ops.segment_sum(src, seg, n)
kernel_name = 'mk_gps_d4_gnn_r32_0f34b1'

def setup_inputs(seed: int=0):
    np.random.seed(seed)
    _w = jnp.asarray

    def _rec_inputs():
        import jax
        import jax.numpy as jnp
        _gk = jax.random.key(seed)
        x = -0.000125 + 0.9999 * jax.random.normal(jax.random.fold_in(_gk, 1), (2048, 512), jnp.float32)
        _s = jax.random.randint(jax.random.fold_in(_gk, 2), (16384,), 0, 2048, jnp.int32)
        _d = jax.random.randint(jax.random.fold_in(_gk, 3), (16384,), 0, 2048, jnp.int32)
        _loop = jnp.arange(2048, dtype=jnp.int32)
        src = jnp.concatenate([_s, _d, _loop])
        dst = jnp.concatenate([_d, _s, _loop])
        _o = jnp.argsort(dst, stable=True)
        src = src[_o]
        dst = dst[_o]
        return (x, src, dst)
    x, src, dst = _rec_inputs()

    def _L0_gnn_setup():
        import jax, jax.numpy as jnp
        import numpy as np
        N = 2048
        F = 512
        H = 512
        E = 16384
        key = jax.random.key(seed)
        ks = jax.random.split(key, 12)
        s = 0.02
        return {'x': jax.random.normal(ks[0], (N, F), dtype=jnp.float32), 'edge_index': jax.random.randint(ks[1], (2, E), 0, N, dtype=jnp.int64), 'W_rel1': jax.random.normal(ks[2], (H, F), dtype=jnp.float32) * s, 'b_rel1': jnp.zeros((H,), dtype=jnp.float32), 'W_root1': jax.random.normal(ks[3], (H, F), dtype=jnp.float32) * s, 'W_lin1': jax.random.normal(ks[4], (H, H), dtype=jnp.float32) * s, 'b_lin1': jnp.zeros((H,), dtype=jnp.float32), 'W_rel2': jax.random.normal(ks[5], (H, H), dtype=jnp.float32) * s, 'b_rel2': jnp.zeros((H,), dtype=jnp.float32), 'W_root2': jax.random.normal(ks[6], (H, H), dtype=jnp.float32) * s, 'W_lin2': jax.random.normal(ks[7], (H, H), dtype=jnp.float32) * s, 'b_lin2': jnp.zeros((H,), dtype=jnp.float32)}
    _L0_gnn_all = _L0_gnn_setup()
    _L0_gnn_in = {k: v for k, v in _L0_gnn_all.items() if k in ('W_rel1', 'b_rel1', 'W_root1', 'W_lin1', 'b_lin1', 'W_rel2', 'b_rel2', 'W_root2', 'W_lin2', 'b_lin2')}
    del _L0_gnn_all

    def _L0_mix_setup():
        import jax, jax.numpy as jnp
        import numpy as np
        B, L, HID, H, FF = (32, 1024, 512, 8, 64)
        DH = HID // H
        KEPS = 0.001
        LN_EPS = 1e-06

        def _layernorm(x, scale, bias):
            mu = jnp.mean(x, axis=-1, keepdims=True)
            var = jnp.mean(jnp.square(x - mu), axis=-1, keepdims=True)
            return (x - mu) * jax.lax.rsqrt(var + LN_EPS) * scale + bias

        def _favor_bidirectional(q, k, v):
            qp = jax.nn.relu(q) + KEPS
            kp = jax.nn.relu(k) + KEPS
            kv = jnp.einsum('blhm,blhd->bhmd', kp, v)
            num = jnp.einsum('blhm,bhmd->blhd', qp, kv)
            den = jnp.einsum('blhm,bhm->blh', qp, kp.sum(axis=1))
            return num / den[..., None]
        key = jax.random.key(seed)
        ks = jax.random.split(key, 12)
        sa = 1.0 / np.sqrt(HID)
        sf = 1.0 / np.sqrt(FF)
        return {'x': jax.random.normal(ks[0], (B, L, HID), jnp.float32), 'Wq': jax.random.normal(ks[1], (HID, H, DH), jnp.float32) * sa, 'bq': jnp.zeros((H, DH), jnp.float32), 'Wk': jax.random.normal(ks[2], (HID, H, DH), jnp.float32) * sa, 'bk': jnp.zeros((H, DH), jnp.float32), 'Wv': jax.random.normal(ks[3], (HID, H, DH), jnp.float32) * sa, 'bv': jnp.zeros((H, DH), jnp.float32), 'Wo': jax.random.normal(ks[4], (H, DH, HID), jnp.float32) * sa, 'bo': jnp.zeros((HID,), jnp.float32), 'ln1_scale': jnp.ones((HID,), jnp.float32), 'ln1_bias': jnp.zeros((HID,), jnp.float32), 'W1': jax.random.normal(ks[5], (HID, FF), jnp.float32) * sa, 'b1': jnp.zeros((FF,), jnp.float32), 'W2': jax.random.normal(ks[6], (FF, HID), jnp.float32) * sf, 'b2': jnp.zeros((HID,), jnp.float32), 'ln2_scale': jnp.ones((HID,), jnp.float32), 'ln2_bias': jnp.zeros((HID,), jnp.float32)}
    _L0_mix_all = _L0_mix_setup()
    _L0_mix_in = {k: v for k, v in _L0_mix_all.items() if k in ('Wq', 'bq', 'Wk', 'bk', 'Wv', 'bv', 'Wo', 'bo', 'ln1_scale', 'ln1_bias', 'W1', 'b1', 'W2', 'b2', 'ln2_scale', 'ln2_bias')}
    del _L0_mix_all

    def _L0_ffn_setup():
        import jax, jax.numpy as jnp
        import numpy as np
        import math
        B, T, D, H, E, TOPK = (8, 128, 512, 64, 8, 2)
        CAP_FRAC = 1.0

        def _expert_ffn(x, w1, w2, w3):
            h = jax.nn.gelu(x @ w2 * (x @ w1), approximate=False)
            return h @ w3
        key = jax.random.key(seed)
        ks = jax.random.split(key, 6)
        x = jax.random.normal(ks[0], (B, T, D), dtype=jnp.float32)
        Wr = jax.random.normal(ks[1], (D, E), dtype=jnp.float32) * 0.02
        br = jnp.zeros((E,), dtype=jnp.float32)
        W1 = jax.random.normal(ks[2], (E, D, H), dtype=jnp.float32) * 0.02
        W2 = jax.random.normal(ks[3], (E, D, H), dtype=jnp.float32) * 0.02
        W3 = jax.random.normal(ks[4], (E, H, D), dtype=jnp.float32) * 0.02
        return {'x': x, 'Wr': Wr, 'br': br, 'W1': W1, 'W2': W2, 'W3': W3}
    _L0_ffn_all = _L0_ffn_setup()
    _L0_ffn_in = {k: v for k, v in _L0_ffn_all.items() if k in ('Wr', 'br', 'W1', 'W2', 'W3')}
    del _L0_ffn_all

    def _L1_gnn_setup():
        import jax, jax.numpy as jnp
        import numpy as np
        D = 512
        H = 8
        DH = D // H
        F = 64
        L = 2
        N = 625
        E = 10000
        EPS = 1e-05

        def _xavier(key, shape):
            fan_out, fan_in = (shape[-2], shape[-1])
            lim = float(np.sqrt(6.0 / (fan_in + fan_out)))
            return jax.random.uniform(key, shape, jnp.float32, -lim, lim)

        def _batchnorm(x, g, b):
            mu = jnp.mean(x, axis=0)
            var = jnp.mean(jnp.square(x - mu), axis=0)
            return (x - mu) * jax.lax.rsqrt(var + EPS) * g + b

        def _layernorm(x, g, b):
            mu = jnp.mean(x, axis=-1, keepdims=True)
            var = jnp.mean(jnp.square(x - mu), axis=-1, keepdims=True)
            return (x - mu) * jax.lax.rsqrt(var + EPS) * g + b
        key = jax.random.key(seed)
        ks = jax.random.split(key, 12)
        src = jax.random.normal(ks[0], (N, D), jnp.float32)
        edge_index = jax.random.randint(ks[1], (2, E), 0, N)
        return {'src': src, 'edge_index': edge_index, 'Wq': _xavier(ks[2], (L, D, D)), 'bq': jnp.zeros((L, D), jnp.float32), 'Wk': _xavier(ks[3], (L, D, D)), 'Wv': _xavier(ks[4], (L, D, D)), 'Wo': _xavier(ks[5], (L, D, D)), 'bo': jnp.zeros((L, D), jnp.float32), 'W1': _xavier(ks[6], (L, F, D)), 'b1': jnp.zeros((L, F), jnp.float32), 'W2': _xavier(ks[7], (L, D, F)), 'b2': jnp.zeros((L, D), jnp.float32), 'g1': jnp.ones((L, D), jnp.float32), 'beta1': jnp.zeros((L, D), jnp.float32), 'g2': jnp.ones((L, D), jnp.float32), 'beta2': jnp.zeros((L, D), jnp.float32), 'ln_g': jnp.ones((D,), jnp.float32), 'ln_b': jnp.zeros((D,), jnp.float32)}
    _L1_gnn_all = _L1_gnn_setup()
    _L1_gnn_in = {k: v for k, v in _L1_gnn_all.items() if k in ('Wq', 'bq', 'Wk', 'Wv', 'Wo', 'bo', 'W1', 'b1', 'W2', 'b2', 'g1', 'beta1', 'g2', 'beta2', 'ln_g', 'ln_b')}
    del _L1_gnn_all

    def _L1_mix_setup():
        import jax, jax.numpy as jnp
        import numpy as np
        B, N, C = (8, 128, 512)
        key = jax.random.key(seed)
        ks = jax.random.split(key, 6)
        s = 1.0 / np.sqrt(C)
        return {'x': jax.random.normal(ks[0], (B, N, C), jnp.float32), 'Wq': jax.random.normal(ks[1], (C, C), jnp.float32) * s, 'Wk': jax.random.normal(ks[2], (C, C), jnp.float32) * s, 'Wv': jax.random.normal(ks[3], (C, C), jnp.float32) * s, 'W1': jax.random.normal(ks[4], (C, C), jnp.float32) * s, 'W2': jax.random.normal(ks[5], (C, C), jnp.float32) * s}
    _L1_mix_all = _L1_mix_setup()
    _L1_mix_in = {k: v for k, v in _L1_mix_all.items() if k in ('Wq', 'Wk', 'Wv', 'W1', 'W2')}
    del _L1_mix_all

    def _L1_ffn_setup():
        import jax, jax.numpy as jnp
        import numpy as np
        TOP_K = 2
        key = jax.random.key(seed)
        ks = jax.random.split(key, 6)
        B, T, C, E, H = (4, 128, 512, 8, 64)
        x = jax.random.normal(ks[0], (B, T, C), dtype=jnp.float32)
        W_router = jax.random.normal(ks[1], (C, E), dtype=jnp.float32) * 0.02
        W1 = jax.random.normal(ks[2], (E, C, H), dtype=jnp.float32) * 0.02
        b1 = jnp.zeros((E, H), dtype=jnp.float32)
        W2 = jax.random.normal(ks[3], (E, H, C), dtype=jnp.float32) * 0.02
        b2 = jnp.zeros((E, C), dtype=jnp.float32)
        return {'x': x, 'W_router': W_router, 'W1': W1, 'b1': b1, 'W2': W2, 'b2': b2}
    _L1_ffn_all = _L1_ffn_setup()
    _L1_ffn_in = {k: v for k, v in _L1_ffn_all.items() if k in ('W_router', 'W1', 'b1', 'W2', 'b2')}
    del _L1_ffn_all

    def _L2_gnn_setup():
        import jax, jax.numpy as jnp
        import numpy as np
        N = 50000
        E = 12500
        D_IN = 512
        D_HID = 64
        D_OUT = 512
        key = jax.random.key(seed)
        k1, k2, k3, k4 = jax.random.split(key, 4)
        x = jax.random.normal(k1, (N, D_IN), dtype=jnp.float32)
        edge_index = jax.random.randint(k2, (2, E), 0, N, dtype=jnp.int64)
        W1 = jax.random.normal(k3, (D_IN, D_HID), dtype=jnp.float32) * (1.0 / np.sqrt(D_IN))
        b1 = jnp.zeros((D_HID,), dtype=jnp.float32)
        W2 = jax.random.normal(k4, (D_HID, D_OUT), dtype=jnp.float32) * (1.0 / np.sqrt(D_HID))
        b2 = jnp.zeros((D_OUT,), dtype=jnp.float32)
        return {'x': x, 'edge_index': edge_index, 'W1': W1, 'b1': b1, 'W2': W2, 'b2': b2}
    _L2_gnn_all = _L2_gnn_setup()
    _L2_gnn_in = {k: v for k, v in _L2_gnn_all.items() if k in ('W1', 'b1', 'W2', 'b2')}
    del _L2_gnn_all

    def _L2_mix_setup():
        import jax, jax.numpy as jnp
        import numpy as np
        HEADS = 8
        EPS_LN = 1e-05
        EPS_NORM = 1e-08
        key = jax.random.key(seed)
        ks = jax.random.split(key, 3)
        B, N, C = (4, 256, 512)
        x = jax.random.normal(ks[0], (B, N, C), dtype=jnp.float32)
        qkv_w = jax.random.normal(ks[1], (3 * C, C), dtype=jnp.float32) / np.sqrt(C)
        qkv_b = jnp.zeros((3 * C,), dtype=jnp.float32)
        out_w = jax.random.normal(ks[2], (C, C), dtype=jnp.float32) / np.sqrt(C)
        out_b = jnp.zeros((C,), dtype=jnp.float32)
        ln_gamma = jnp.ones((C,), dtype=jnp.float32)
        ln_beta = jnp.zeros((C,), dtype=jnp.float32)
        return {'x': x, 'qkv_w': qkv_w, 'qkv_b': qkv_b, 'out_w': out_w, 'out_b': out_b, 'ln_gamma': ln_gamma, 'ln_beta': ln_beta}
    _L2_mix_all = _L2_mix_setup()
    _L2_mix_in = {k: v for k, v in _L2_mix_all.items() if k in ('qkv_w', 'qkv_b', 'out_w', 'out_b', 'ln_gamma', 'ln_beta')}
    del _L2_mix_all

    def _L2_ffn_setup():
        import jax, jax.numpy as jnp
        import numpy as np
        NUM_EXPERTS = 8
        TOP_K = 2
        key = jax.random.key(seed)
        k0, k1, k2, k3, k4 = jax.random.split(key, 5)
        sl, bs, hs, ffn = (64, 2, 512, 64)
        T = sl * bs
        x = jax.random.normal(k0, (sl, bs, hs), jnp.float32)
        expert_weights = jax.random.uniform(k1, (T, TOP_K), jnp.float32)
        expert_indices = jax.random.randint(k2, (T, TOP_K), 0, NUM_EXPERTS)
        w1 = jax.random.normal(k3, (NUM_EXPERTS, hs, ffn), jnp.float32) * hs ** (-0.5)
        w2 = jax.random.normal(k4, (NUM_EXPERTS, ffn, hs), jnp.float32) * ffn ** (-0.5)
        return dict(x=x, expert_weights=expert_weights, expert_indices=expert_indices, w1=w1, w2=w2)
    _L2_ffn_all = _L2_ffn_setup()
    _L2_ffn_in = {k: v for k, v in _L2_ffn_all.items() if k in ('expert_weights', 'expert_indices', 'w1', 'w2')}
    del _L2_ffn_all

    def _L3_gnn_setup():
        import jax, jax.numpy as jnp
        import numpy as np
        N_NODES = 50000
        N_EDGES = 46875
        D = 512
        LN_EPS = 1e-05

        def _layer_norm(x, gamma, beta):
            mu = jnp.mean(x, axis=-1, keepdims=True)
            var = jnp.mean(jnp.square(x - mu), axis=-1, keepdims=True)
            return (x - mu) * jax.lax.rsqrt(var + LN_EPS) * gamma + beta
        key = jax.random.key(seed)
        ks = jax.random.split(key, 8)
        scale = 1.0 / np.sqrt(D)
        return {'node_feature': jax.random.normal(ks[0], (N_NODES, D), dtype=jnp.float32), 'edge_index': jax.random.randint(ks[1], (2, N_EDGES), 0, N_NODES, dtype=jnp.int32), 'W_l': jax.random.uniform(ks[2], (D, D), jnp.float32, -scale, scale), 'b_l': jnp.zeros((D,), jnp.float32), 'W_r': jax.random.uniform(ks[3], (D, D), jnp.float32, -scale, scale), 'gamma': jnp.ones((D,), jnp.float32), 'beta': jnp.zeros((D,), jnp.float32)}
    _L3_gnn_all = _L3_gnn_setup()
    _L3_gnn_in = {k: v for k, v in _L3_gnn_all.items() if k in ('W_l', 'b_l', 'W_r', 'gamma', 'beta')}
    del _L3_gnn_all

    def _L3_mix_setup():
        import jax, jax.numpy as jnp
        import numpy as np
        B, N, D_MODEL = (4, 256, 512)
        N_HEAD, D_HEAD = (8, 64)
        NB_FEAT = 266
        MLP_DIM = 1024

        def _layernorm(x, g, b, eps=1e-05):
            m = jnp.mean(x, -1, keepdims=True)
            v = jnp.var(x, -1, keepdims=True)
            return (x - m) * jax.lax.rsqrt(v + eps) * g + b

        def _softmax_kernel(data, proj, is_query, eps=0.0001):
            norm = data.shape[-1] ** (-0.25)
            ratio = proj.shape[0] ** (-0.5)
            dd = jnp.einsum('bhnd,rd->bhnr', data * norm, proj)
            diag = 0.5 * jnp.sum((data * norm) ** 2, axis=-1, keepdims=True)
            if is_query:
                stab = jnp.max(dd, axis=-1, keepdims=True)
            else:
                stab = jnp.max(dd)
            return ratio * (jnp.exp(dd - diag - stab) + eps)

        def _fast_attention_block(x, Wq, Wk, Wv, Wo, bo, proj, ln0_g, ln0_b, W1, b1, W2, b2, ln1_g, ln1_b):
            b, n, d = x.shape
            h, dh = (N_HEAD, d // N_HEAD)
            split = lambda t: t.reshape(b, n, h, dh).transpose(0, 2, 1, 3)
            q = split(x @ Wq)
            k = split(x @ Wk)
            v = split(x @ Wv)
            qp = _softmax_kernel(q, proj, is_query=True)
            kp = _softmax_kernel(k, proj, is_query=False)
            ksum = jnp.sum(kp, axis=2)
            d_inv = 1.0 / jnp.einsum('bhnr,bhr->bhn', qp, ksum)
            ctx = jnp.einsum('bhnr,bhnd->bhrd', kp, v)
            out = jnp.einsum('bhnr,bhrd,bhn->bhnd', qp, ctx, d_inv)
            out = out.transpose(0, 2, 1, 3).reshape(b, n, d) @ Wo + bo
            hdd = _layernorm(x + out, ln0_g, ln0_b)
            mlp = jax.nn.gelu(hdd @ W1 + b1, approximate=False) @ W2 + b2
            return _layernorm(hdd + mlp, ln1_g, ln1_b)
        key = jax.random.key(seed)
        ks = jax.random.split(key, 10)
        s = lambda k, shape: jax.random.normal(k, shape, jnp.float32) * 0.02
        return {'x': jax.random.normal(ks[0], (B, N, D_MODEL), jnp.float32), 'Wq': s(ks[1], (D_MODEL, D_MODEL)), 'Wk': s(ks[2], (D_MODEL, D_MODEL)), 'Wv': s(ks[3], (D_MODEL, D_MODEL)), 'Wo': s(ks[4], (D_MODEL, D_MODEL)), 'bo': jnp.zeros((D_MODEL,), jnp.float32), 'proj': jax.random.normal(ks[5], (NB_FEAT, D_HEAD), jnp.float32), 'ln0_g': jnp.ones((D_MODEL,), jnp.float32), 'ln0_b': jnp.zeros((D_MODEL,), jnp.float32), 'W1': s(ks[6], (D_MODEL, MLP_DIM)), 'b1': jnp.zeros((MLP_DIM,), jnp.float32), 'W2': s(ks[7], (MLP_DIM, D_MODEL)), 'b2': jnp.zeros((D_MODEL,), jnp.float32), 'ln1_g': jnp.ones((D_MODEL,), jnp.float32), 'ln1_b': jnp.zeros((D_MODEL,), jnp.float32)}
    _L3_mix_all = _L3_mix_setup()
    _L3_mix_in = {k: v for k, v in _L3_mix_all.items() if k in ('Wq', 'Wk', 'Wv', 'Wo', 'bo', 'proj', 'ln0_g', 'ln0_b', 'W1', 'b1', 'W2', 'b2', 'ln1_g', 'ln1_b')}
    del _L3_mix_all

    def _L3_ffn_setup():
        import jax, jax.numpy as jnp
        import numpy as np
        DIM = 512
        FFN_DIM = 1408
        GROUP = 128
        EPS = 1e-05

        def _quantize_weight(w, group_size):
            o, i = w.shape
            wg = w.reshape(o, i // group_size, group_size)
            scale = jnp.mean(jnp.abs(wg), axis=-1, keepdims=True) + EPS
            wq = jnp.clip(jnp.round(wg / scale), -1.0, 1.0) * scale
            return wq.reshape(o, i)

        def _bitlinear(x, w, group_size=GROUP):
            wq = w + jax.lax.stop_gradient(_quantize_weight(w, group_size) - w)
            return jnp.einsum('bsd,fd->bsf', x, wq)
        key = jax.random.key(seed)
        k_x, k_g, k_u, k_d = jax.random.split(key, 4)
        x = jax.random.normal(k_x, (8, 128, DIM), dtype=jnp.float32)
        sd_in = 1.0 / np.sqrt(DIM)
        sd_ffn = 1.0 / np.sqrt(FFN_DIM)
        w_gate = jax.random.normal(k_g, (FFN_DIM, DIM), dtype=jnp.float32) * sd_in
        w_up = jax.random.normal(k_u, (FFN_DIM, DIM), dtype=jnp.float32) * sd_in
        w_down = jax.random.normal(k_d, (DIM, FFN_DIM), dtype=jnp.float32) * sd_ffn
        return {'x': x, 'w_gate': w_gate, 'w_up': w_up, 'w_down': w_down}
    _L3_ffn_all = _L3_ffn_setup()
    _L3_ffn_in = {k: v for k, v in _L3_ffn_all.items() if k in ('w_gate', 'w_up', 'w_down')}
    del _L3_ffn_all
    return {'x': x, 'src': src, 'dst': dst, 'L0_gnn_W_rel1': _L0_gnn_in['W_rel1'], 'L0_gnn_b_rel1': _L0_gnn_in['b_rel1'], 'L0_gnn_W_root1': _L0_gnn_in['W_root1'], 'L0_gnn_W_lin1': _L0_gnn_in['W_lin1'], 'L0_gnn_b_lin1': _L0_gnn_in['b_lin1'], 'L0_gnn_W_rel2': _L0_gnn_in['W_rel2'], 'L0_gnn_b_rel2': _L0_gnn_in['b_rel2'], 'L0_gnn_W_root2': _L0_gnn_in['W_root2'], 'L0_gnn_W_lin2': _L0_gnn_in['W_lin2'], 'L0_gnn_b_lin2': _L0_gnn_in['b_lin2'], 'L0_mix_Wq': _L0_mix_in['Wq'], 'L0_mix_bq': _L0_mix_in['bq'], 'L0_mix_Wk': _L0_mix_in['Wk'], 'L0_mix_bk': _L0_mix_in['bk'], 'L0_mix_Wv': _L0_mix_in['Wv'], 'L0_mix_bv': _L0_mix_in['bv'], 'L0_mix_Wo': _L0_mix_in['Wo'], 'L0_mix_bo': _L0_mix_in['bo'], 'L0_mix_ln1_scale': _L0_mix_in['ln1_scale'], 'L0_mix_ln1_bias': _L0_mix_in['ln1_bias'], 'L0_mix_W1': _L0_mix_in['W1'], 'L0_mix_b1': _L0_mix_in['b1'], 'L0_mix_W2': _L0_mix_in['W2'], 'L0_mix_b2': _L0_mix_in['b2'], 'L0_mix_ln2_scale': _L0_mix_in['ln2_scale'], 'L0_mix_ln2_bias': _L0_mix_in['ln2_bias'], 'L0_ffn_Wr': _L0_ffn_in['Wr'], 'L0_ffn_br': _L0_ffn_in['br'], 'L0_ffn_W1': _L0_ffn_in['W1'], 'L0_ffn_W2': _L0_ffn_in['W2'], 'L0_ffn_W3': _L0_ffn_in['W3'], 'L1_gnn_Wq': _L1_gnn_in['Wq'], 'L1_gnn_bq': _L1_gnn_in['bq'], 'L1_gnn_Wk': _L1_gnn_in['Wk'], 'L1_gnn_Wv': _L1_gnn_in['Wv'], 'L1_gnn_Wo': _L1_gnn_in['Wo'], 'L1_gnn_bo': _L1_gnn_in['bo'], 'L1_gnn_W1': _L1_gnn_in['W1'], 'L1_gnn_b1': _L1_gnn_in['b1'], 'L1_gnn_W2': _L1_gnn_in['W2'], 'L1_gnn_b2': _L1_gnn_in['b2'], 'L1_gnn_g1': _L1_gnn_in['g1'], 'L1_gnn_beta1': _L1_gnn_in['beta1'], 'L1_gnn_g2': _L1_gnn_in['g2'], 'L1_gnn_beta2': _L1_gnn_in['beta2'], 'L1_gnn_ln_g': _L1_gnn_in['ln_g'], 'L1_gnn_ln_b': _L1_gnn_in['ln_b'], 'L1_mix_Wq': _L1_mix_in['Wq'], 'L1_mix_Wk': _L1_mix_in['Wk'], 'L1_mix_Wv': _L1_mix_in['Wv'], 'L1_mix_W1': _L1_mix_in['W1'], 'L1_mix_W2': _L1_mix_in['W2'], 'L1_ffn_W_router': _L1_ffn_in['W_router'], 'L1_ffn_W1': _L1_ffn_in['W1'], 'L1_ffn_b1': _L1_ffn_in['b1'], 'L1_ffn_W2': _L1_ffn_in['W2'], 'L1_ffn_b2': _L1_ffn_in['b2'], 'L2_gnn_W1': _L2_gnn_in['W1'], 'L2_gnn_b1': _L2_gnn_in['b1'], 'L2_gnn_W2': _L2_gnn_in['W2'], 'L2_gnn_b2': _L2_gnn_in['b2'], 'L2_mix_qkv_w': _L2_mix_in['qkv_w'], 'L2_mix_qkv_b': _L2_mix_in['qkv_b'], 'L2_mix_out_w': _L2_mix_in['out_w'], 'L2_mix_out_b': _L2_mix_in['out_b'], 'L2_mix_ln_gamma': _L2_mix_in['ln_gamma'], 'L2_mix_ln_beta': _L2_mix_in['ln_beta'], 'L2_ffn_expert_weights': _L2_ffn_in['expert_weights'], 'L2_ffn_expert_indices': _L2_ffn_in['expert_indices'], 'L2_ffn_w1': _L2_ffn_in['w1'], 'L2_ffn_w2': _L2_ffn_in['w2'], 'L3_gnn_W_l': _L3_gnn_in['W_l'], 'L3_gnn_b_l': _L3_gnn_in['b_l'], 'L3_gnn_W_r': _L3_gnn_in['W_r'], 'L3_gnn_gamma': _L3_gnn_in['gamma'], 'L3_gnn_beta': _L3_gnn_in['beta'], 'L3_mix_Wq': _L3_mix_in['Wq'], 'L3_mix_Wk': _L3_mix_in['Wk'], 'L3_mix_Wv': _L3_mix_in['Wv'], 'L3_mix_Wo': _L3_mix_in['Wo'], 'L3_mix_bo': _L3_mix_in['bo'], 'L3_mix_proj': _L3_mix_in['proj'], 'L3_mix_ln0_g': _L3_mix_in['ln0_g'], 'L3_mix_ln0_b': _L3_mix_in['ln0_b'], 'L3_mix_W1': _L3_mix_in['W1'], 'L3_mix_b1': _L3_mix_in['b1'], 'L3_mix_W2': _L3_mix_in['W2'], 'L3_mix_b2': _L3_mix_in['b2'], 'L3_mix_ln1_g': _L3_mix_in['ln1_g'], 'L3_mix_ln1_b': _L3_mix_in['ln1_b'], 'L3_ffn_w_gate': _L3_ffn_in['w_gate'], 'L3_ffn_w_up': _L3_ffn_in['w_up'], 'L3_ffn_w_down': _L3_ffn_in['w_down']}

def reference(x, src, dst, L0_gnn_W_rel1, L0_gnn_b_rel1, L0_gnn_W_root1, L0_gnn_W_lin1, L0_gnn_b_lin1, L0_gnn_W_rel2, L0_gnn_b_rel2, L0_gnn_W_root2, L0_gnn_W_lin2, L0_gnn_b_lin2, L0_mix_Wq, L0_mix_bq, L0_mix_Wk, L0_mix_bk, L0_mix_Wv, L0_mix_bv, L0_mix_Wo, L0_mix_bo, L0_mix_ln1_scale, L0_mix_ln1_bias, L0_mix_W1, L0_mix_b1, L0_mix_W2, L0_mix_b2, L0_mix_ln2_scale, L0_mix_ln2_bias, L0_ffn_Wr, L0_ffn_br, L0_ffn_W1, L0_ffn_W2, L0_ffn_W3, L1_gnn_Wq, L1_gnn_bq, L1_gnn_Wk, L1_gnn_Wv, L1_gnn_Wo, L1_gnn_bo, L1_gnn_W1, L1_gnn_b1, L1_gnn_W2, L1_gnn_b2, L1_gnn_g1, L1_gnn_beta1, L1_gnn_g2, L1_gnn_beta2, L1_gnn_ln_g, L1_gnn_ln_b, L1_mix_Wq, L1_mix_Wk, L1_mix_Wv, L1_mix_W1, L1_mix_W2, L1_ffn_W_router, L1_ffn_W1, L1_ffn_b1, L1_ffn_W2, L1_ffn_b2, L2_gnn_W1, L2_gnn_b1, L2_gnn_W2, L2_gnn_b2, L2_mix_qkv_w, L2_mix_qkv_b, L2_mix_out_w, L2_mix_out_b, L2_mix_ln_gamma, L2_mix_ln_beta, L2_ffn_expert_weights, L2_ffn_expert_indices, L2_ffn_w1, L2_ffn_w2, L3_gnn_W_l, L3_gnn_b_l, L3_gnn_W_r, L3_gnn_gamma, L3_gnn_beta, L3_mix_Wq, L3_mix_Wk, L3_mix_Wv, L3_mix_Wo, L3_mix_bo, L3_mix_proj, L3_mix_ln0_g, L3_mix_ln0_b, L3_mix_W1, L3_mix_b1, L3_mix_W2, L3_mix_b2, L3_mix_ln1_g, L3_mix_ln1_b, L3_ffn_w_gate, L3_ffn_w_up, L3_ffn_w_down):
    import jax
    import jax.numpy as jnp

    def _L0_gnn_ref(x, edge_index, W_rel1, b_rel1, W_root1, W_lin1, b_lin1, W_rel2, b_rel2, W_root2, W_lin2, b_lin2):
        import jax, jax.numpy as jnp
        import numpy as np
        N = 2048
        F = 512
        H = 512
        E = 16384
        src, dst = (edge_index[0], edge_index[1])

        def graph_conv(h, W_rel, b_rel, W_root):
            agg = jax.ops.segment_sum(h[src], dst, num_segments=N)
            return agg @ W_rel.T + b_rel + h @ W_root.T
        h = jax.nn.relu(graph_conv(x, W_rel1, b_rel1, W_root1) @ W_lin1.T + b_lin1)
        h = jax.nn.relu(graph_conv(h, W_rel2, b_rel2, W_root2) @ W_lin2.T + b_lin2)
        return h

    def _L0_mix_ref(x, Wq, bq, Wk, bk, Wv, bv, Wo, bo, ln1_scale, ln1_bias, W1, b1, W2, b2, ln2_scale, ln2_bias):
        import jax, jax.numpy as jnp
        import numpy as np
        B, L, HID, H, FF = (32, 1024, 512, 8, 64)
        DH = HID // H
        KEPS = 0.001
        LN_EPS = 1e-06

        def _layernorm(x, scale, bias):
            mu = jnp.mean(x, axis=-1, keepdims=True)
            var = jnp.mean(jnp.square(x - mu), axis=-1, keepdims=True)
            return (x - mu) * jax.lax.rsqrt(var + LN_EPS) * scale + bias

        def _favor_bidirectional(q, k, v):
            qp = jax.nn.relu(q) + KEPS
            kp = jax.nn.relu(k) + KEPS
            kv = jnp.einsum('blhm,blhd->bhmd', kp, v)
            num = jnp.einsum('blhm,bhmd->blhd', qp, kv)
            den = jnp.einsum('blhm,bhm->blh', qp, kp.sum(axis=1))
            return num / den[..., None]
        q = jnp.einsum('blc,chd->blhd', x, Wq) + bq
        k = jnp.einsum('blc,chd->blhd', x, Wk) + bk
        v = jnp.einsum('blc,chd->blhd', x, Wv) + bv
        attn = _favor_bidirectional(q, k, v)
        attended = jnp.einsum('blhd,hdc->blc', attn, Wo) + bo
        h = _layernorm(attended + x, ln1_scale, ln1_bias)
        ff = jax.nn.relu(h @ W1 + b1) @ W2 + b2
        return _layernorm(ff + h, ln2_scale, ln2_bias)

    def _L0_ffn_ref(x, Wr, br, W1, W2, W3):
        import jax, jax.numpy as jnp
        import numpy as np
        import math
        B, T, D, H, E, TOPK = (8, 128, 512, 64, 8, 2)
        CAP_FRAC = 1.0

        def _expert_ffn(x, w1, w2, w3):
            h = jax.nn.gelu(x @ w2 * (x @ w1), approximate=False)
            return h @ w3
        b, t, d = x.shape
        Bt = b * t
        x_flat = x.reshape(Bt, d)
        logits = x_flat.astype(jnp.float32) @ Wr + br
        vals, idx = jax.lax.top_k(logits, TOPK)
        scores = jax.nn.softmax(vals, axis=-1).astype(x.dtype).reshape(b, t, TOPK)
        onehot = jax.nn.one_hot(idx, E, dtype=jnp.float32)
        pos = jnp.cumsum(jnp.cumsum(onehot, axis=0), axis=1).astype(jnp.int32)
        capacity = math.floor(Bt * CAP_FRAC)
        mask3 = onehot * (pos < capacity)
        token_mask = mask3.sum(-1).reshape(b, t, TOPK)
        assign = jnp.einsum('tke,e->tk', mask3, jnp.arange(E, dtype=jnp.float32)).astype(jnp.int32)
        i_max = assign.reshape(b, t, TOPK).max(axis=-1)
        y = jnp.zeros_like(x)
        for i in range(E):
            yi = _expert_ffn(x, W1[i], W2[i], W3[i])
            y = jnp.where((i_max == i)[..., None], yi, y)
        expert_outputs = jnp.where(token_mask[..., None] > 0, y[:, :, None, :], x[:, :, None, :])
        return jnp.einsum('btkD,btk->btD', expert_outputs, scores)

    def _L1_gnn_ref(src, edge_index, Wq, bq, Wk, Wv, Wo, bo, W1, b1, W2, b2, g1, beta1, g2, beta2, ln_g, ln_b):
        import jax, jax.numpy as jnp
        import numpy as np
        D = 512
        H = 8
        DH = D // H
        F = 64
        L = 2
        N = 625
        E = 10000
        EPS = 1e-05

        def _xavier(key, shape):
            fan_out, fan_in = (shape[-2], shape[-1])
            lim = float(np.sqrt(6.0 / (fan_in + fan_out)))
            return jax.random.uniform(key, shape, jnp.float32, -lim, lim)

        def _batchnorm(x, g, b):
            mu = jnp.mean(x, axis=0)
            var = jnp.mean(jnp.square(x - mu), axis=0)
            return (x - mu) * jax.lax.rsqrt(var + EPS) * g + b

        def _layernorm(x, g, b):
            mu = jnp.mean(x, axis=-1, keepdims=True)
            var = jnp.mean(jnp.square(x - mu), axis=-1, keepdims=True)
            return (x - mu) * jax.lax.rsqrt(var + EPS) * g + b
        n = src.shape[0]
        scaling = float(DH) ** (-0.5)
        tgt = edge_index[1]
        srcidx = edge_index[0]
        x = src
        for l in range(L):
            q = ((x @ Wq[l].T + bq[l]) * scaling).reshape(n, H, DH)
            k = (x @ Wk[l].T).reshape(n, H, DH)
            v = (x @ Wv[l].T).reshape(n, H, DH)
            scores = jnp.einsum('ehd,ehd->eh', q[tgt], k[srcidx])
            m = jax.ops.segment_max(scores, tgt, num_segments=n)
            p = jnp.exp(scores - m[tgt])
            s = jax.ops.segment_sum(p, tgt, num_segments=n)
            w = p / (s[tgt] + 1e-16)
            agg = jax.ops.segment_sum(w[:, :, None] * v[srcidx], tgt, num_segments=n)
            attn = agg.reshape(n, D) @ Wo[l].T + bo[l]
            x = _batchnorm(x + attn, g1[l], beta1[l])
            ff = jax.nn.relu(x @ W1[l].T + b1[l]) @ W2[l].T + b2[l]
            x = _batchnorm(x + ff, g2[l], beta2[l])
        return _layernorm(x, ln_g, ln_b)

    def _L1_mix_ref(x, Wq, Wk, Wv, W1, W2):
        import jax, jax.numpy as jnp
        import numpy as np
        B, N, C = (8, 128, 512)
        q = x @ Wq.T
        k = x @ Wk.T
        v = x @ Wv.T
        dim = q.shape[-1]
        q = jax.nn.softmax(q, axis=-1) * dim ** (-0.5)
        k = jax.nn.softmax(k, axis=-2)
        context = jnp.einsum('bnd,bne->bde', k, v)
        attn = jnp.einsum('bnd,bde->bne', q, context)
        x = attn + x
        return x @ W1.T @ W2.T + x

    def _L1_ffn_ref(x, W_router, W1, b1, W2, b2):
        import jax, jax.numpy as jnp
        import numpy as np
        TOP_K = 2
        B, T, C = x.shape
        E = W_router.shape[1]
        x_flat = x.reshape(B * T, C)
        logits = x_flat @ W_router
        probs = jax.nn.softmax(logits, axis=-1)
        topk_p, topk_i = jax.lax.top_k(probs, TOP_K)
        topk_p = topk_p / topk_p.sum(axis=-1, keepdims=True)
        combine = (jax.nn.one_hot(topk_i, E, dtype=x_flat.dtype) * topk_p[..., None]).sum(axis=1)
        out = jnp.zeros_like(x_flat)
        for e in range(E):
            h = jax.nn.relu(x_flat @ W1[e] + b1[e])
            y = h @ W2[e] + b2[e]
            out = out + combine[:, e:e + 1] * y
        return out.reshape(B, T, C)

    def _L2_gnn_ref(x, edge_index, W1, b1, W2, b2):
        import jax, jax.numpy as jnp
        import numpy as np
        N = 50000
        E = 12500
        D_IN = 512
        D_HID = 64
        D_OUT = 512
        h = jax.nn.relu(x @ W1 + b1) @ W2 + b2
        row, col = (edge_index[0], edge_index[1])
        agg = jax.ops.segment_sum(h[col], row, num_segments=h.shape[0])
        return h + agg

    def _L2_mix_ref(x, qkv_w, qkv_b, out_w, out_b, ln_gamma, ln_beta):
        import jax, jax.numpy as jnp
        import numpy as np
        HEADS = 8
        EPS_LN = 1e-05
        EPS_NORM = 1e-08
        B, N, C = x.shape
        h = HEADS
        d = C // h
        residual = x
        mu = jnp.mean(x, axis=-1, keepdims=True)
        var = jnp.var(x, axis=-1, keepdims=True)
        xn = (x - mu) / jnp.sqrt(var + EPS_LN) * ln_gamma + ln_beta
        qkv = xn @ qkv_w.T + qkv_b
        qkv = qkv.reshape(B, N, 3, h, d).transpose(2, 0, 3, 1, 4)
        q, k, v = (qkv[0], qkv[1], qkv[2])
        q = jax.nn.elu(q) + 1.0
        k = jax.nn.elu(k) + 1.0
        kv = jnp.einsum('bhnd,bhne->bhde', k, v)
        k_sum = jnp.sum(k, axis=2)
        out = jnp.einsum('bhnd,bhde->bhne', q, kv)
        normalizer = jnp.einsum('bhnd,bhd->bhn', q, k_sum)
        out = out / (normalizer[..., None] + EPS_NORM)
        out = out.transpose(0, 2, 1, 3).reshape(B, N, C)
        out = out @ out_w.T + out_b
        return out + residual

    def _L2_ffn_ref(x, expert_weights, expert_indices, w1, w2):
        import jax, jax.numpy as jnp
        import numpy as np
        NUM_EXPERTS = 8
        TOP_K = 2
        'Dropless MoE: sort assignments by expert, gather tokens, grouped MLP,\n            scatter-combine with top-k router weights (megablocks gather/scatter semantics).'
        in_shape = x.shape
        hs = in_shape[-1]
        x_flat = x.reshape(-1, hs)
        T = x_flat.shape[0]
        flat_ids = expert_indices.reshape(-1)
        order = jnp.argsort(flat_ids)
        bin_ids = flat_ids[order]
        token_ids = order // TOP_K
        xg = x_flat[token_ids]
        y = jnp.zeros_like(xg)
        for e in range(NUM_EXPERTS):
            h = jax.nn.gelu(xg @ w1[e], approximate=False)
            y = jnp.where((bin_ids == e)[:, None], h @ w2[e], y)
        w = expert_weights.reshape(-1)[order][:, None]
        out = jnp.zeros((T, hs), x.dtype).at[token_ids].add(w * y)
        return out.reshape(in_shape)

    def _L3_gnn_ref(node_feature, edge_index, W_l, b_l, W_r, gamma, beta):
        import jax, jax.numpy as jnp
        import numpy as np
        N_NODES = 50000
        N_EDGES = 46875
        D = 512
        LN_EPS = 1e-05

        def _layer_norm(x, gamma, beta):
            mu = jnp.mean(x, axis=-1, keepdims=True)
            var = jnp.mean(jnp.square(x - mu), axis=-1, keepdims=True)
            return (x - mu) * jax.lax.rsqrt(var + LN_EPS) * gamma + beta
        n = node_feature.shape[0]
        residual = node_feature
        h = _layer_norm(node_feature, gamma, beta)
        src, dst = (edge_index[0], edge_index[1])
        summed = jax.ops.segment_sum(h[src], dst, num_segments=n)
        cnt = jax.ops.segment_sum(jnp.ones((src.shape[0],), h.dtype), dst, num_segments=n)
        mean = summed / jnp.maximum(cnt, 1.0)[:, None]
        out = mean @ W_l.T + b_l + h @ W_r.T
        out = jax.nn.relu(out)
        return out + residual

    def _L3_mix_ref(x, Wq, Wk, Wv, Wo, bo, proj, ln0_g, ln0_b, W1, b1, W2, b2, ln1_g, ln1_b):
        import jax, jax.numpy as jnp
        import numpy as np
        B, N, D_MODEL = (4, 256, 512)
        N_HEAD, D_HEAD = (8, 64)
        NB_FEAT = 266
        MLP_DIM = 1024

        def _layernorm(x, g, b, eps=1e-05):
            m = jnp.mean(x, -1, keepdims=True)
            v = jnp.var(x, -1, keepdims=True)
            return (x - m) * jax.lax.rsqrt(v + eps) * g + b

        def _softmax_kernel(data, proj, is_query, eps=0.0001):
            norm = data.shape[-1] ** (-0.25)
            ratio = proj.shape[0] ** (-0.5)
            dd = jnp.einsum('bhnd,rd->bhnr', data * norm, proj)
            diag = 0.5 * jnp.sum((data * norm) ** 2, axis=-1, keepdims=True)
            if is_query:
                stab = jnp.max(dd, axis=-1, keepdims=True)
            else:
                stab = jnp.max(dd)
            return ratio * (jnp.exp(dd - diag - stab) + eps)

        def _fast_attention_block(x, Wq, Wk, Wv, Wo, bo, proj, ln0_g, ln0_b, W1, b1, W2, b2, ln1_g, ln1_b):
            b, n, d = x.shape
            h, dh = (N_HEAD, d // N_HEAD)
            split = lambda t: t.reshape(b, n, h, dh).transpose(0, 2, 1, 3)
            q = split(x @ Wq)
            k = split(x @ Wk)
            v = split(x @ Wv)
            qp = _softmax_kernel(q, proj, is_query=True)
            kp = _softmax_kernel(k, proj, is_query=False)
            ksum = jnp.sum(kp, axis=2)
            d_inv = 1.0 / jnp.einsum('bhnr,bhr->bhn', qp, ksum)
            ctx = jnp.einsum('bhnr,bhnd->bhrd', kp, v)
            out = jnp.einsum('bhnr,bhrd,bhn->bhnd', qp, ctx, d_inv)
            out = out.transpose(0, 2, 1, 3).reshape(b, n, d) @ Wo + bo
            hdd = _layernorm(x + out, ln0_g, ln0_b)
            mlp = jax.nn.gelu(hdd @ W1 + b1, approximate=False) @ W2 + b2
            return _layernorm(hdd + mlp, ln1_g, ln1_b)
        return _fast_attention_block(x, Wq, Wk, Wv, Wo, bo, proj, ln0_g, ln0_b, W1, b1, W2, b2, ln1_g, ln1_b)

    def _L3_ffn_ref(x, w_gate, w_up, w_down):
        import jax, jax.numpy as jnp
        import numpy as np
        DIM = 512
        FFN_DIM = 1408
        GROUP = 128
        EPS = 1e-05

        def _quantize_weight(w, group_size):
            o, i = w.shape
            wg = w.reshape(o, i // group_size, group_size)
            scale = jnp.mean(jnp.abs(wg), axis=-1, keepdims=True) + EPS
            wq = jnp.clip(jnp.round(wg / scale), -1.0, 1.0) * scale
            return wq.reshape(o, i)

        def _bitlinear(x, w, group_size=GROUP):
            wq = w + jax.lax.stop_gradient(_quantize_weight(w, group_size) - w)
            return jnp.einsum('bsd,fd->bsf', x, wq)
        gate = _bitlinear(x, w_gate)
        up = _bitlinear(x, w_up)
        h = jax.nn.silu(gate) * up
        return _bitlinear(h, w_down)
    edge_index = jnp.stack([src, dst])
    xn = _layernorm(x, axis=-1)
    x = x + _L0_gnn_ref(xn, edge_index, L0_gnn_W_rel1, L0_gnn_b_rel1, L0_gnn_W_root1, L0_gnn_W_lin1, L0_gnn_b_lin1, L0_gnn_W_rel2, L0_gnn_b_rel2, L0_gnn_W_root2, L0_gnn_W_lin2, L0_gnn_b_lin2) + _L0_mix_ref(xn[None], L0_mix_Wq, L0_mix_bq, L0_mix_Wk, L0_mix_bk, L0_mix_Wv, L0_mix_bv, L0_mix_Wo, L0_mix_bo, L0_mix_ln1_scale, L0_mix_ln1_bias, L0_mix_W1, L0_mix_b1, L0_mix_W2, L0_mix_b2, L0_mix_ln2_scale, L0_mix_ln2_bias)[0]
    x = x + _L0_ffn_ref(_layernorm(x, axis=-1)[None], L0_ffn_Wr, L0_ffn_br, L0_ffn_W1, L0_ffn_W2, L0_ffn_W3)[0]
    xn = _layernorm(x, axis=-1)
    x = x + _L1_gnn_ref(xn, edge_index, L1_gnn_Wq, L1_gnn_bq, L1_gnn_Wk, L1_gnn_Wv, L1_gnn_Wo, L1_gnn_bo, L1_gnn_W1, L1_gnn_b1, L1_gnn_W2, L1_gnn_b2, L1_gnn_g1, L1_gnn_beta1, L1_gnn_g2, L1_gnn_beta2, L1_gnn_ln_g, L1_gnn_ln_b) + _L1_mix_ref(xn[None], L1_mix_Wq, L1_mix_Wk, L1_mix_Wv, L1_mix_W1, L1_mix_W2)[0]
    x = x + _L1_ffn_ref(_layernorm(x, axis=-1)[None], L1_ffn_W_router, L1_ffn_W1, L1_ffn_b1, L1_ffn_W2, L1_ffn_b2)[0]
    xn = _layernorm(x, axis=-1)
    x = x + _L2_gnn_ref(xn, edge_index, L2_gnn_W1, L2_gnn_b1, L2_gnn_W2, L2_gnn_b2) + _L2_mix_ref(xn[None], L2_mix_qkv_w, L2_mix_qkv_b, L2_mix_out_w, L2_mix_out_b, L2_mix_ln_gamma, L2_mix_ln_beta)[0]
    x = x + _L2_ffn_ref(_layernorm(x, axis=-1)[None], L2_ffn_expert_weights, L2_ffn_expert_indices, L2_ffn_w1, L2_ffn_w2)[0]
    xn = _layernorm(x, axis=-1)
    x = x + _L3_gnn_ref(xn, edge_index, L3_gnn_W_l, L3_gnn_b_l, L3_gnn_W_r, L3_gnn_gamma, L3_gnn_beta) + _L3_mix_ref(xn[None], L3_mix_Wq, L3_mix_Wk, L3_mix_Wv, L3_mix_Wo, L3_mix_bo, L3_mix_proj, L3_mix_ln0_g, L3_mix_ln0_b, L3_mix_W1, L3_mix_b1, L3_mix_W2, L3_mix_b2, L3_mix_ln1_g, L3_mix_ln1_b)[0]
    x = x + _L3_ffn_ref(_layernorm(x, axis=-1)[None], L3_ffn_w_gate, L3_ffn_w_up, L3_ffn_w_down)[0]
    return x

_drawn_inputs = setup_inputs


def setup_inputs(seed=0):
    import zlib

    import numpy as np

    out = dict(_drawn_inputs(seed))
    spreads = {'L0_gnn_b_rel1': (0.0, 0.28),
     'L0_gnn_b_lin1': (0.0, 0.1),
     'L0_gnn_b_rel2': (0.0, 0.607),
     'L0_gnn_b_lin2': (0.0, 0.1),
     'L0_mix_bq': (0.0, 0.8),
     'L0_mix_bk': (0.0, 0.8),
     'L0_mix_bv': (0.0, 0.1),
     'L0_mix_bo': (0.0, 0.1),
     'L0_mix_ln1_scale': (1.0, 0.2),
     'L0_mix_ln1_bias': (0.0, 0.1),
     'L0_mix_b1': (0.0, 0.388),
     'L0_mix_b2': (0.0, 0.1),
     'L0_mix_ln2_scale': (1.0, 0.2),
     'L0_mix_ln2_bias': (0.0, 0.1),
     'L0_ffn_br': (0.0, 0.8),
     'L1_gnn_bq': (0.0, 0.8),
     'L1_gnn_bo': (0.0, 2.0),
     'L1_gnn_b1': (0.0, 2.0),
     'L1_gnn_b2': (0.0, 2.0),
     'L1_gnn_g1': (1.0, 0.581),
     'L1_gnn_beta1': (0.0, 2.0),
     'L1_gnn_g2': (1.0, 0.6),
     'L1_gnn_beta2': (0.0, 0.267),
     'L1_gnn_ln_g': (1.0, 0.6),
     'L1_gnn_ln_b': (0.0, 0.308),
     'L1_ffn_b1': (0.0, 0.8),
     'L1_ffn_b2': (0.0, 0.577),
     'L2_gnn_b1': (0.0, 0.1),
     'L2_gnn_b2': (0.0, 0.1),
     'L2_mix_qkv_b': (0.0, 0.8),
     'L2_mix_out_b': (0.0, 0.761),
     'L2_mix_ln_gamma': (1.0, 0.6),
     'L2_mix_ln_beta': (0.0, 0.715),
     'L3_gnn_b_l': (0.0, 2.0),
     'L3_gnn_gamma': (1.0, 0.6),
     'L3_gnn_beta': (0.0, 2.0),
     'L3_mix_bo': (0.0, 2.0),
     'L3_mix_ln0_g': (1.0, 0.6),
     'L3_mix_ln0_b': (0.0, 0.8),
     'L3_mix_b1': (0.0, 2.0),
     'L3_mix_b2': (0.0, 2.0),
     'L3_mix_ln1_g': (1.0, 0.6),
     'L3_mix_ln1_b': (0.0, 0.8)}
    factors = {'L0_mix_Wq': 8.0,
     'L0_mix_Wk': 8.0,
     'L0_mix_Wv': 5.251,
     'L0_ffn_Wr': 8.0,
     'L0_ffn_W1': 8.0,
     'L0_ffn_W2': 8.0,
     'L0_ffn_W3': 8.0,
     'L1_mix_Wq': 8.0,
     'L1_mix_Wk': 8.0,
     'L1_mix_Wv': 8.0,
     'L1_ffn_W_router': 5.035,
     'L1_ffn_W1': 8.0,
     'L1_ffn_W2': 8.0,
     'L2_ffn_expert_weights': 8.0,
     'L2_ffn_w1': 4.468,
     'L2_ffn_w2': 4.062,
     'L3_mix_Wq': 64.0,
     'L3_mix_Wk': 8.0,
     'L3_mix_Wv': 3.905,
     'L3_mix_Wo': 4.008,
     'L3_mix_proj': 64.0,
     'L3_mix_W1': 4.057,
     'L3_mix_W2': 3.741,
     'L3_ffn_w_gate': 4.071,
     'L3_ffn_w_up': 3.802,
     'L3_ffn_w_down': 3.806,
     'L3_gnn_W_l': 2.735}
    for name, (base, spread) in spreads.items():
        noise = np.random.default_rng([zlib.crc32(name.encode()), seed]).standard_normal(out[name].shape)
        drawn = base * np.exp(spread * noise) if base else spread * noise
        out[name] = jnp.asarray(drawn.astype(out[name].dtype))
    for name, factor in factors.items():
        out[name] = (out[name] * factor).astype(out[name].dtype)
    return out
```

```python
from contextlib import ExitStack

import numpy as np
import concourse.bass as bass
from concourse import mybir

ALU = mybir.AluOpType
ACT = mybir.ActivationFunctionType
F32 = mybir.dt.float32
BF16 = mybir.dt.bfloat16
F16 = mybir.dt.float16
I32 = mybir.dt.int32
AX = mybir.AxisListType

P = 128
N = 2048
D = 512
T = N // P
KC = D // P
CH = 512
NC = N // CH
RING = 4
LOOPS = 4
E = 34816
EPS = 1e-5



class Signal:

    def __init__(self, ctx, nc, name):
        self.sem = ctx.enter_context(nc.semaphore(name))
        self.base = 0

    def count(self, n):
        return self.base + n


class Core:

    def __init__(self, ctx, nc, ins):
        self.nc, self.ins = nc, ins

        def sb(name, shape, dt):
            return ctx.enter_context(nc.sbuf_tensor(name, shape, dt))

        self.x = sb("x_tokens", [P, T, D], F32)
        self.store = sb("store", [P, 4 * T * D], F32)
        self.big = [self.store[:, i * T * D:(i + 1) * T * D] for i in range(4)]
        self.weights = [sb(f"weights{i}", [P, 2, KC, D], BF16) for i in range(2)]
        self.staging = sb("staging", [P, KC, D], F32)
        self.tmp = sb("tmp", [P, RING, D], F32)
        self.rows = sb("rows", [P, 3, D], F32)
        self.cols = sb("cols", [P, ins["cols"].shape[1]], F32)
        self.zeros = sb("zeros", [P, 512], BF16)
        self.ones = sb("ones", [P, 2], BF16)
        self.headmask = sb("headmask", [P, P], F32)
        self.kv = sb("kv", [P, 2, 2, KC, P], BF16)
        self.small = sb("small", [P, 9, T], F32)
        self.xweight = sb("xweight", [P, T], F32)
        self.counts = sb("counts", [P, 2, EXPERTS], F32)
        self.hots = sb("hots", [P, 2, T, EXPERTS], BF16)
        self.ones128 = sb("ones128", [P, P], BF16)
        self.small_top = sb("edge_top", [P, T, 8], F32)
        self.table = self.hots[0:1, :, :, :].rearrange("p a t e -> p (a t e)").bitcast(I32)[:, 0:3 * T].rearrange(
            "p (a b) -> p a b", a=3)
        self.iota = self.rows[:, :, :].rearrange("p a d -> p (a d)").bitcast(F16)[:, 0:N]
        self.rdegree = sb("rdegree", [P, T], F32)
        self.onesf = sb("onesf", [P, P], F32)
        self.ident = sb("ident", [P, P], BF16)
        self.identf = sb("identf", [P, P], F32)
        self.moments = sb("moments", [P, T, 6], F32)
        self.tile_top = self.moments[:, :, :].rearrange("p t s -> p (t s)")[:, 0:HEADS]
        self.meanvar = sb("meanvar", [P, T, 2], F32)
        self.rstd = sb("rstd", [P, T], F32)
        self.psum = ctx.enter_context(nc.psum_tensor("banks", [P, 8, 512], F32))
        self.bank = [self.psum[:, i, :] for i in range(8)]

        def sig(name):
            return Signal(ctx, nc, name)

        self.full = sig("bank_full")
        self.valued = sig("value_ready")
        self.hi = sig("hi_ready")
        self.lo = sig("lo_ready")
        self.step = sig("vector_step")
        self.astep = sig("scalar_step")
        self.staged = sig("weight_staged")
        self.whi = sig("weight_hi")
        self.wlo = sig("weight_lo")
        self.loaded = sig("params_loaded")
        self.ring = [sig(f"ring_dma{j}") for j in range(RING)]
        self.atg = [sig(f"adjacency_group{g}") for g in range(4)]
        self.stat = sig("row_statistics")
        self.aux = sig("aux")
        self.aux2 = sig("aux2")
        self.hot_ready = sig("one_hots_ready")
        self.hot_used = sig("one_hots_used")
        self.queue = []
        self.slot = 0
        self.staged_spec = None
        self.slot_ready = False

    def big_pair(self, i):
        return self.store[:, i * T * D:(i + 2) * T * D].bitcast(BF16).rearrange("p (t n) -> p t n", t=T)

    def F(self, i):
        return self.big[i][:, :].bitcast(BF16).rearrange("p (b n) -> p b n", b=2 * KC)

    def TH(self, i):
        return self.big[i][:, :].bitcast(BF16).rearrange("p (t h d) -> p t h d", t=T, h=2)

    def T32(self, i):
        return self.big[i][:, :].rearrange("p (t d) -> p t d", t=T)

    def F32v(self, i):
        return self.big[i][:, :].rearrange("p (b n) -> p b n", b=KC)

    def col(self, name, width=1):
        c = self.ins["col_index"][name]
        return self.cols[:, c:c + width]


def done(k, **counts):
    for name, n in counts.items():
        k_sig = {"full": k.full, "valued": k.valued, "hi": k.hi, "lo": k.lo, "step": k.step, "astep": k.astep,
                 "staged": k.staged, "whi": k.whi, "wlo": k.wlo, "loaded": k.loaded, "stat": k.stat,
                 "aux": k.aux, "aux2": k.aux2}[name]
        k_sig.base += n



class WeightTurn:

    def __init__(self, k):
        self.k = k
        self.split = None if k.slot_ready else k.staged_spec
        self.slot = 1 - k.slot
        self.next = None
        if self.split is not None:
            k.slot_ready, k.staged_spec = True, None
        if k.staged_spec is None and k.queue:
            self.next = k.staged_spec = k.queue.pop(0)

    def scalar(self, act):
        k = self.k
        if self.split is not None:
            _, p, c, n, _ = self.split
            act.wait_ge(k.staged.sem, k.staged.count(0))
            k.nc.scalar.activation(k.weights[self.slot][0:p, 0, 0:c, 0:n], k.staging[0:p, 0:c, 0:n],
                                   ACT.Copy).then_inc(k.whi.sem, 1)

    def vector(self, dve):
        k = self.k
        if self.split is not None:
            _, p, c, n, _ = self.split
            dve.wait_ge(k.whi.sem, k.whi.count(1))
            k.nc.vector.tensor_tensor(k.weights[self.slot][0:p, 1, 0:c, 0:n], k.staging[0:p, 0:c, 0:n],
                                      k.weights[self.slot][0:p, 0, 0:c, 0:n],
                                      ALU.subtract).then_inc(k.wlo.sem, 1)

    def sync(self, sp):
        k = self.k
        if self.next is not None:
            if self.split is not None:
                sp.wait_ge(k.wlo.sem, k.wlo.count(1))
            ap, p, c, n, _ = self.next
            sp.dma_start(k.staging[0:p, 0:c, 0:n], ap).then_inc(k.staged.sem, 16)

    def finish(self):
        k = self.k
        done(k, whi=int(self.split is not None), wlo=int(self.split is not None),
             staged=16 * int(self.next is not None))
        if self.next is not None and self.next[4]:
            quantize_stage(k)


def use_weight(k):
    assert k.slot_ready
    k.slot_ready = False
    k.slot = 1 - k.slot
    return k.weights[k.slot]



def accumulate(pe, out, pairs, start=True, stop=True):
    last = None
    for n, (stationary, moving) in enumerate(pairs):
        last = pe.matmul(out, stationary, moving, start=start and n == 0, stop=stop and n == len(pairs) - 1,
                         skip_group_check=True)
    return last


def start_copies(k, sp, copies):
    for dst, src in copies:
        sp.dma_start(dst, src).then_inc(k.loaded.sem, 16)


def end_copies(k, sp, copies):
    if copies:
        sp.wait_ge(k.loaded.sem, k.loaded.count(16 * len(copies)))


def tokens_out(act_f, w, i_tile, blocks=KC, n=D):
    out = []
    for c in range(blocks):
        hi = act_f[:, c, bass.ts(i_tile, P)]
        lo = act_f[:, KC + c, bass.ts(i_tile, P)]
        out += [(hi, w[:, 0, c, 0:n]), (hi, w[:, 1, c, 0:n]), (lo, w[:, 0, c, 0:n])]
    return out


def features_out(act_f, w, f, i_chunk, m=P, chunk=CH):
    out = []
    for c in range(KC):
        hi = act_f[:, c, bass.ts(i_chunk, chunk)]
        lo = act_f[:, KC + c, bass.ts(i_chunk, chunk)]
        whi, wlo = w[:, 0, c, f * P:f * P + m], w[:, 1, c, f * P:f * P + m]
        out += [(whi, hi), (whi, lo), (wlo, hi)]
    return out


def product_stage(k, pairs, value, halves=None, in_place=False, value_on="vector", steps=1, rows_out=P, width=RING,
                  trips=LOOPS, turn=True, cols_out=D, pairs2=None, pre=None, copies=(), needs_copies=False,
                  stats=None, trip_store=None):
    nc = k.nc
    turn = WeightTurn(k) if turn else None
    stores = trips * len(trip_store(0)) if trip_store else 0
    with nc.Block() as block:

        @block.sync
        def _(sp):
            if turn:
                turn.sync(sp)
            start_copies(k, sp, copies)
            if trip_store:
                with sp.Fori(0, trips) as i:
                    sp.wait_ge(k.lo.sem, i * width + k.lo.count(RING + width))
                    for dst, src in trip_store(i):
                        sp.dma_start(dst, src).then_inc(k.aux2.sem, 16)
                sp.wait_ge(k.aux2.sem, k.aux2.count(16 * stores))
            end_copies(k, sp, copies)

        @block.tensor
        def _(pe):
            with pe.Fori(0, trips) as i:
                for j in range(width):
                    pe.wait_ge(k.valued.sem, i * width + k.valued.count(j + 1 + RING - width))
                    if pairs2:
                        accumulate(pe, k.bank[RING + j][0:rows_out, 0:cols_out], pairs2(i, j))
                    accumulate(pe, k.bank[j][0:rows_out, 0:cols_out], pairs(i, j)).then_inc(k.full.sem, 1)

        def value_program(eng):
            if needs_copies:
                eng.wait_ge(k.loaded.sem, k.loaded.count(16 * len(copies)))
            with eng.Fori(0, trips) as i:
                for j in range(width):
                    n = i * width + j
                    eng.wait_ge(k.full.sem, i * width + k.full.count(j + 1))
                    if pre:
                        eng.wait_ge(k.aux.sem, i * width + k.aux.count(j + 1))
                    if halves:
                        eng.wait_ge(k.lo.sem, i * width + k.lo.count(j + 1 + RING - width))
                    sig = k.step if eng is nc.vector or value_on == "vector" else k.astep

                    def chain(ins, s, n=n, sig=sig):
                        ins.then_inc(sig.sem, 1)
                        eng.wait_ge(sig.sem, i * (width * (steps - 1)) + sig.count(j * (steps - 1) + s))

                    value(eng, i, j, k.bank[j][0:rows_out, 0:cols_out], k.tmp[0:rows_out, j, 0:cols_out],
                          chain).then_inc(k.valued.sem, 1)
                    if stats is not None:
                        eng.wait_ge(k.valued.sem, i * width + k.valued.count(RING + j + 1))
                        eng.bn_stats(k.moments[:, bass.ds(tile_of(i, j), 1), :].rearrange("p a s -> p (a s)"),
                                     stats[:, tile_of(i, j), :]).then_inc(k.stat.sem, 1)

        def hi_program(eng, copy):
            with eng.Fori(0, trips) as i:
                for j in range(width):
                    eng.wait_ge(k.valued.sem, i * width + k.valued.count(RING + j + 1))
                    if in_place and j == 0:
                        eng.wait_ge(k.full.sem, i * width + k.full.count(width))
                    copy(halves(i, j)[0], k.tmp[0:rows_out, j, 0:cols_out]).then_inc(k.hi.sem, 1)

        @block.vector
        def _(dve):
            if turn:
                turn.vector(dve)
            if value_on == "vector":
                value_program(dve)
            elif halves:
                hi_program(dve, lambda o, a: dve.tensor_copy(o, a))

        @block.scalar
        def _(act):
            if turn:
                turn.scalar(act)
            if value_on == "scalar":
                value_program(act)
            elif pre:
                with act.Fori(0, trips) as i:
                    for j in range(width):
                        act.wait_ge(k.full.sem, i * width + k.full.count(j + 1))
                        pre(act, i, j, k.bank[j][0:rows_out, 0:cols_out]).then_inc(k.aux.sem, 1)
                    for j in range(width if halves else 0):
                        act.wait_ge(k.valued.sem, i * width + k.valued.count(RING + j + 1))
                        act.activation(halves(i, j)[0], k.tmp[0:rows_out, j, 0:cols_out],
                                       ACT.Copy).then_inc(k.hi.sem, 1)
            elif halves:
                hi_program(act, lambda o, a: act.activation(o, a, ACT.Copy))

        @block.gpsimd
        def _(pool):
            if halves:
                with pool.Fori(0, trips) as i:
                    for j in range(width):
                        pool.wait_ge(k.hi.sem, i * width + k.hi.count(j + 1))
                        hi, lo = halves(i, j)
                        pool.tensor_tensor(lo, k.tmp[0:rows_out, j, 0:cols_out], hi,
                                           ALU.subtract).then_inc(k.lo.sem, 1)

    n = trips * width
    done(k, full=n, valued=n)
    if steps > 1:
        done(k, **{"step" if value_on == "vector" else "astep": n * (steps - 1)})
    if halves:
        done(k, hi=n, lo=n)
    if pre:
        done(k, aux=n)
    done(k, loaded=16 * len(copies), stat=n if stats is not None else 0, aux2=16 * stores)
    if turn:
        turn.finish()


def moments_stage(k, src, eps, copies=(), tiles=T):
    nc = k.nc
    with nc.Block() as block:

        @block.sync
        def _(sp):
            start_copies(k, sp, copies)
            end_copies(k, sp, copies)

        @block.vector
        def _(dve):
            for t in range(tiles):
                dve.bn_stats(k.moments[:, t, :], src[:, t, :]).then_inc(k.step.sem, 1)
            for t in range(T):
                if t < tiles:
                    dve.wait_ge(k.step.sem, k.step.count(t + 1))
                dve.bn_aggr(k.meanvar[:, t, :], k.moments[:, t, :]).then_inc(k.aux.sem, 1)
            dve.wait_ge(k.aux.sem, k.aux.count(T))
            dve.tensor_scalar(k.rstd[:, :], k.meanvar[:, :, 1], eps, None, ALU.add).then_inc(k.step.sem, 1)
            dve.wait_ge(k.hi.sem, k.hi.count(1))
            dve.reciprocal(k.rstd[:, :], k.rstd[:, :]).then_inc(k.step.sem, 1)

        @block.scalar
        def _(act):
            act.wait_ge(k.step.sem, k.step.count(tiles + 1))
            act.activation(k.rstd[:, :], k.rstd[:, :], ACT.Sqrt).then_inc(k.hi.sem, 1)

    done(k, step=tiles + 2, aux=T, hi=1, loaded=16 * len(copies))


def transpose_stage(k, make, dst, steps=1, turn=False, store=None, trips=LOOPS, width=RING,
                    copies=()):
    nc = k.nc
    turn = WeightTurn(k) if turn else None
    with nc.Block() as block:

        @block.vector
        def _(dve):
            if turn:
                turn.vector(dve)
            with dve.Fori(0, trips) as i:
                for j in range(width):
                    if store is not None:
                        dve.wait_ge(k.ring[j].sem, i * 16 + k.ring[j].count(16))

                    def chain(ins, s):
                        ins.then_inc(k.step.sem, 1)
                        dve.wait_ge(k.step.sem, i * (width * (steps - 1)) + k.step.count(j * (steps - 1) + s))

                    make(dve, i, j, k.tmp[:, j, :], chain).then_inc(k.aux.sem, 1)
                for j in range(width):
                    dve.wait_ge(k.hi.sem, i * width + k.hi.count(j + 1))
                    dve.tensor_tensor(dst[:, KC:2 * KC, bass.ts(i * width + j, P)],
                                      k.bank[j][:, :].rearrange("p (c n) -> p c n", c=KC),
                                      dst[:, 0:KC, bass.ts(i * width + j, P)], ALU.subtract).then_inc(k.valued.sem, 1)

        @block.tensor
        def _(pe):
            with pe.Fori(0, trips) as i:
                for j in range(width):
                    pe.wait_ge(k.aux.sem, i * width + k.aux.count(j + 1))
                    pe.wait_ge(k.valued.sem, i * width + k.valued.count(j + 1 + RING - width))
                    for c in range(KC):
                        last = pe.transpose(k.bank[j][:, c * P:(c + 1) * P], k.tmp[:, j, c * P:(c + 1) * P],
                                            k.identf[:, :])
                    last.then_inc(k.full.sem, 1)

        @block.scalar
        def _(act):
            if turn:
                turn.scalar(act)
            with act.Fori(0, trips) as i:
                for j in range(width):
                    act.wait_ge(k.full.sem, i * width + k.full.count(j + 1))
                    act.activation(dst[:, 0:KC, bass.ts(i * width + j, P)],
                                   k.bank[j][:, :].rearrange("p (c n) -> p c n", c=KC),
                                   ACT.Copy).then_inc(k.hi.sem, 1)

        @block.sync
        def _(sp):
            if turn:
                turn.sync(sp)
            start_copies(k, sp, copies)
            if store is not None:
                with sp.Fori(0, trips) as i:
                    for j in range(width):
                        sp.wait_ge(k.aux.sem, i * width + k.aux.count(j + 1))
                        sp.dma_start(store(i * width + j), k.tmp[:, j, :]).then_inc(k.ring[j].sem, 16)
                for j in range(width):
                    sp.wait_ge(k.ring[j].sem, k.ring[j].count(16 * (trips + 1)))
            end_copies(k, sp, copies)

    n = trips * width
    done(k, aux=n, hi=n, full=n, valued=n, step=n * (steps - 1), loaded=16 * len(copies))
    if store is not None:
        for j in range(width):
            k.ring[j].base += 16 * trips
    if turn:
        turn.finish()


def tile_of(i, j):
    return i * RING + j



def setup_stage(k):
    nc, ins = k.nc, k.ins
    turn = WeightTurn(k)
    with nc.Block() as block:

        @block.gpsimd
        def _(pool):
            pool.memset(k.zeros[:, :], 0.0).then_inc(k.aux.sem, 1)
            pool.memset(k.ones[:, :], 1.0).then_inc(k.aux.sem, 1)
            pool.memset(k.identf[:, :], 0.0).then_inc(k.aux.sem, 1)
            pool.wait_ge(k.aux.sem, 3)
            pool.affine_select(out=k.identf[:, :], in_=k.identf[:, :], compare_op=ALU.not_equal, fill=1.0,
                               base=0, pattern=[[-1, P]], channel_multiplier=1).then_inc(k.aux.sem, 1)
            pool.wait_ge(k.aux.sem, 4)
            pool.tensor_copy(k.ident[:, :], k.identf[:, :]).then_inc(k.aux.sem, 1)
            pool.memset(k.headmask[:, :], 0.0).then_inc(k.aux.sem, 1)
            pool.wait_ge(k.aux.sem, 6)
            pool.memset(k.ones128[:, :], 1.0).then_inc(k.aux.sem, 1)
            pool.memset(k.onesf[:, :], 1.0).then_inc(k.aux.sem, 1)

        @block.sync
        def _(sp):
            turn.sync(sp)
            sp.dma_start(k.x[:, :, :], ins["x"].rearrange("(t p) d -> p t d", p=P)).then_inc(k.loaded.sem, 16)
            sp.dma_start(k.cols[:, :], ins["cols"]).then_inc(k.ring[0].sem, 16)
            sp.wait_ge(k.loaded.sem, 16)
            sp.wait_ge(k.ring[0].sem, 16)

        @block.vector
        def _(dve):
            dve.sem_inc(k.valued.sem, RING)
            dve.sem_inc(k.lo.sem, RING)
            dve.wait_ge(k.ring[0].sem, 16)
            for j in range(1, RING):
                dve.sem_inc(k.ring[j].sem, 16)
            dve.wait_ge(k.aux.sem, 7)
            for h in range(2):
                dve.memset(k.headmask[64 * h:64 * h + 64, 64 * h:64 * h + 64], 1.0).then_inc(k.aux.sem, 1)

    done(k, aux=10, loaded=16)
    turn.finish()


def row_loads(k, *names, **last):
    slots = [*enumerate(names), *((2, n) for n in last.values())]
    return [(k.rows[:, s, :], k.ins["rows"][r:r + 1, :].rearrange("a d -> (a d)").partition_broadcast(P))
            for s, r in ((s, k.ins["row_index"][n]) for s, n in slots)]


def tile_in(buf):
    return lambda t: buf[:, bass.ds(t, 1), :].rearrange("p a d -> p (a d)")


def norm_add_stage(k, src, gain, bias):
    nc = k.nc
    with nc.Block() as block:

        @block.vector
        def _(dve):
            with dve.Fori(0, LOOPS) as i:
                for s in range(4):
                    for j in range(RING):
                        t = tile_of(i, j)
                        if s:
                            dve.wait_ge(k.step.sem, i * (4 * RING) + k.step.count((s - 1) * RING + j + 1))
                        elif j == 0:
                            dve.wait_ge(k.step.sem, i * (4 * RING) + k.step.count(0))
                        y = k.tmp[:, j, :]
                        if s == 0:
                            ins = dve.tensor_scalar(y, src[:, t, :], k.meanvar[:, t, 0:1], k.rstd[:, bass.ds(t, 1)],
                                                    ALU.subtract, ALU.mult)
                        elif s == 1:
                            ins = dve.tensor_tensor(y, y, gain, ALU.mult)
                        elif s == 2:
                            ins = dve.tensor_tensor(y, y, bias, ALU.add)
                        else:
                            ins = dve.tensor_tensor(k.x[:, t, :], k.x[:, t, :], y, ALU.add)
                        ins.then_inc(k.step.sem, 1)

    done(k, step=4 * T)


def normalise(k, src, gain=None, bias=None):

    def make(dve, i, j, y, chain):
        t = tile_of(i, j)
        ins = dve.tensor_scalar(y, src[:, t, :], k.meanvar[:, t, 0:1], k.rstd[:, bass.ds(t, 1)],
                                ALU.subtract, ALU.mult)
        if gain is not None:
            chain(ins, 1)
            ins = dve.tensor_tensor(y, y, gain, ALU.mult)
            chain(ins, 2)
            ins = dve.tensor_tensor(y, y, bias, ALU.add)
        return ins

    return make


def key_value_stage(k, kp, v, kv):
    nc = k.nc
    with nc.Block() as block:

        @block.tensor
        def _(pe):
            for b in range(2):
                pe.matmul(k.bank[b][:, :], k.zeros[:, 0:P], k.zeros[:, :], start=True, stop=False,
                          skip_group_check=True)
            with pe.Fori(0, T) as t:
                for p in range(KC):
                    f = slice(p * P, p * P + P)
                    hi, lo = kp[:, t, 0, f], kp[:, t, 1, f]
                    for s, m in ((hi, v[:, t, 0, f]), (hi, v[:, t, 1, f]), (lo, v[:, t, 0, f])):
                        pe.matmul(k.bank[0][:, f], s, m, start=False, stop=False, skip_group_check=True)
                    for s in (hi, lo):
                        pe.matmul(k.bank[1][:, p:p + 1], s, k.ones[:, 0:1], start=False, stop=False,
                                  skip_group_check=True)
            pe.matmul(k.bank[1][:, :], k.zeros[:, 0:P], k.zeros[:, :], start=False, stop=True,
                      skip_group_check=True).then_inc(k.full.sem, 1)

        @block.vector
        def _(dve):
            dve.wait_ge(k.full.sem, k.full.count(1))
            n = 0
            for p in range(KC):
                f = slice(p * P, p * P + P)
                dve.tensor_tensor(k.tmp[:, 0, f], k.bank[0][:, f], k.headmask[:, :], ALU.mult).then_inc(k.step.sem, 1)
                dve.tensor_scalar(k.tmp[:, 1, f], k.headmask[:, :], k.bank[1][:, p:p + 1], None,
                                  ALU.mult).then_inc(k.step.sem, 1)
            dve.wait_ge(k.step.sem, k.step.count(2 * KC))
            for b in range(2):
                hi = kv[:, b, 0, :, :].rearrange("p a d -> p (a d)")
                dve.tensor_copy(hi, k.tmp[:, b, :]).then_inc(k.step.sem, 1)
            dve.wait_ge(k.step.sem, k.step.count(2 * KC + 2))
            for b in range(2):
                hi = kv[:, b, 0, :, :].rearrange("p a d -> p (a d)")
                lo = kv[:, b, 1, :, :].rearrange("p a d -> p (a d)")
                dve.tensor_tensor(lo, k.tmp[:, b, :], hi, ALU.subtract).then_inc(k.step.sem, 1)

    done(k, full=1, step=2 * KC + 4)


def aggregate_stage(k, u, at_ring, at_dram, root, w, value, halves, in_place):
    nc = k.nc
    turn = WeightTurn(k)
    with nc.Block() as block:

        @block.sync
        def _(sp):
            turn.sync(sp)
            with sp.Fori(0, NC) as i:
                for g in range(RING):
                    sp.wait_ge(k.aux2.sem, i * RING + k.aux2.count(g + 1))
                    sp.dma_start(at_ring[:, g, :, :],
                                 at_dram[4 * g:4 * g + 4, :, bass.ts(i, CH)].rearrange("s p n -> p s n")
                                 ).then_inc(k.ring[g].sem, 16)

        @block.tensor
        def _(pe):
            pe.sem_inc(k.aux2.sem, RING)
            with pe.Fori(0, NC) as i:
                for g in range(RING):
                    pe.wait_ge(k.ring[g].sem, i * 16 + k.ring[g].count(32))
                    for f in range(KC):
                        if g == 0:
                            pe.wait_ge(k.valued.sem, i * KC + k.valued.count(f + 1))
                        pairs = [(u[:, 4 * g + s, h, f * P:f * P + P], at_ring[:, g, s, :])
                                 for s in range(4) for h in range(2)]
                        last = accumulate(pe, k.bank[f][:, :], pairs, start=g == 0, stop=False)
                    last.then_inc(k.aux2.sem, 1)
                for f in range(KC):
                    accumulate(pe, k.bank[f][:, :], features_out(root, w, f, i), start=False).then_inc(k.full.sem, 1)

        @block.vector
        def _(dve):
            turn.vector(dve)
            with dve.Fori(0, NC) as i:
                for f in range(KC):
                    dve.wait_ge(k.full.sem, i * KC + k.full.count(f + 1))
                    dve.wait_ge(k.lo.sem, i * KC + k.lo.count(f + 1))
                    value(dve, i, f, k.bank[f][:, :], k.tmp[:, f, :]).then_inc(k.valued.sem, 1)

        @block.scalar
        def _(act):
            turn.scalar(act)
            with act.Fori(0, NC) as i:
                for f in range(KC):
                    act.wait_ge(k.valued.sem, i * KC + k.valued.count(RING + f + 1))
                    if in_place and f == 0:
                        act.wait_ge(k.full.sem, i * KC + k.full.count(KC))
                    act.activation(halves(i, f)[0], k.tmp[:, f, :], ACT.Copy).then_inc(k.hi.sem, 1)

        @block.gpsimd
        def _(pool):
            with pool.Fori(0, NC) as i:
                for f in range(KC):
                    pool.wait_ge(k.hi.sem, i * KC + k.hi.count(f + 1))
                    pool.tensor_tensor(halves(i, f)[1], k.tmp[:, f, :], halves(i, f)[0],
                                       ALU.subtract).then_inc(k.lo.sem, 1)

    n = NC * KC
    done(k, full=n, valued=n, hi=n, lo=n, aux2=n + RING)
    for g in range(RING):
        k.ring[g].base += 16 * NC
    turn.finish()



def all_tiles(dram):
    return dram.rearrange("t p d -> p t d")


def f_halves(buf):
    return lambda i, j: (buf[:, j, bass.ts(i, CH)], buf[:, KC + j, bass.ts(i, CH)])


def t_halves(buf):
    return lambda i, j: (buf[:, tile_of(i, j), 0, :], buf[:, tile_of(i, j), 1, :])


def plus_col(col, relu=False):
    def value(dve, i, j, ps, y, chain=None):
        return dve.tensor_scalar(y, ps, col[:, j:j + 1], 0.0 if relu else None, ALU.add,
                                 *([ALU.max] if relu else []))
    return value


def plus_row(row):
    return lambda dve, i, j, ps, y, chain: dve.tensor_tensor(y, ps, row, ALU.add)


def as_is(eng, i, j, ps, y, chain):
    return eng.activation(y, ps, ACT.Copy)


def weight(ap, c=KC, quantized=False):
    return ap.rearrange("(c p) n -> p c n", p=P), P, c, ap.shape[1], quantized



def layer0_mix(k):
    xn, q, f1 = k.F(0), k.F(1), k.F(2)
    kp, v, t32 = k.TH(2), k.TH(3), k.T32(3)
    kv = k.big[2][:, 0:1024].bitcast(BF16).rearrange("p (b h a d) -> p b h a d", b=2, h=2, a=KC)
    keps = 0.001
    bq = k.col("L0_mix_bq", KC)

    def relu_col(dve, i, j, ps, y, chain):
        chain(dve.tensor_scalar(y, ps, bq[:, j:j + 1], 0.0, ALU.add, ALU.max), 1)
        return dve.tensor_scalar(y, y, keps, None, ALU.add)

    def relu_row(dve, i, j, ps, y, chain):
        chain(dve.tensor_tensor(y, ps, k.rows[:, 0, :], ALU.add), 1)
        return dve.tensor_scalar(y, y, 0.0, keps, ALU.max, ALU.add)

    wq = use_weight(k)
    product_stage(k, lambda i, j: features_out(xn, wq, j, i), relu_col, f_halves(q), steps=2)
    wk = use_weight(k)
    product_stage(k, lambda i, j: tokens_out(xn, wk, tile_of(i, j)), relu_row, t_halves(kp), steps=2)
    wv = use_weight(k)
    product_stage(k, lambda i, j: tokens_out(xn, wv, tile_of(i, j)), plus_row(k.rows[:, 1, :]), t_halves(v))
    key_value_stage(k, kp, v, k.kv)
    linear_attention(k, q, k.kv, 0.0, [(t32, all_tiles(k.ins["xn_dram"])),
                                       *row_loads(k, "L0_mix_ln1_scale", "L0_mix_ln1_bias")])
    wo = use_weight(k)

    def residual(row):
        def value(dve, i, j, ps, y, chain):
            chain(dve.tensor_tensor(y, ps, row, ALU.add), 1)
            return dve.tensor_tensor(t32[:, tile_of(i, j), :], y, t32[:, tile_of(i, j), :], ALU.add)
        return value

    product_stage(k, lambda i, j: tokens_out(q, wo, tile_of(i, j)), residual(k.rows[:, 2, :]), steps=2, stats=t32)
    moments_stage(k, t32, 1e-6, tiles=0)
    transpose_stage(k, normalise(k, t32, k.rows[:, 0, :], k.rows[:, 1, :]), q, steps=3, store=tile_in(t32),
                    copies=row_loads(k, b2="L0_mix_b2"))
    w1 = use_weight(k)
    product_stage(k, lambda i, j: features_out(q, w1, 0, i), plus_col(k.col("L0_mix_b1"), relu=True),
                  lambda i, j: (f1[:, 0, bass.ts(i, CH)], f1[:, KC, bass.ts(i, CH)]), width=1,
                  copies=row_loads(k, "L0_mix_ln2_scale", "L0_mix_ln2_bias"))
    w2 = use_weight(k)
    product_stage(k, lambda i, j: tokens_out(f1, w2, tile_of(i, j), blocks=1), residual(k.rows[:, 2, :]), steps=2,
                  stats=t32)
    moments_stage(k, t32, 1e-6, tiles=0)
    norm_add_stage(k, t32, k.rows[:, 0, :], k.rows[:, 1, :])


def linear_attention(k, q, kv, eps, copies):

    def pairs(b):
        def products(i, j):
            hi, lo = q[:, j, bass.ts(i, CH)], q[:, KC + j, bass.ts(i, CH)]
            return [(kv[:, b, 0, j, :], hi), (kv[:, b, 0, j, :], lo), (kv[:, b, 1, j, :], hi)]
        return products

    def value(dve, i, j, ps, y, chain):
        chain(dve.tensor_scalar(y, k.bank[RING + j][:, :], eps, None, ALU.add), 1)
        chain(dve.reciprocal(y, y), 2)
        return dve.tensor_tensor(y, ps, y, ALU.mult)

    product_stage(k, pairs(0), value, f_halves(q), in_place=True, steps=3, pairs2=pairs(1), turn=False,
                  copies=copies)


def layer0_graph(k):
    xn, a, b = k.F(0), k.F(1), k.F(2)
    at_ring = k.big[3][:, 0:RING * 1024].bitcast(BF16).rearrange("p (g s n) -> p g s n", g=RING, s=4)
    at_dram = k.ins["at_dram"]
    root, u = xn, k.TH(1)
    for layer in (1, 2):
        ub, cb = ((1, 2), (2, 1))[layer - 1]
        u = k.TH(ub)
        w = use_weight(k)
        product_stage(k, lambda i, j, w=w, root=root: tokens_out(root, w, tile_of(i, j)), as_is, t_halves(u),
                      value_on="scalar", copies=row_loads(k, "L0_gnn_b_lin2") if layer == 1 else ())
        w = use_weight(k)
        c = k.F(cb)
        aggregate_stage(k, u, at_ring, at_dram, root, w, plus_col(k.col(f"L0_gnn_b_rel{layer}", KC)), f_halves(c),
                        in_place=layer == 2)
        w = use_weight(k)
        if layer == 1:
            h = k.F(1)
            product_stage(k, lambda i, j, w=w, c=c: features_out(c, w, j, i),
                          plus_col(k.col("L0_gnn_b_lin1", KC), relu=True), f_halves(h))
            root = h
        else:

            def value(dve, i, j, ps, y, chain):
                chain(dve.tensor_tensor(y, ps, k.rows[:, 0, :], ALU.add), 1)
                return dve.scalar_tensor_tensor(k.x[:, tile_of(i, j), :], y, 0.0, k.x[:, tile_of(i, j), :],
                                                ALU.max, ALU.add)

            product_stage(k, lambda i, j, w=w, c=c: tokens_out(c, w, tile_of(i, j)), value, steps=2,
                          stats=k.x)


def input_norm(k, tiles, copies):
    moments_stage(k, k.x, EPS, tiles=tiles)
    xn = k.ins["xn_dram"]
    transpose_stage(k, normalise(k, k.x), k.F(0), turn=True, copies=copies,
                    store=lambda t: xn[bass.ds(t, 1), :, :].rearrange("a p d -> p (a d)"))



EXPERTS = 8


def routes(k):
    r = k.kv[:, :, :, :, :].rearrange("p a b c d -> p (a b c d)").bitcast(F32)
    return [r[:, n * P:(n + 1) * P].rearrange("p (t e) -> p t e", e=EXPERTS) for n in range(8)]


def router_stage(k, logits, bias=None):
    w = use_weight(k)
    xn = k.F(0)

    def value(dve, i, j, ps, y, chain):
        if bias is None:
            return dve.tensor_copy(logits[:, tile_of(i, j), :], ps)
        return dve.tensor_tensor(logits[:, tile_of(i, j), :], ps, bias, ALU.add)

    product_stage(k, lambda i, j: tokens_out(xn, w, tile_of(i, j), n=EXPERTS), value, cols_out=EXPERTS)


def top2_stage(k, capacity):
    nc = k.nc
    logits, key, hot0, hot1, work, iota, down, coef = routes(k)
    one = k.small
    m0, m1, s0, s1, keep0, keep1, idx0, idx1, last = (one[:, n, :] for n in range(9))
    counts = k.counts
    steps = [0]

    def wide(a):
        return a.unsqueeze(2).to_broadcast([P, T, EXPERTS])

    def over_tokens(a):
        return a.unsqueeze(1).to_broadcast([P, T, EXPERTS])

    with nc.Block() as block:

        @block.gpsimd
        def _(pool):
            pool.iota(iota, pattern=[[0, T], [1, EXPERTS]], base=0, channel_multiplier=0,
                      allow_small_or_imprecise_dtypes=True).then_inc(k.aux.sem, 1)
            pool.iota(down, pattern=[[0, T], [-1, EXPERTS]], base=EXPERTS, channel_multiplier=0,
                      allow_small_or_imprecise_dtypes=True).then_inc(k.aux.sem, 1)
            pool.memset(last, 0.0).then_inc(k.aux.sem, 1)
            pool.wait_ge(k.aux.sem, k.aux.count(3))
            pool.affine_select(out=last, in_=last, compare_op=ALU.not_equal, fill=1.0, base=-(N - 1),
                               pattern=[[P, T]], channel_multiplier=1).then_inc(k.aux.sem, 1)

        @block.vector
        def _(dve):

            def do(ins):
                ins.then_inc(k.step.sem, 1)
                steps[0] += 1
                dve.wait_ge(k.step.sem, k.step.count(steps[0]))

            def best(scores, m, hot):
                do(dve.tensor_reduce(m, scores, AX.X, ALU.max))
                do(dve.tensor_tensor(key, scores, wide(m), ALU.is_equal))
                do(dve.tensor_tensor(key, key, down, ALU.mult))
                do(dve.tensor_reduce(s0, key, AX.X, ALU.max))
                do(dve.tensor_tensor(hot, key, wide(s0), ALU.is_equal))

            dve.wait_ge(k.aux.sem, k.aux.count(4))
            best(logits, m0, hot0)
            do(dve.scalar_tensor_tensor(work, hot0, -1e30, logits, ALU.mult, ALU.add))
            best(work, m1, hot1)
            do(dve.tensor_tensor(s1, m1, m0, ALU.subtract))
            dve.wait_ge(k.hi.sem, k.hi.count(1))
            do(dve.tensor_scalar(s0, s1, 1.0, None, ALU.add))
            do(dve.reciprocal(s0, s0))
            do(dve.tensor_tensor(s1, s1, s0, ALU.mult))
            if not capacity:
                do(dve.tensor_tensor(hot0, hot0, wide(s0), ALU.mult))
                do(dve.tensor_tensor(hot1, hot1, wide(s1), ALU.mult))
                do(dve.tensor_tensor(coef, hot0, hot1, ALU.add))
                return
            do(dve.tensor_copy(k.hots[:, 0, :, :], hot0))
            do(dve.tensor_tensor(k.hots[:, 1, :, :], hot0, hot1, ALU.add))
            dve.wait_ge(k.full.sem, k.full.count(1))
            for n, (hot, keep, idx) in enumerate(((hot0, keep0, idx0), (hot1, keep1, idx1))):
                do(dve.tensor_reduce(counts[:, n, :], k.bank[0][:, n * P:(n + 1) * P]
                                     .rearrange("p (t e) -> p e t", e=EXPERTS), AX.X, ALU.add))
                do(dve.tensor_scalar(counts[:, n, :], counts[:, n, :], float(N), None, ALU.is_ge))
                do(dve.tensor_tensor(work, hot, over_tokens(counts[:, n, :]), ALU.mult))
                do(dve.tensor_reduce(keep, work, AX.X, ALU.add))
                do(dve.tensor_tensor(keep, keep, last, ALU.mult))
                do(dve.tensor_scalar(keep, keep, -1.0, 1.0, ALU.mult, ALU.add))
                do(dve.tensor_tensor(work, hot, iota, ALU.mult))
                do(dve.tensor_reduce(idx, work, AX.X, ALU.add))
                do(dve.tensor_tensor(idx, idx, keep, ALU.mult))
            do(dve.tensor_tensor(idx0, idx0, idx1, ALU.max))
            do(dve.tensor_tensor(m0, s0, s1, ALU.add))
            do(dve.tensor_tensor(s0, s0, keep0, ALU.mult))
            do(dve.tensor_tensor(s1, s1, keep1, ALU.mult))
            do(dve.tensor_tensor(s0, s0, s1, ALU.add))
            do(dve.tensor_tensor(k.xweight[:, :], m0, s0, ALU.subtract))
            do(dve.tensor_tensor(hot0, iota, wide(idx0), ALU.is_equal))
            do(dve.tensor_tensor(coef, hot0, wide(s0), ALU.mult))

        before_exp = 12

        @block.scalar
        def _(act):
            act.wait_ge(k.step.sem, k.step.count(before_exp))
            act.activation(s1, s1, ACT.Exp).then_inc(k.hi.sem, 1)

        if capacity:

            @block.tensor
            def _(pe):
                pe.wait_ge(k.step.sem, k.step.count(before_exp + 5))
                pe.matmul(k.bank[0][:, 0:2 * P], k.ones128[:, :], k.hots[:, :, :, :].rearrange("p a t e -> p (a t e)"),
                          start=True, stop=True).then_inc(k.full.sem, 1)

    done(k, aux=4, step=steps[0], hi=1, full=int(capacity))


def act_stage(k, dst, src, func):
    nc = k.nc
    with nc.Block() as block:

        @block.scalar
        def _(act):
            for t in range(0, T, 4):
                act.activation(dst[:, t:t + 4, :], src[:, t:t + 4, :], func).then_inc(k.hi.sem, 1)

    done(k, hi=T // 4)


def weigh_experts(a32, coef):
    def make(dve, i, j, y, chain):
        t = tile_of(i, j)
        return dve.tensor_tensor(y.rearrange("p (e h) -> p e h", e=EXPERTS),
                                 a32[:, t, :].rearrange("p (e h) -> p e h", e=EXPERTS),
                                 coef[:, t, :].unsqueeze(2).to_broadcast([P, EXPERTS, D // EXPERTS]), ALU.mult)
    return make


def layer0_experts(k):
    xn, a32, hidden, t32 = k.F(0), k.T32(1), k.F(2), k.T32(3)
    logits, coef = routes(k)[0], routes(k)[7]
    router_stage(k, logits, k.rows[:, 0, 0:EXPERTS])
    top2_stage(k, capacity=True)
    w1 = use_weight(k)
    product_stage(k, lambda i, j: tokens_out(xn, w1, tile_of(i, j)),
                  lambda act, i, j, ps, y, chain: act.activation(a32[:, tile_of(i, j), :], ps, ACT.Copy),
                  value_on="scalar", copies=[(t32, all_tiles(k.ins["xn_dram"]))])
    w2 = use_weight(k)
    product_stage(k, lambda i, j: tokens_out(xn, w2, tile_of(i, j)),
                  lambda dve, i, j, ps, y, chain: dve.tensor_tensor(a32[:, tile_of(i, j), :], ps,
                                                                    a32[:, tile_of(i, j), :], ALU.mult))
    act_stage(k, a32, a32, ACT.Gelu)
    transpose_stage(k, weigh_experts(a32, coef), hidden)

    def value(dve, i, j, ps, y, chain):
        t = tile_of(i, j)
        chain(dve.tensor_tensor(k.x[:, t, :], ps, k.x[:, t, :], ALU.add), 1)
        return dve.scalar_tensor_tensor(k.x[:, t, :], t32[:, t, :], k.xweight[:, bass.ds(t, 1)], k.x[:, t, :],
                                        ALU.mult, ALU.add)

    w3 = use_weight(k)
    product_stage(k, lambda i, j: tokens_out(hidden, w3, tile_of(i, j)), value, steps=2, stats=k.x)


def layer1_experts(k):
    xn, a32, hidden, comb = k.F(0), k.T32(1), k.F(2), k.F(3)
    logits, coef = routes(k)[0], routes(k)[7]
    router_stage(k, logits)
    top2_stage(k, capacity=False)
    combine_stage(k, coef, comb)
    w1 = use_weight(k)

    def relu_row(dve, i, j, ps, y, chain):
        chain(dve.tensor_tensor(y, ps, k.rows[:, 0, :], ALU.add), 1)
        return dve.tensor_scalar(a32[:, tile_of(i, j), :], y, 0.0, None, ALU.max)

    product_stage(k, lambda i, j: tokens_out(xn, w1, tile_of(i, j)), relu_row, steps=2)
    transpose_stage(k, weigh_experts(a32, coef), hidden)
    add = lambda dve, i, j, ps, y, chain: dve.tensor_tensor(k.x[:, tile_of(i, j), :], ps, k.x[:, tile_of(i, j), :],
                                                            ALU.add)
    b2 = use_weight(k)
    product_stage(k, lambda i, j: tokens_out(comb, b2, tile_of(i, j), blocks=1), add)
    w2 = use_weight(k)
    product_stage(k, lambda i, j: tokens_out(hidden, w2, tile_of(i, j)), add, stats=k.x)


def combine_stage(k, coef, comb):
    nc = k.nc
    with nc.Block() as block:

        @block.gpsimd
        def _(pool):
            for h in range(2):
                pool.memset(comb[:, h * KC, :], 0.0).then_inc(k.aux.sem, 1)

        @block.tensor
        def _(pe):
            for t in range(T):
                last = pe.transpose(k.bank[t // 4][0:EXPERTS, t % 4 * P:(t % 4 + 1) * P], coef[:, t, :],
                                    k.identf[:, :])
                if t % 4 == 3:
                    last.then_inc(k.full.sem, 1)

        @block.vector
        def _(dve):
            dve.wait_ge(k.aux.sem, k.aux.count(2))
            for b in range(4):
                dve.wait_ge(k.full.sem, k.full.count(b + 1))
                hi = comb[0:EXPERTS, 0, b * CH:(b + 1) * CH]
                lo = comb[0:EXPERTS, KC, b * CH:(b + 1) * CH]
                ps = k.bank[b][0:EXPERTS, :]
                dve.tensor_copy(hi, ps).then_inc(k.step.sem, 1)
                dve.wait_ge(k.step.sem, k.step.count(2 * b + 1))
                dve.tensor_tensor(lo, ps, hi, ALU.subtract).then_inc(k.step.sem, 1)

    done(k, aux=2, full=4, step=8)


def assignments(k):
    return k.small[:, 0, 0:2].bitcast(I32), k.small[:, 1, 0:2]


def layer2_experts(k):
    nc, ins = k.nc, k.ins
    xn, a32, hidden = k.F(0), k.T32(1), k.F(2)
    _, key, _, _, idxf, iota, _, coef = routes(k)
    idx, ew = assignments(k)
    with nc.Block() as block:

        @block.gpsimd
        def _(pool):
            pool.iota(iota[:, 0, :], pattern=[[1, EXPERTS]], base=0, channel_multiplier=0,
                      allow_small_or_imprecise_dtypes=True).then_inc(k.aux.sem, 1)

        @block.vector
        def _(dve):
            n = [0]

            def do(ins):
                ins.then_inc(k.step.sem, 1)
                n[0] += 1
                dve.wait_ge(k.step.sem, k.step.count(n[0]))

            dve.wait_ge(k.aux.sem, k.aux.count(1))
            do(dve.tensor_copy(idxf[:, 0, 0:2], idx))
            for c in range(2):
                do(dve.tensor_scalar(key[:, c, :], iota[:, 0, :], idxf[:, 0, c:c + 1], ew[:, c:c + 1],
                                     ALU.is_equal, ALU.mult))
            do(dve.tensor_tensor(coef[:, 0, :], key[:, 0, :], key[:, 1, :], ALU.add))

    done(k, aux=1, step=4)
    w1 = use_weight(k)
    product_stage(k, lambda i, j: tokens_out(xn, w1, 0), lambda act, i, j, ps, y, chain:
                  act.activation(a32[:, 0, :], ps, ACT.Gelu), value_on="scalar", trips=1, width=1)
    tile0 = weigh_experts(a32, coef)
    transpose_stage(k, lambda dve, i, j, y, chain: tile0(dve, 0, 0, y, chain), hidden, trips=1, width=1)
    w2 = use_weight(k)
    product_stage(k, lambda i, j: tokens_out(hidden, w2, 0), lambda dve, i, j, ps, y, chain:
                  dve.tensor_tensor(k.x[:, 0, :], ps, k.x[:, 0, :], ALU.add), trips=1, width=1)



def whole_stage(k, vector=None, scalar=None, pool=None, sync=None):
    with k.nc.Block() as block:
        for eng, prog in ((block.vector, vector), (block.scalar, scalar), (block.gpsimd, pool), (block.sync, sync)):
            if prog is not None:
                eng(prog)


def turn_back_stage(k, make, dst):
    nc = k.nc
    with nc.Block() as block:

        @block.scalar
        def _(act):
            with act.Fori(0, LOOPS) as i:
                for j in range(RING):
                    act.wait_ge(k.valued.sem, i * RING + k.valued.count(j + 1))
                    make(act, i, j, k.tmp[:, j, :]).then_inc(k.aux.sem, 1)

        @block.tensor
        def _(pe):
            with pe.Fori(0, LOOPS) as i:
                for j in range(RING):
                    pe.wait_ge(k.aux.sem, i * RING + k.aux.count(j + 1))
                    for c in range(KC):
                        last = pe.transpose(k.bank[j][:, c * P:(c + 1) * P], k.tmp[:, j, c * P:(c + 1) * P],
                                            k.identf[:, :])
                    last.then_inc(k.full.sem, 1)

        @block.vector
        def _(dve):
            with dve.Fori(0, LOOPS) as i:
                for j in range(RING):
                    hi, lo = dst(i, j)
                    dve.wait_ge(k.full.sem, i * RING + k.full.count(j + 1))
                    dve.tensor_copy(hi, k.bank[j][:, :]).then_inc(k.hi.sem, 1)
                    dve.wait_ge(k.hi.sem, i * RING + k.hi.count(j + 1))
                    dve.tensor_tensor(lo, k.bank[j][:, :], hi, ALU.subtract).then_inc(k.valued.sem, 1)

    done(k, aux=T, hi=T, full=T, valued=T)


def context_stage(k, kt, v, ctx):
    nc = k.nc
    with nc.Block() as block:

        @block.tensor
        def _(pe):
            for b in range(KC + 1):
                pe.matmul(k.bank[b][:, :], k.zeros[:, 0:P], k.zeros[:, :], start=True, stop=False,
                          skip_group_check=True)
            with pe.Fori(0, T) as t:
                for f in range(KC):
                    hi, lo = kt[:, t, 0, f * P:(f + 1) * P], kt[:, t, 1, f * P:(f + 1) * P]
                    accumulate(pe, k.bank[f][:, :], [(hi, v[:, t, 0, :]), (hi, v[:, t, 1, :]), (lo, v[:, t, 0, :])],
                               start=False, stop=False)
                    accumulate(pe, k.bank[KC][:, f:f + 1], [(hi, k.ones[:, 0:1]), (lo, k.ones[:, 0:1])],
                               start=False, stop=False)
            for b in range(KC + 1):
                last = pe.matmul(k.bank[b][:, :], k.zeros[:, 0:P], k.zeros[:, :], start=False, stop=True,
                                 skip_group_check=True)
            last.then_inc(k.full.sem, 1)

        @block.vector
        def _(dve):
            dve.wait_ge(k.full.sem, k.full.count(1))
            r = k.small[:, 0, 0:KC]
            dve.reciprocal(r, k.bank[KC][:, 0:KC]).then_inc(k.step.sem, 1)
            dve.wait_ge(k.step.sem, k.step.count(1))
            for f in range(KC):
                dve.tensor_scalar(k.tmp[:, f, :], k.bank[f][:, :], r[:, f:f + 1], None, ALU.mult).then_inc(k.step.sem, 1)
            dve.wait_ge(k.step.sem, k.step.count(1 + KC))
            dve.tensor_copy(ctx[:, 0, :, :], k.tmp[:, :, :]).then_inc(k.step.sem, 1)
            dve.wait_ge(k.step.sem, k.step.count(2 + KC))
            dve.tensor_tensor(ctx[:, 1, :, :], k.tmp[:, :, :], ctx[:, 0, :, :], ALU.subtract).then_inc(k.step.sem, 1)

    done(k, full=1, step=KC + 3)


def layer1_mix(k):
    xn = k.F(0)
    kf32, kt, v = k.F32v(1), k.TH(2), k.TH(3)
    ctx = k.big[2][:, 0:2048].bitcast(BF16).rearrange("p (h c n) -> p h c n", h=2, c=KC)
    wk = use_weight(k)
    product_stage(k, lambda i, j: features_out(xn, wk, j, i),
                  lambda act, i, j, ps, y, chain: act.activation(kf32[:, j, bass.ts(i, CH)], ps, ACT.Copy),
                  value_on="scalar")
    top = k.small[:, 1, 0:KC]

    def key_max(dve):
        dve.tensor_reduce(top, kf32, AX.X, ALU.max, negate=True).then_inc(k.step.sem, 1)

    whole_stage(k, vector=key_max)
    done(k, step=1)

    def exp_keys(act, i, j, y):
        for c in range(KC):
            last = act.activation(y[:, c * P:(c + 1) * P], kf32[:, c, bass.ts(tile_of(i, j), P)], ACT.Exp,
                                  bias=top[:, c:c + 1])
        return last

    turn_back_stage(k, exp_keys, t_halves(kt))
    wv = use_weight(k)
    product_stage(k, lambda i, j: tokens_out(xn, wv, tile_of(i, j)), as_is, t_halves(v), value_on="scalar")
    context_stage(k, kt, v, ctx)
    wq = use_weight(k)
    q32, qf, t32 = k.T32(1), k.F(3), k.T32(1)
    product_stage(k, lambda i, j: tokens_out(xn, wq, tile_of(i, j)),
                  lambda act, i, j, ps, y, chain: act.activation(q32[:, tile_of(i, j), :], ps, ACT.Copy),
                  value_on="scalar")
    qtop, qsum = k.small[:, 2, :], k.small[:, 3, :]

    def query_rows(dve):
        dve.tensor_reduce(qtop, q32, AX.X, ALU.max, negate=True).then_inc(k.step.sem, 1)
        dve.wait_ge(k.hi.sem, k.hi.count(T))
        dve.reciprocal(qsum, qsum).then_inc(k.step.sem, 1)
        dve.wait_ge(k.step.sem, k.step.count(2))
        dve.tensor_scalar(qsum, qsum, D ** -0.5, None, ALU.mult).then_inc(k.step.sem, 1)

    def query_exp(act):
        act.wait_ge(k.step.sem, k.step.count(1))
        for t in range(T):
            act.activation(q32[:, t, :], q32[:, t, :], ACT.Exp, bias=qtop[:, t:t + 1],
                           accum_out=qsum[:, t:t + 1]).then_inc(k.hi.sem, 1)

    whole_stage(k, vector=query_rows, scalar=query_exp)
    done(k, step=3, hi=T)
    transpose_stage(k, lambda dve, i, j, y, chain: dve.tensor_scalar(
        y, q32[:, tile_of(i, j), :], qsum[:, bass.ds(tile_of(i, j), 1)], None, ALU.mult), qf)
    product_stage(k, lambda i, j: tokens_out(qf, ctx, tile_of(i, j)),
                  lambda dve, i, j, ps, y, chain: dve.tensor_tensor(t32[:, tile_of(i, j), :], ps,
                                                                    t32[:, tile_of(i, j), :], ALU.add), turn=False,
                  copies=[(t32, all_tiles(k.ins["xn_dram"]))], needs_copies=True)
    x2f, yf = k.F(2), k.F(3)
    transpose_stage(k, lambda dve, i, j, y, chain: dve.tensor_copy(y, t32[:, tile_of(i, j), :]), x2f)
    w1 = use_weight(k)
    product_stage(k, lambda i, j: features_out(x2f, w1, j, i), as_is, f_halves(yf), value_on="scalar")
    w2 = use_weight(k)
    product_stage(k, lambda i, j: tokens_out(yf, w2, tile_of(i, j)), add_to_x(k, t32), steps=2)


def add_to_x(k, t32, row=None):
    def value(dve, i, j, ps, y, chain):
        x = k.x[:, tile_of(i, j), :]
        if row is not None:
            chain(dve.tensor_tensor(y, ps, row, ALU.add), 1)
            chain(dve.tensor_tensor(x, x, y, ALU.add), 2)
        else:
            chain(dve.tensor_tensor(x, ps, x, ALU.add), 1)
        return dve.tensor_tensor(x, x, t32[:, tile_of(i, j), :], ALU.add)
    return value



def layer2_graph(k):
    nc = k.nc
    xn, z = k.F(0), k.F(2)
    tt = k.big[1][:, 0:2048].bitcast(BF16).rearrange("p (t h m) -> p t h m", t=T, h=2)
    ring = k.big[3][:, 0:RING * 1024].bitcast(BF16).rearrange("p (g s n) -> p g s n", g=RING, s=4)
    w1 = use_weight(k)

    def relu_row(dve, i, j, ps, y, chain):
        chain(dve.tensor_tensor(y, ps, k.rows[:, 0, 0:P], ALU.add), 1)
        return dve.tensor_scalar(y, y, 0.0, None, ALU.max)

    product_stage(k, lambda i, j: tokens_out(xn, w1, tile_of(i, j), n=P), relu_row,
                  lambda i, j: (tt[:, tile_of(i, j), 0, :], tt[:, tile_of(i, j), 1, :]), steps=2, cols_out=P)
    with nc.Block() as block:

        @block.sync
        def _(sp):
            with sp.Fori(0, NC) as i:
                for g in range(RING):
                    sp.wait_ge(k.aux2.sem, i * RING + k.aux2.count(g + 1))
                    sp.dma_start(ring[:, g, :, :], k.ins["a_dram"][4 * g:4 * g + 4, :, bass.ts(i, CH)]
                                 .rearrange("s p n -> p s n")).then_inc(k.ring[g].sem, 16)

        @block.tensor
        def _(pe):
            pe.sem_inc(k.aux2.sem, RING)
            with pe.Fori(0, NC) as i:
                pe.wait_ge(k.valued.sem, i + k.valued.count(RING))
                for g in range(RING):
                    pe.wait_ge(k.ring[g].sem, i * 16 + k.ring[g].count(32))
                    pairs = [(tt[:, 4 * g + s, h, :], ring[:, g, s, :]) for s in range(4) for h in range(2)]
                    accumulate(pe, k.bank[0][:, :], pairs, start=g == 0, stop=False).then_inc(k.aux2.sem, 1)
                for s in range(4):
                    pairs = [(tt[:, i * 4 + s, h, :], k.ident[:, :]) for h in range(2)]
                    last = accumulate(pe, k.bank[0][:, s * P:(s + 1) * P], pairs, start=False, stop=s == 3)
                last.then_inc(k.full.sem, 1)

        @block.vector
        def _(dve):
            with dve.Fori(0, NC) as i:
                hi, lo = z[:, 0, bass.ts(i, CH)], z[:, KC, bass.ts(i, CH)]
                dve.wait_ge(k.full.sem, i + k.full.count(1))
                dve.tensor_copy(hi, k.bank[0][:, :]).then_inc(k.step.sem, 1)
                dve.wait_ge(k.step.sem, i + k.step.count(1))
                dve.tensor_tensor(lo, k.bank[0][:, :], hi, ALU.subtract).then_inc(k.valued.sem, 1)

    done(k, aux2=RING * NC + RING, full=NC, valued=NC, step=NC)
    for g in range(RING):
        k.ring[g].base += 16 * NC
    w2 = use_weight(k)
    product_stage(k, lambda i, j: tokens_out(z, w2, tile_of(i, j), blocks=1),
                  lambda dve, i, j, ps, y, chain: dve.tensor_tensor(k.x[:, tile_of(i, j), :], ps,
                                                                    k.x[:, tile_of(i, j), :], ALU.add),
                  copies=[(k.T32(1), all_tiles(k.ins["xn_dram"])), *row_loads(k, "L2_mix_ln_gamma", "L2_mix_ln_beta")])


def layer2_mix(k):
    x2, q = k.F(0), k.F(1)
    kp, v, t32 = k.TH(2), k.TH(3), k.T32(1)
    ebuf = k.big[3][:, 0:RING * D].rearrange("p (r d) -> p r d", r=RING)
    moments_stage(k, t32, EPS)
    transpose_stage(k, normalise(k, t32, k.rows[:, 0, :], k.rows[:, 1, :]), x2, steps=3)
    bq = k.col("L2_mix_bq", KC)

    def elu(dve, y, e, j):
        return dve.scalar_tensor_tensor(y, e, 1.0, y, ALU.min, ALU.add)

    def q_value(dve, i, j, ps, y, chain):
        chain(dve.tensor_scalar(y, ps, bq[:, j:j + 1], 0.0, ALU.add, ALU.max), 1)
        return elu(dve, y, ebuf[:, j, :], j)

    wq = use_weight(k)
    product_stage(k, lambda i, j: features_out(x2, wq, j, i), q_value, f_halves(q), steps=2,
                  pre=lambda act, i, j, ps: act.activation(ebuf[:, j, :], ps, ACT.Exp, bias=bq[:, j:j + 1]),
                  copies=row_loads(k, "L2_mix_bk", "L2_mix_bv", "L2_mix_out_b"))
    wk = use_weight(k)
    t2 = k.T32(3)

    product_stage(k, lambda i, j: tokens_out(x2, wk, tile_of(i, j)),
                  lambda dve, i, j, ps, y, chain: dve.tensor_tensor(t2[:, tile_of(i, j), :], ps, k.rows[:, 0, :],
                                                                    ALU.add))
    elu_stage(k, t2, kp)
    wv = use_weight(k)
    product_stage(k, lambda i, j: tokens_out(x2, wv, tile_of(i, j)), plus_row(k.rows[:, 1, :]), t_halves(v))
    key_value_stage(k, kp, v, k.kv)
    linear_attention(k, q, k.kv, 1e-8, [(t2, all_tiles(k.ins["xn_dram"]))])
    wo = use_weight(k)
    product_stage(k, lambda i, j: tokens_out(q, wo, tile_of(i, j)), add_to_x(k, t2, k.rows[:, 2, :]), steps=3,
                  stats=k.x)


def elu_stage(k, src, dst):
    nc = k.nc
    with nc.Block() as block:

        @block.scalar
        def _(act):
            with act.Fori(0, LOOPS) as i:
                for j in range(RING):
                    act.wait_ge(k.lo.sem, i * RING + k.lo.count(j + 1))
                    act.activation(k.tmp[:, j, :], src[:, tile_of(i, j), :], ACT.Exp).then_inc(k.aux.sem, 1)
                for j in range(RING):
                    act.wait_ge(k.valued.sem, i * RING + k.valued.count(RING + j + 1))
                    act.activation(dst[:, tile_of(i, j), 0, :], k.tmp[:, j, :], ACT.Copy).then_inc(k.hi.sem, 1)

        @block.vector
        def _(dve):
            with dve.Fori(0, LOOPS) as i:
                for j in range(RING):
                    s = src[:, tile_of(i, j), :]
                    dve.wait_ge(k.aux.sem, i * RING + k.aux.count(j + 1))
                    dve.tensor_scalar(s, s, 0.0, None, ALU.max).then_inc(k.step.sem, 1)
                    dve.wait_ge(k.step.sem, i * RING + k.step.count(j + 1))
                    dve.scalar_tensor_tensor(k.tmp[:, j, :], k.tmp[:, j, :], 1.0, s, ALU.min,
                                             ALU.add).then_inc(k.valued.sem, 1)

        @block.gpsimd
        def _(pool):
            with pool.Fori(0, LOOPS) as i:
                for j in range(RING):
                    pool.wait_ge(k.hi.sem, i * RING + k.hi.count(j + 1))
                    pool.tensor_tensor(dst[:, tile_of(i, j), 1, :], k.tmp[:, j, :], dst[:, tile_of(i, j), 0, :],
                                       ALU.subtract).then_inc(k.lo.sem, 1)

    done(k, aux=T, valued=T, hi=T, lo=T, step=T)



def layer3_graph(k):
    nc, ins = k.nc, k.ins
    t32, h, u, xn32 = k.T32(1), k.F(2), k.TH(1), k.T32(0)
    ring = k.big[3][:, 0:RING * 1024].bitcast(BF16).rearrange("p (g s n) -> p g s n", g=RING, s=4)
    moments_stage(k, t32, EPS, row_loads(k, "L3_gnn_gamma", "L3_gnn_beta", "L3_gnn_b_l"))
    transpose_stage(k, normalise(k, t32, k.rows[:, 0, :], k.rows[:, 1, :]), h, steps=3)
    wl = use_weight(k)
    product_stage(k, lambda i, j: tokens_out(h, wl, tile_of(i, j)), as_is, t_halves(u), value_on="scalar")
    wr = use_weight(k)
    turn = WeightTurn(k)
    with nc.Block() as block:

        @block.sync
        def _(sp):
            turn.sync(sp)
            with sp.Fori(0, NC) as i:
                for g in range(RING):
                    sp.wait_ge(k.aux2.sem, i * RING + k.aux2.count(g + 1))
                    sp.dma_start(ring[:, g, :, :], ins["at_dram"][4 * g:4 * g + 4, :, bass.ts(i, CH)]
                                 .rearrange("s p n -> p s n")).then_inc(k.ring[g].sem, 16)

        @block.tensor
        def _(pe):
            pe.sem_inc(k.aux2.sem, RING)
            with pe.Fori(0, NC) as i:
                for g in range(RING):
                    pe.wait_ge(k.ring[g].sem, i * 16 + k.ring[g].count(32))
                    for j in range(4):
                        if g == 0:
                            pe.wait_ge(k.valued.sem, i * RING + k.valued.count(j + 1))
                        pairs = [(ring[:, g, s, j * P:(j + 1) * P], u[:, 4 * g + s, h_, :])
                                 for s in range(4) for h_ in range(2)]
                        last = accumulate(pe, k.bank[j][:, :], pairs, start=g == 0, stop=g == RING - 1)
                    last.then_inc(k.aux2.sem, 1)
                for j in range(4):
                    accumulate(pe, k.bank[RING + j][:, :], tokens_out(h, wr, tile_of(i, j))).then_inc(k.full.sem, 1)

        @block.vector
        def _(dve):
            turn.vector(dve)
            with dve.Fori(0, NC) as i:
                for j in range(4):
                    t, y = tile_of(i, j), k.tmp[:, j, :]
                    n = 0
                    dve.wait_ge(k.full.sem, i * RING + k.full.count(j + 1))

                    def do(ins_):
                        nonlocal n
                        ins_.then_inc(k.step.sem, 1)
                        n += 1
                        dve.wait_ge(k.step.sem, i * (RING * 4) + k.step.count(j * 4 + n))

                    do(dve.tensor_scalar(y, k.bank[j][:, :], k.rdegree[:, bass.ds(t, 1)], None, ALU.mult))
                    do(dve.tensor_tensor(y, y, k.rows[:, 2, :], ALU.add))
                    do(dve.tensor_tensor(y, k.bank[RING + j][:, :], y, ALU.add))
                    do(dve.scalar_tensor_tensor(y, y, 0.0, xn32[:, t, :], ALU.max, ALU.add))
                    dve.tensor_tensor(k.x[:, t, :], k.x[:, t, :], y, ALU.add).then_inc(k.valued.sem, 1)

        @block.scalar
        def _(act):
            turn.scalar(act)

    done(k, aux2=RING * NC + RING, full=T, valued=T, step=4 * T)
    for g in range(RING):
        k.ring[g].base += 16 * NC
    turn.finish()


def quantize_stage(k):
    nc = k.nc
    _, p, blocks, n, _ = k.staged_spec
    magic = 1.5 * 2.0 ** 23
    with nc.Block() as block:

        @block.scalar
        def _(act):
            act.wait_ge(k.staged.sem, k.staged.count(0))
            for c in range(blocks):
                act.activation(k.tmp[:, c, 0:n], k.staging[:, c, 0:n], ACT.Abs).then_inc(k.hi.sem, 1)

        @block.tensor
        def _(pe):
            for c in range(blocks):
                pe.wait_ge(k.hi.sem, k.hi.count(c + 1))
                pe.matmul(k.bank[c][:, 0:n], k.onesf[:, :], k.tmp[:, c, 0:n], start=True,
                          stop=True).then_inc(k.full.sem, 1)

        @block.vector
        def _(dve):
            count = 0
            for s in range(6):
                for c in range(blocks):
                    w, scale, y = k.staging[:, c, 0:n], k.bank[RING + c][:, 0:n], k.tmp[:, c, 0:n]
                    if s == 0:
                        dve.wait_ge(k.full.sem, k.full.count(c + 1))
                        ins = dve.tensor_scalar(scale, k.bank[c][:, 0:n], 1.0 / P, EPS, ALU.mult, ALU.add)
                    else:
                        dve.wait_ge(k.step.sem, k.step.count((s - 1) * blocks + c + 1))
                        if s == 1:
                            ins = dve.reciprocal(y, scale)
                        elif s == 2:
                            ins = dve.tensor_tensor(y, w, y, ALU.mult)
                        elif s == 3:
                            ins = dve.tensor_scalar(y, y, magic, magic, ALU.add, ALU.subtract)
                        elif s == 4:
                            ins = dve.tensor_scalar(y, y, -1.0, 1.0, ALU.max, ALU.min)
                        else:
                            ins = dve.tensor_tensor(w, y, scale, ALU.mult)
                    ins.then_inc(k.step.sem, 1)

    done(k, hi=blocks, full=blocks, step=6 * blocks)


def layer3_ffn(k):
    xn, gate, hidden = k.F(0), k.F32v(1), k.F(2)
    for n in (4, 4, 3):
        wg = use_weight(k)
        product_stage(k, lambda i, j: features_out(xn, wg, j, i),
                      lambda act, i, j, ps, y, chain: act.activation(gate[:, j, bass.ts(i, CH)], ps, ACT.Silu),
                      value_on="scalar", width=n)
        wu = use_weight(k)
        product_stage(k, lambda i, j: features_out(xn, wu, j, i),
                      lambda dve, i, j, ps, y, chain: dve.tensor_tensor(y, ps, gate[:, j, bass.ts(i, CH)], ALU.mult),
                      f_halves(hidden), width=n)
        wd = use_weight(k)
        product_stage(k, lambda i, j: tokens_out(hidden, wd, tile_of(i, j), blocks=n),
                      lambda dve, i, j, ps, y, chain: dve.tensor_tensor(k.x[:, tile_of(i, j), :], ps,
                                                                        k.x[:, tile_of(i, j), :], ALU.add))



HEADS, DH = 8, 64
FEATS = 266
R_CHUNKS = [(0, 128), (128, 128), (256, 10)]
KERNEL_EPS = 1e-4
UNIT = 4


class Performer:

    def __init__(self, k):
        w = k.big[0]
        n = UNIT * FEATS
        self.e = [w[:, g * n:(g + 1) * n].rearrange("p (h r) -> p h r", h=UNIT) for g in range(2)]
        self.kh = [w[:, (2 + g) * n:(3 + g) * n].bitcast(BF16).rearrange("p (a h r) -> p a h r", a=2, h=UNIT)
                   for g in range(2)]
        self.ctx = w[:, 4 * n:4 * n + 1584].bitcast(BF16).rearrange("p (c a h d) -> p c a h d", c=3, a=2, h=HEADS)
        w = k.kv[:, :, :, :, :].rearrange("p a b c d -> p (a b c d)").bitcast(F32)
        self.tops = w[:, 0:T * HEADS].rearrange("p (t h) -> p t h", t=T)
        self.stab = w[:, 128:130]
        self.halfsel = w[:, 130:132]
        self.bias = w[:, 132:140].rearrange("p (g h) -> p g h", g=2)
        self.top = w[:, 140:148].rearrange("p (g h) -> p g h", g=2)
        self.rden = w[:, 148:156].rearrange("p (g h) -> p g h", g=2)


def features_of(src, pj, t, g, bank):
    out = []
    for hh in range(UNIT):
        b = 2 * g + hh // 2
        hi, lo = src[:, b, bass.ts(t, P)], src[:, KC + b, bass.ts(t, P)]
        whi, wlo = pj[:, 0, hh % 2, 0:FEATS], pj[:, 1, hh % 2, 0:FEATS]
        out.append((bank[hh][:, 0:FEATS], [(hi, whi), (hi, wlo), (lo, whi)]))
    return out


def key_top_stage(k, pf, src, pj):
    nc = k.nc
    with nc.Block() as block:

        @block.tensor
        def _(pe):
            with pe.Fori(0, T) as t:
                for g in range(2):
                    pe.wait_ge(k.aux.sem, t * 2 + k.aux.count(g + 1))
                    for out, pairs in features_of(src, pj, t, g, k.bank[4 * g:4 * g + 4]):
                        last = accumulate(pe, out, pairs)
                    last.then_inc(k.full.sem, 1)

        @block.vector
        def _(dve):
            dve.sem_inc(k.aux.sem, 2)
            dve.tensor_scalar(pf.halfsel, k.headmask[:, 0:P:DH], 0.5, None, ALU.mult).then_inc(k.step.sem, 1)
            with dve.Fori(0, T) as t:
                for g in range(2):
                    dve.wait_ge(k.full.sem, t * 2 + k.full.count(g + 1))
                    for hh in range(UNIT):
                        last = dve.tensor_reduce(pf.tops[:, t, UNIT * g + hh:UNIT * g + hh + 1],
                                                 k.bank[4 * g + hh][:, 0:FEATS], AX.X, ALU.max)
                    last.then_inc(k.aux.sem, 1)
            dve.wait_ge(k.aux.sem, k.aux.count(2 * T + 2))
            dve.tensor_reduce(pf.stab[:, 1:2], pf.tops, AX.XY, ALU.max).then_inc(k.step.sem, 1)
            dve.wait_ge(k.aux2.sem, k.aux2.count(1))
            dve.tensor_scalar(pf.stab[:, 0:1], pf.stab[:, 0:1], -1.0, None, ALU.mult).then_inc(k.step.sem, 1)

        @block.gpsimd
        def _(pool):
            pool.wait_ge(k.step.sem, k.step.count(2))
            pool.partition_all_reduce(pf.stab[:, 0:1], pf.stab[:, 1:2], P,
                                      bass.bass_isa.ReduceOp.max).then_inc(k.aux2.sem, 1)

    done(k, aux=2 * T + 2, full=2 * T, step=3, aux2=1)


def squares(dve, k, src, t, g, n):
    y = k.tmp[:, g, 0:2 * P].rearrange("p (b n) -> p b n", b=2)
    dve.tensor_tensor(y, src[:, 2 * g:2 * g + 2, bass.ts(t, P)], src[:, KC + 2 * g:KC + 2 * g + 2, bass.ts(t, P)],
                      ALU.add).then_inc(k.step.sem, 1)
    n()
    dve.tensor_tensor(y, y, y, ALU.mult).then_inc(k.aux.sem, 1)


def unit_products(pe, k, pf, src, pj, t, g):
    for b in range(2):
        pe.matmul(k.bank[4][:, 300 + 2 * b:302 + 2 * b], k.tmp[:, g, b * P:(b + 1) * P], pf.halfsel,
                  start=True, stop=True, skip_group_check=True)
    for out, pairs in features_of(src, pj, t, g, k.bank[4:8]):
        last = accumulate(pe, out, pairs)
    last.then_inc(k.full.sem, 1)


def key_features_stage(k, pf, src, v, pj):
    nc = k.nc
    ratio = FEATS ** -0.5
    with nc.Block() as block:

        @block.tensor
        def _(pe):
            for b in range(4):
                pe.matmul(k.bank[b][:, :], k.zeros[:, 0:P], k.zeros[:, :], start=True, stop=False,
                          skip_group_check=True)
            with pe.Fori(0, T) as t:
                for g in range(2):
                    pe.wait_ge(k.aux.sem, t * 2 + k.aux.count(g + 1))
                    pe.wait_ge(k.valued.sem, t * 2 + k.valued.count(RING + g))
                    unit_products(pe, k, pf, src, pj, t, g)
                for g in range(2):
                    pe.wait_ge(k.lo.sem, t * 2 + k.lo.count(RING + g + 1))
                    for hh in range(UNIT):
                        h = UNIT * g + hh
                        for c, (r0, m) in enumerate(R_CHUNKS):
                            hi, lo = (pf.kh[g][:, a, hh, r0:r0 + m] for a in range(2))
                            vh, vl = (v[:, t, a, h * DH:(h + 1) * DH] for a in range(2))
                            accumulate(pe, k.bank[c][0:m, h * DH:(h + 1) * DH], [(hi, vh), (hi, vl), (lo, vh)],
                                       start=False, stop=False)
                            last = accumulate(pe, k.bank[3][0:m, 8 * c + h:8 * c + h + 1],
                                              [(hi, k.ones[:, 0:1]), (lo, k.ones[:, 0:1])], start=False, stop=False)
                    last.then_inc(k.aux2.sem, 1)
            for b in range(4):
                last = pe.matmul(k.bank[b][:, :], k.zeros[:, 0:P], k.zeros[:, :], start=False, stop=True,
                                 skip_group_check=True)
            last.then_inc(k.full.sem, 1)

        @block.vector
        def _(dve):
            with dve.Fori(0, T) as t:
                for g in range(2):
                    if g == 0:
                        dve.wait_ge(k.full.sem, t * 2 + k.full.count(0))
                    squares(dve, k, src, t, g, lambda: dve.wait_ge(k.step.sem, t * 4 + k.step.count(g + 1)))
                for g in range(2):
                    dve.wait_ge(k.full.sem, t * 2 + k.full.count(g + 1))
                    dve.wait_ge(k.valued.sem, t * 2 + k.valued.count(RING + g - 2 + 2))
                    dve.tensor_scalar(pf.bias[:, g, :], k.bank[4][:, 300:304], -1.0, pf.stab[:, 0:1], ALU.mult,
                                      ALU.add).then_inc(k.step.sem, 1)
                    dve.wait_ge(k.valued.sem, t * 2 + k.valued.count(RING + g + 1))
                    dve.tensor_scalar(pf.e[g], pf.e[g], KERNEL_EPS, ratio, ALU.add, ALU.mult).then_inc(k.astep.sem, 1)

        @block.scalar
        def _(act):
            with act.Fori(0, T) as t:
                for g in range(2):
                    act.wait_ge(k.step.sem, t * 4 + k.step.count(3 + g))
                    act.wait_ge(k.lo.sem, t * 2 + k.lo.count(RING + g - 1))
                    for hh in range(UNIT):
                        last = act.activation(pf.e[g][:, hh, :], k.bank[4 + hh][:, 0:FEATS], ACT.Exp,
                                              bias=pf.bias[:, g, hh:hh + 1])
                    last.then_inc(k.valued.sem, 1)
                    act.wait_ge(k.astep.sem, t * 2 + k.astep.count(g + 1))
                    act.wait_ge(k.aux2.sem, t * 2 + k.aux2.count(g + 1))
                    act.activation(pf.kh[g][:, 0, :, :], pf.e[g], ACT.Copy).then_inc(k.hi.sem, 1)

        @block.gpsimd
        def _(pool):
            pool.sem_inc(k.aux2.sem, 2)
            with pool.Fori(0, T) as t:
                for g in range(2):
                    pool.wait_ge(k.hi.sem, t * 2 + k.hi.count(g + 1))
                    pool.tensor_tensor(pf.kh[g][:, 1, :, :], pf.e[g], pf.kh[g][:, 0, :, :],
                                       ALU.subtract).then_inc(k.lo.sem, 1)

    done(k, aux=2 * T, full=2 * T + 1, valued=2 * T, step=4 * T, astep=2 * T, hi=2 * T, lo=2 * T, aux2=2 * T + 2)


def performer_context_stage(k, pf):
    with k.nc.Block() as block:

        @block.vector
        def _(dve):
            for s in range(2):
                for c, (_, m) in enumerate(R_CHUNKS):
                    for ps, d in ((k.bank[c][0:m, :].rearrange("p (h d) -> p h d", h=HEADS), slice(0, DH)),
                                  (k.bank[3][0:m, 8 * c:8 * c + 8].unsqueeze(2), slice(DH, DH + 1))):
                        hi, lo = (pf.ctx[0:m, c, a, :, d] for a in range(2))
                        if s == 0:
                            dve.tensor_copy(hi, ps).then_inc(k.step.sem, 1)
                        else:
                            dve.wait_ge(k.step.sem, k.step.count(6))
                            dve.tensor_tensor(lo, ps, hi, ALU.subtract).then_inc(k.step.sem, 1)

    done(k, step=12)


def query_features_stage(k, pf, src, pj, qt, out):
    nc = k.nc
    ratio = FEATS ** -0.5
    ncol = DH + 1
    with nc.Block() as block:

        @block.tensor
        def _(pe):
            with pe.Fori(0, T) as t:
                for g in range(2):
                    pe.wait_ge(k.aux.sem, t * 2 + k.aux.count(g + 1))
                    pe.wait_ge(k.valued.sem, t * 2 + k.valued.count(RING + g))
                    unit_products(pe, k, pf, src, pj, t, g)
                for g in range(2):
                    pe.wait_ge(k.astep.sem, t * 2 + k.astep.count(g + 1))
                    pe.wait_ge(k.lo.sem, t * 2 + k.lo.count(RING + g))
                    for c, (r0, m) in enumerate(R_CHUNKS):
                        for hh in range(UNIT):
                            last = pe.transpose(k.bank[c][0:m, hh * P:(hh + 1) * P], pf.e[g][:, hh, r0:r0 + m],
                                                k.identf[:, :])
                    last.then_inc(k.aux2.sem, 1)
                    pe.wait_ge(k.lo.sem, t * 2 + k.lo.count(RING + g + 1))
                    pe.wait_ge(k.whi.sem, t * 2 + k.whi.count(g + 1))
                    for hh in range(UNIT):
                        pairs = []
                        for c, (r0, m) in enumerate(R_CHUNKS):
                            qh, ql = (qt[0:m, c, a, hh * P:(hh + 1) * P] for a in range(2))
                            ch, cl = (pf.ctx[0:m, c, a, UNIT * g + hh, 0:ncol] for a in range(2))
                            pairs += [(qh, ch), (qh, cl), (ql, ch)]
                        last = accumulate(pe, k.bank[3][:, hh * ncol:(hh + 1) * ncol], pairs)
                    last.then_inc(k.wlo.sem, 1)

        @block.vector
        def _(dve):
            dve.sem_inc(k.whi.sem, 1)
            with dve.Fori(0, T) as t:
                for g in range(2):
                    if g == 0:
                        dve.wait_ge(k.full.sem, t * 2 + k.full.count(0))
                    squares(dve, k, src, t, g, lambda: dve.wait_ge(k.step.sem, t * 6 + k.step.count(g + 1)))
                for g in range(2):
                    dve.wait_ge(k.full.sem, t * 2 + k.full.count(g + 1))
                    for hh in range(UNIT):
                        last = dve.tensor_reduce(pf.top[:, g, hh:hh + 1], k.bank[4 + hh][:, 0:FEATS], AX.X, ALU.max)
                    last.then_inc(k.step.sem, 1)
                    dve.wait_ge(k.step.sem, t * 6 + k.step.count(3 + 2 * g))
                    dve.scalar_tensor_tensor(pf.bias[:, g, :], k.bank[4][:, 300:304], -1.0, pf.top[:, g, :],
                                             ALU.mult, ALU.subtract).then_inc(k.step.sem, 1)
                    dve.wait_ge(k.valued.sem, t * 2 + k.valued.count(RING + g + 1))
                    dve.tensor_scalar(pf.e[g], pf.e[g], KERNEL_EPS, ratio, ALU.add, ALU.mult).then_inc(k.astep.sem, 1)
                for g in range(2):
                    dve.wait_ge(k.hi.sem, t * 2 + k.hi.count(g + 1))
                    for c, (_, m) in enumerate(R_CHUNKS):
                        last = dve.tensor_tensor(qt[0:m, c, 1, :], k.bank[c][0:m, :], qt[0:m, c, 0, :], ALU.subtract)
                    last.then_inc(k.lo.sem, 1)
                    num = k.bank[3][:, 0:UNIT * ncol].rearrange("p (h d) -> p h d", h=UNIT)
                    dve.wait_ge(k.wlo.sem, t * 2 + k.wlo.count(g + 1))
                    dve.reciprocal(pf.rden[:, g, :].unsqueeze(2), num[:, :, DH:ncol]).then_inc(k.staged.sem, 1)
                    dve.wait_ge(k.staged.sem, t * 2 + k.staged.count(g + 1))
                    dve.tensor_tensor(out[:, t, UNIT * g * DH:UNIT * (g + 1) * DH].rearrange("p (h d) -> p h d", h=UNIT),
                                      num[:, :, 0:DH], pf.rden[:, g, :].unsqueeze(2).to_broadcast([P, UNIT, DH]),
                                      ALU.mult).then_inc(k.whi.sem, 1)

        @block.scalar
        def _(act):
            with act.Fori(0, T) as t:
                for g in range(2):
                    act.wait_ge(k.step.sem, t * 6 + k.step.count(4 + 2 * g))
                    if g == 0:
                        act.wait_ge(k.aux2.sem, t * 2 + k.aux2.count(0))
                    for hh in range(UNIT):
                        last = act.activation(pf.e[g][:, hh, :], k.bank[4 + hh][:, 0:FEATS], ACT.Exp,
                                              bias=pf.bias[:, g, hh:hh + 1])
                    last.then_inc(k.valued.sem, 1)
                for g in range(2):
                    act.wait_ge(k.aux2.sem, t * 2 + k.aux2.count(g + 1))
                    act.wait_ge(k.wlo.sem, t * 2 + k.wlo.count(g))
                    for c, (_, m) in enumerate(R_CHUNKS):
                        last = act.activation(qt[0:m, c, 0, :], k.bank[c][0:m, :], ACT.Copy)
                    last.then_inc(k.hi.sem, 1)

    n = 2 * T
    done(k, aux=n, full=n, valued=n, step=6 * T, astep=n, hi=n, lo=n, aux2=n, whi=n + 1, wlo=n, staged=n)


def layer3_mix(k):
    xn, kf, v, qf = k.F(0), k.F(1), k.TH(2), k.F(3)
    norm = float(DH) ** -0.25
    scaled = lambda act, i, j, ps, y, chain: act.activation(y, ps, ACT.Copy, scale=norm)
    wq = use_weight(k)
    product_stage(k, lambda i, j: features_out(xn, wq, j, i), scaled, f_halves(qf), value_on="scalar")
    wk = use_weight(k)
    product_stage(k, lambda i, j: features_out(xn, wk, j, i), scaled, f_halves(kf), value_on="scalar")
    wv = use_weight(k)
    product_stage(k, lambda i, j: tokens_out(xn, wv, tile_of(i, j)), as_is, t_halves(v), value_on="scalar")
    pj = use_weight(k)
    pf = Performer(k)
    key_top_stage(k, pf, kf, pj)
    key_features_stage(k, pf, kf, v, pj)
    performer_context_stage(k, pf)
    qt = k.big[1][:, 0:1536].bitcast(BF16).rearrange("p (c a n) -> p c a n", c=3, a=2)
    attn = k.T32(2)
    query_features_stage(k, pf, qf, pj, qt, attn)
    af, t32 = k.F(1), k.T32(2)
    transpose_stage(k, lambda dve, i, j, y, chain: dve.tensor_copy(y, attn[:, tile_of(i, j), :]), af, turn=True)

    def add_t32(row):
        def value(dve, i, j, ps, y, chain):
            t = t32[:, tile_of(i, j), :]
            if row is None:
                return dve.tensor_tensor(t, ps, t, ALU.add)
            chain(dve.tensor_tensor(y, ps, row, ALU.add), 1)
            return dve.tensor_tensor(t, y, t, ALU.add)
        return value

    wo = use_weight(k)
    product_stage(k, lambda i, j: tokens_out(af, wo, tile_of(i, j)), add_t32(k.rows[:, 0, :]), steps=2,
                  copies=[*row_loads(k, "L3_mix_bo", "L3_mix_ln0_g", "L3_mix_ln0_b"),
                          (t32, all_tiles(k.ins["xn_dram"]))], needs_copies=True, stats=t32)
    moments_stage(k, t32, EPS, tiles=0)
    h = k.F(0)
    transpose_stage(k, normalise(k, t32, k.rows[:, 1, :], k.rows[:, 2, :]), h, steps=3, store=tile_in(t32))
    for part, dst in enumerate((k.F(1), k.F(3))):
        w1 = use_weight(k)
        b1 = k.cols[:, k.ins["col_index"]["L3_mix_b1"] + KC * part:][:, 0:KC]
        product_stage(k, lambda i, j: features_out(h, w1, j, i), lambda act, i, j, ps, y, chain:
                      act.activation(y, ps, ACT.Gelu, bias=b1[:, j:j + 1]), f_halves(dst), value_on="scalar",
                      copies=() if part else row_loads(k, "L3_mix_b2", "L3_mix_ln1_g", "L3_mix_ln1_b"))
    xn_dram = all_tiles(k.ins["xn_dram"])
    for part, src in enumerate((k.F(1), k.F(3))):
        w2 = use_weight(k)
        product_stage(k, lambda i, j: tokens_out(src, w2, tile_of(i, j)), add_t32(None if part else k.rows[:, 0, :]),
                      steps=1 if part else 2, stats=t32 if part else None,
                      copies=[(k.T32(1), xn_dram), (k.T32(0), xn_dram)] if part else ())
    moments_stage(k, t32, EPS, tiles=0)
    norm_add_stage(k, t32, k.rows[:, 1, :], k.rows[:, 2, :])



TILES = E // P
PAIRS = TILES // 2
NOWHERE = 4096.0


def edge_range_stage(k, dst_f, src_f, table):
    nc, ins = k.nc, k.ins
    w = k.big[3]
    raw = w[:, 0:2 * TILES].bitcast(I32).rearrange("p (a t) -> p a t", a=2)
    consts = w[:, 600:600 + 6 + 2 * T]
    reach = w[:, 700:706]
    near = w[:, 710:710 + T]
    cand = w[:, 800:800 + 6 * T].rearrange("p (g a b) -> p g a b", g=3, a=2)
    ends = w[0:T, 1000:1002]
    row = w[0:1, 1010:1010 + 5 * T].rearrange("p (a b) -> p a b", a=5)
    groups = [min(P, TILES - g * P) for g in range(3)]
    with nc.Block() as block:

        @block.sync
        def _(sp):
            sp.dma_start(raw[:, 0, :], ins["dst"]).then_inc(k.loaded.sem, 16)
            sp.dma_start(raw[:, 1, :], ins["src"]).then_inc(k.loaded.sem, 16)
            sp.dma_start(consts, ins["edge_consts"]).then_inc(k.loaded.sem, 16)
            sp.dma_start(k.iota, ins["iota"].rearrange("a n -> (a n)").partition_broadcast(P)
                         ).then_inc(k.loaded.sem, 16)

        @block.tensor
        def _(pe):
            pe.wait_ge(k.aux.sem, k.aux.count(1))
            for g, n in enumerate(groups):
                last = pe.transpose(k.bank[g][0:n, 0:P], dst_f[:, g * P:g * P + n], k.identf[:, :])
            last.then_inc(k.full.sem, 1)
            pe.wait_ge(k.aux.sem, k.aux.count(2))
            for a in range(2):
                for g in range(3):
                    last = pe.transpose(k.bank[4 + a][0:T, g * P:(g + 1) * P], cand[:, g, a, :], k.identf[:, :])
            last.then_inc(k.full.sem, 1)
            pe.wait_ge(k.aux.sem, k.aux.count(3))
            for a in range(2):
                last = pe.transpose(k.bank[6][0:1, a * T:(a + 1) * T], ends[:, a:a + 1], k.identf[0:T, 0:T])
            last.then_inc(k.full.sem, 1)

        @block.vector
        def _(dve):
            n = [0]

            def do(x, sig=None):
                if sig is not None:
                    x.then_inc(sig.sem, 1)
                    return
                x.then_inc(k.step.sem, 1)
                n[0] += 1
                dve.wait_ge(k.step.sem, k.step.count(n[0]))

            dve.wait_ge(k.loaded.sem, k.loaded.count(64))
            do(dve.tensor_copy(dst_f, raw[:, 0, :]), k.aux)
            do(dve.tensor_copy(src_f, raw[:, 1, :]))
            do(dve.memset(reach[:, 0:3], NOWHERE))
            do(dve.memset(reach[:, 3:6], -1.0))
            dve.wait_ge(k.full.sem, k.full.count(1))
            for g, m in enumerate(groups):
                do(dve.tensor_reduce(reach[0:m, g:g + 1], k.bank[g][0:m, 0:P], AX.X, ALU.min))
                do(dve.tensor_reduce(reach[0:m, 3 + g:4 + g], k.bank[g][0:m, 0:P], AX.X, ALU.max))
            start, end = consts[:, 6:6 + T], consts[:, 6 + T:6 + 2 * T]
            for g in range(3):
                do(dve.tensor_scalar(near, end, reach[:, g:g + 1], None, ALU.is_gt))
                do(dve.scalar_tensor_tensor(near, start, reach[:, 3 + g:4 + g], near, ALU.is_le, ALU.mult))
                do(dve.tensor_scalar(cand[:, g, 0, :], near, consts[:, 3 + g:4 + g], NOWHERE, ALU.mult, ALU.add))
                do(dve.tensor_scalar(cand[:, g, 1, :], near, consts[:, g:g + 1], None, ALU.mult))
            dve.sem_inc(k.aux.sem, 1)
            dve.wait_ge(k.full.sem, k.full.count(2))
            do(dve.tensor_reduce(ends[:, 0:1], k.bank[4][0:T, 0:3 * P], AX.X, ALU.min))
            do(dve.tensor_reduce(ends[:, 1:2], k.bank[5][0:T, 0:3 * P], AX.X, ALU.max))
            do(dve.tensor_tensor(ends[:, 0:1], ends[:, 0:1], ends[:, 1:2], ALU.min))
            dve.sem_inc(k.aux.sem, 1)
            dve.wait_ge(k.full.sem, k.full.count(3))
            do(dve.tensor_copy(row[:, 0:2, :], k.bank[6][0:1, 0:2 * T].rearrange("p (a b) -> p a b", a=2)))
            do(dve.tensor_scalar(row[:, 1, :], row[:, 1, :], 1.0, None, ALU.add))
            do(dve.tensor_tensor(row[:, 2, :], row[:, 1, :], row[:, 0, :], ALU.subtract))
            do(dve.tensor_copy(row[:, 3, :], row[:, 2, :]))
            a, b = 3, 4
            for s in (1, 2, 4, 8):
                do(dve.tensor_copy(row[:, b, 0:s], row[:, a, 0:s]))
                do(dve.tensor_tensor(row[:, b, s:T], row[:, a, s:T], row[:, a, 0:T - s], ALU.add))
                a, b = b, a
            do(dve.tensor_tensor(row[:, 1, :], row[:, a, :], row[:, 2, :], ALU.subtract))
            do(dve.tensor_copy(row[:, 2, :], row[:, a, :]))
            do(dve.tensor_copy(table, row[:, 0:3, :]))
            k.range_steps = n[0]

    done(k, loaded=64, aux=3, full=3, step=k.range_steps)


def adjacency_stage(k, dst_f, src_f, table, a):
    nc = k.nc
    hot_src = k.tmp[:, :, :].rearrange("p r n -> p (r n)").bitcast(BF16).rearrange("p (s n) -> p s n", s=2)
    hot_dst = k.kv[:, 0, 0, :, :]
    with nc.Block() as block:

        def block_range(eng, b, *names):
            top = (PAIRS - 1, T * PAIRS, T * PAIRS)
            return [eng.value_load(table[0:1, n, bass.ds(b, 1)], min_val=0, max_val=top[n]) for n in names]

        @block.vector
        def _(dve):
            dve.sem_inc(k.hot_used.sem, 2)
            with dve.Fori(0, T) as b:
                first, before, end = block_range(dve, b, 0, 1, 2)
                with dve.Fori(before, end) as q:
                    pair = nc.s_assert_within(q + first - before, 0, PAIRS - 1, skip_runtime_bounds_check_because=(
                        "q runs over as many pairs as the block's range has, and the range lies within all pairs"))
                    for s in range(2):
                        e = pair * 2 + s
                        dve.wait_ge(k.hot_used.sem, q * 2 + (s + 1))
                        dve.tensor_scalar(hot_dst[:, s, :], k.iota[:, bass.ts(b, P)], dst_f[:, bass.ds(e, 1)], None,
                                          ALU.is_equal).then_inc(k.hot_ready.sem, 1)
                        dve.tensor_scalar(hot_src[:, s, :], k.iota, src_f[:, bass.ds(e, 1)], None,
                                          ALU.is_equal).then_inc(k.hot_ready.sem, 1)

        @block.tensor
        def _(pe):
            with pe.Fori(0, T // 2) as i:
                for h in range(2):
                    b = i * 2 + h
                    before, end = block_range(pe, b, 1, 2)
                    pe.wait_ge(k.step.sem, b + k.step.count(1))
                    for c in range(NC):
                        pe.matmul(k.bank[4 * h + c], k.zeros[:, 0:P], k.zeros[:, :], start=True, stop=False,
                                  skip_group_check=True)
                    with pe.Fori(before, end) as q:
                        for s in range(2):
                            pe.wait_ge(k.hot_ready.sem, q * 4 + (2 * s + 2))
                            for c in range(NC):
                                m = pe.matmul(k.bank[4 * h + c], hot_dst[:, s, :],
                                              hot_src[:, s, c * CH:(c + 1) * CH], start=False, stop=False,
                                              skip_group_check=True)
                            m.then_inc(k.hot_used.sem, 1)
                    pe.matmul(k.bank[4 * h + NC - 1], k.zeros[:, 0:P], k.zeros[:, :], start=False, stop=True,
                              skip_group_check=True).then_inc(k.full.sem, 1)

        @block.scalar
        def _(act):
            act.sem_inc(k.step.sem, 2)
            with act.Fori(0, T // 2) as i:
                for h in range(2):
                    act.wait_ge(k.full.sem, i * 2 + k.full.count(h + 1))
                    act.activation(a[:, bass.ds(i * 2 + h, 1), :].rearrange("p a n -> p (a n)"),
                                   k.psum[:, 4 * h:4 * h + 4, :].rearrange("p a n -> p (a n)"),
                                   ACT.Copy).then_inc(k.step.sem, 1)

    done(k, full=T, step=T + 2)


def adjacency_out_stage(k, a, at):
    nc, ins = k.nc, k.ins
    with nc.Block() as block:

        @block.tensor
        def _(pe):
            with pe.Fori(0, T) as s:
                for c in range(NC):
                    pe.wait_ge(k.valued.sem, s * NC + k.valued.count(c + 1))
                    for d in range(4):
                        last = pe.matmul(k.bank[c][:, d * P:(d + 1) * P], a[:, 4 * c + d, bass.ts(s, P)],
                                         k.ident[:, :], start=True, stop=True)
                    last.then_inc(k.full.sem, 1)

        @block.scalar
        def _(act):
            with act.Fori(0, T) as s:
                for c in range(NC):
                    act.wait_ge(k.full.sem, s * NC + k.full.count(c + 1))
                    act.activation(at[:, bass.ds(s, 1), c * CH:(c + 1) * CH].rearrange("p a n -> p (a n)"),
                                   k.bank[c], ACT.Copy).then_inc(k.valued.sem, 1)

        @block.vector
        def _(dve):
            for b in range(T):
                dve.tensor_reduce(k.rdegree[:, b:b + 1], a[:, b, :], AX.X, ALU.add).then_inc(k.step.sem, 1)
            dve.wait_ge(k.step.sem, k.step.count(T))
            dve.tensor_scalar(k.rdegree[:, :], k.rdegree[:, :], 1.0, None, ALU.max).then_inc(k.step.sem, 1)
            dve.wait_ge(k.step.sem, k.step.count(T + 1))
            dve.reciprocal(k.rdegree[:, :], k.rdegree[:, :]).then_inc(k.step.sem, 1)

        @block.sync
        def _(sp):
            sp.dma_start(ins["a_dram"].rearrange("t p n -> p t n"), a).then_inc(k.loaded.sem, 16)
            for s in range(T):
                sp.wait_ge(k.valued.sem, k.valued.count(RING + NC * (s + 1)))
                sp.dma_start(ins["at_dram"][s], at[:, s, :]).then_inc(k.aux.sem, 16)
            sp.wait_ge(k.aux.sem, k.aux.count(16 * T))
            sp.wait_ge(k.loaded.sem, k.loaded.count(16))

    done(k, full=T * NC, valued=T * NC, step=T + 2, loaded=16, aux=16 * T)


def graph_stages(k):
    whole = k.big_pair(0)
    dst_f, src_f = k.big[2][:, 0:TILES], k.big[2][:, TILES:2 * TILES]
    edge_range_stage(k, dst_f, src_f, k.table[:, :, :])
    adjacency_stage(k, dst_f, src_f, k.table, whole)
    adjacency_out_stage(k, whole, k.big_pair(2))



NEVER = -1e30


def edge_max_stage(k, q_dram, k_dram, top):
    nc, ins = k.nc, k.ins
    keys = [k.big[2 + a][:, :].bitcast(BF16).rearrange("p (h n) -> p h n", h=HEADS) for a in range(2)]
    w = k.big[1][:, :].bitcast(BF16)
    counts = w[:, 0:2 * N].rearrange("p (b n) -> p b n", b=2)
    mask = w[:, 2 * N:4 * N].rearrange("p (b n) -> p b n", b=2)
    qa = w[:, 4 * N:4 * N + 2 * HEADS * P].rearrange("p (b h n) -> p b h n", b=2, h=HEADS)
    scratch = w[:, 5 * N:7 * N].rearrange("p (b n) -> p b n", b=2)
    with nc.Block() as block:

        @block.sync
        def _(sp):
            for a in range(2):
                for r in range(2):
                    sp.dma_start(keys[a][r * DH:(r + 1) * DH, :, :],
                                 k_dram[a].rearrange("(h d) n -> d h n", d=DH)).then_inc(k.loaded.sem, 16)
            with sp.Fori(0, T // 2) as i:
                for b in range(2):
                    t = i * 2 + b
                    sp.wait_ge(k.aux.sem, t + k.aux.count(1))
                    sp.dma_start(counts[:, b, :], ins["a_dram"][bass.ds(t, 1), :, :].rearrange("a p n -> p (a n)")
                                 ).then_inc(k.ring[b].sem, 16)
                    sp.wait_ge(k.valued.sem, t * HEADS + k.valued.count(RING - HEADS))
                    for a in range(2):
                        sp.dma_start(qa[a * DH:(a + 1) * DH, b, :, :],
                                     q_dram[a, :, bass.ts(t, P)].rearrange("(h d) n -> d h n", d=DH)
                                     ).then_inc(k.ring[2 + b].sem, 16)

        @block.tensor
        def _(pe):
            pe.wait_ge(k.loaded.sem, k.loaded.count(64))
            with pe.Fori(0, T // 2) as i:
                for b in range(2):
                    pe.wait_ge(k.ring[2 + b].sem, i * 32 + k.ring[2 + b].count(16 + 32))
                    for h in range(HEADS):
                        pe.wait_ge(k.valued.sem, i * (2 * HEADS) + k.valued.count(RING - 1 + b * HEADS + h))
                        for c in range(NC):
                            pairs = [(qa[:, b, h, :], keys[a][:, h, c * CH:(c + 1) * CH]) for a in range(2)]
                            last = accumulate(pe, k.bank[4 * (h % 2) + c], pairs)
                        last.then_inc(k.full.sem, 1)

        @block.vector
        def _(dve):
            dve.sem_inc(k.aux.sem, 2)
            with dve.Fori(0, T // 2) as i:
                for b in range(2):
                    t = i * 2 + b
                    dve.wait_ge(k.ring[b].sem, i * 16 + k.ring[b].count(32))
                    dve.tensor_scalar(mask[:, b, :], counts[:, b, :], 0.0, NEVER, ALU.is_equal,
                                      ALU.mult).then_inc(k.aux.sem, 1)
                    dve.wait_ge(k.aux.sem, t + k.aux.count(3))
                    dve.wait_ge(k.step.sem, t + k.step.count(0))
                    for h in range(HEADS):
                        dve.wait_ge(k.full.sem, i * (2 * HEADS) + k.full.count(b * HEADS + h + 1))
                        dve.wait_ge(k.valued.sem, i * (2 * HEADS) + k.valued.count(RING - 1 + b * HEADS + h))
                        g = 4 * (h % 2)
                        dve.nop(nofuse=True)
                        dve.tensor_tensor_reduce(
                            scratch[:, h % 2, :], k.psum[:, g:g + 4, :].rearrange("p a n -> p (a n)"), mask[:, b, :],
                            1.0, -3e38, ALU.add, ALU.max, k.tile_top[:, h:h + 1]).then_inc(k.valued.sem, 1)
                    dve.wait_ge(k.valued.sem, t * HEADS + k.valued.count(RING + HEADS))
                    dve.tensor_copy(top[:, bass.ds(t, 1), :].rearrange("p a b -> p (a b)"),
                                    k.tile_top[:, :]).then_inc(k.step.sem, 1)

    done(k, loaded=64, aux=T + 2, full=T * HEADS, valued=T * HEADS, step=T)
    for b in range(2):
        k.ring[b].base += 16 * (T // 2)
        k.ring[2 + b].base += 32 * (T // 2)


def edge_max_out_stage(k, top, m_dram):
    nc = k.nc
    w = k.big[1]
    m32 = w[0:HEADS, 0:N]
    parts = w[0:HEADS, N:N + 3 * N // 2].bitcast(BF16).rearrange("p (a n) -> p a n", a=3)
    with nc.Block() as block:

        @block.tensor
        def _(pe):
            for t in range(T):
                last = pe.transpose(k.bank[t // 4][0:HEADS, t % 4 * P:(t % 4 + 1) * P], top[:, t, :], k.identf[:, :])
            last.then_inc(k.full.sem, 1)

        @block.vector
        def _(dve):
            dve.wait_ge(k.full.sem, k.full.count(1))
            n = [0]

            def do(ins):
                ins.then_inc(k.step.sem, 1)
                n[0] += 1
                dve.wait_ge(k.step.sem, k.step.count(n[0]))

            do(dve.tensor_scalar(m32, k.psum[0:HEADS, 0:4, :].rearrange("p a n -> p (a n)"), -1.0, None, ALU.mult))
            for a in range(3):
                do(dve.tensor_copy(parts[:, a, :], m32))
                if a < 2:
                    do(dve.tensor_tensor(m32, m32, parts[:, a, :], ALU.subtract))

        @block.sync
        def _(sp):
            sp.wait_ge(k.step.sem, k.step.count(6))
            sp.dma_start(m_dram.rearrange("a h n -> h a n"), parts).then_inc(k.loaded.sem, 16)
            sp.wait_ge(k.loaded.sem, k.loaded.count(16))

    done(k, full=1, step=6, loaded=16)


VALUE_COLS = 2 * DH + 1
LEAD = 5


def edge_attention_stage(k, q_dram, k_dram, v_dram, m_dram, out):
    nc, ins = k.nc, k.ins
    w2 = k.big[2][:, :].bitcast(BF16)
    at = w2[:, 0:T * CH].rearrange("p (s n) -> p s n", s=T)
    keys = w2[:, T * CH:T * CH + 4 * N].rearrange("p (b a n) -> p b a n", b=2, a=2)
    w3 = k.big[3]
    vals = w3[:, 0:2080].bitcast(BF16).rearrange("p (b s d) -> p b s d", b=2, s=T)
    probs = w3[:, 2080:2080 + RING * CH].bitcast(BF16).rearrange("p (r a n) -> p r a n", r=RING, a=2)
    qs = w3[:, 4128:4128 + 1024].bitcast(BF16).rearrange("p (b a n) -> p b a n", b=2, a=2)
    summed = w3[:, 5152:5152 + 4 * DH].rearrange("p (t d) -> p t d", t=4)
    rsum = w3[:, 5408:5412].rearrange("p (t a) -> p t a", t=4)
    more = w3[:, 5632:5632 + RING * CH].rearrange("p (r n) -> p r n", r=RING)
    exact = [k.tmp[:, n, :] if n < RING else more[:, n - RING, :] for n in range(2 * RING)]
    acc = [k.psum[:, 4 + 2 * b:6 + 2 * b, :].rearrange("p k (q c) -> p (k q) c", c=CH // 2) for b in range(2)]
    pairs = NC * HEADS // 2
    on_vector = [u for u in range(T) if u % 4 < 2]

    def lows(u):
        return 2 * (u // 4) + u % 2 + 1

    with nc.Block() as block:

        @block.gpsimd
        def _(pool):
            pool.sem_inc(k.aux2.sem, 4)
            with pool.Fori(0, pairs) as g:
                for b in range(2):
                    for u in range(T):
                        if u not in on_vector:
                            pool.wait_ge(k.hi.sem, g * (2 * T) + k.hi.count(b * T + u + 1))
                            pool.tensor_tensor(probs[:, u % RING, 1, :], exact[u % 8],
                                               probs[:, u % RING, 0, :], ALU.subtract).then_inc(k.aux2.sem, 1)

        @block.sync
        def _(sp):

            def load_counts(i, g):
                sp.dma_start(at[:, 4 * g:4 * g + 4, :], ins["at_dram"][4 * g:4 * g + 4, :, bass.ts(i, CH)]
                             .rearrange("s p n -> p s n")).then_inc(k.atg[g].sem, 16)

            def load_head(i, hp, b):
                sp.wait_ge(k.astep.sem, i * (HEADS * T) + hp * (2 * T) + k.astep.count((b + 1) * T))
                s = k.ring[b].sem
                row = hp * P + b * DH
                kh, kl = (k_dram[a, bass.ds(row, DH), :] for a in range(2))
                sp.dma_start(keys[0:DH, b, 0, :], kh).then_inc(s, 16)
                sp.dma_start(keys[DH:P, b, 0, :], kl).then_inc(s, 16)
                sp.dma_start(keys[0:DH, b, 1, :], kh).then_inc(s, 16)
                qh, ql = (q_dram[a, bass.ds(row, DH), bass.ts(i, CH)] for a in range(2))
                sp.dma_start(qs[0:DH, b, 0, :], qh).then_inc(s, 16)
                sp.dma_start(qs[DH:P, b, 0, :], qh).then_inc(s, 16)
                sp.dma_start(qs[0:DH, b, 1, :], ql).then_inc(s, 16)
                sp.dma_start(qs[DH:DH + 3, b, 1, :], m_dram[:, bass.ds(hp * 2 + b, 1), bass.ts(i, CH)]
                             .rearrange("a h n -> (a h) n")).then_inc(s, 16)
                sp.dma_start(vals[:, b, :, 0:2 * DH], v_dram[bass.ds(hp * 2 + b, 1), :, :, :]
                             .rearrange("h p s d -> p (h s) d")).then_inc(s, 16)

            sp.wait_ge(k.loaded.sem, k.loaded.count(4))
            for b in range(2):
                load_head(0, 0, b)
            for g in range(4):
                load_counts(0, g)

            def other_heads(i):
                with sp.Fori(1, HEADS // 2) as hp:
                    for b in range(2):
                        load_head(i, hp, b)

            with sp.Fori(0, NC - 1) as i:
                other_heads(i)
                for b in range(2):
                    load_head(i + 1, 0, b)
                for g in range(4):
                    sp.wait_ge(k.aux.sem, i * (HEADS * T) + k.aux.count(HEADS * T - T + 4 * g + 4))
                    load_counts(i + 1, g)
            other_heads(NC - 1)

        @block.tensor
        def _(pe):
            pe.sem_inc(k.astep.sem, 2 * T)

            def scores(g, n, b, u):
                if u == 0:
                    pe.wait_ge(k.ring[b].sem, g * 128 + k.ring[b].count(16 + 128 * (1 + n // (2 * T))))
                pe.wait_ge(k.valued.sem, g * (2 * T) + k.valued.count(n + 1))
                pe.matmul(k.bank[u % RING], keys[:, b, 0, u * P:(u + 1) * P], qs[:, b, 0, :], start=True, stop=False)
                pe.matmul(k.bank[u % RING], keys[0:DH + 3, b, 1, u * P:(u + 1) * P], qs[0:DH + 3, b, 1, :],
                          start=False, stop=True).then_inc(k.full.sem, 1)

            def pair(g, last):
                for b in range(2):
                    for u in range(T):
                        n = b * T + u + LEAD
                        if n < 2 * T or not last:
                            scores(g, n, n // T % 2, n % T)
                        if u == 0:
                            pe.wait_ge(k.stat.sem, g * 2 + k.stat.count(b + 1))
                        low = k.lo if u in on_vector else k.aux2
                        pe.wait_ge(low.sem, g * T + low.count(4 + b * T // 2 + lows(u)))
                        for t in range(4):
                            hi, lo = (probs[:, u % RING, a, t * P:(t + 1) * P] for a in range(2))
                            pe.matmul(acc[b][:, t, 0:VALUE_COLS], hi, vals[:, b, u, 0:VALUE_COLS],
                                      start=u == 0 and t % 2 == 0, stop=False, skip_group_check=True)
                            last_one = pe.matmul(acc[b][:, t, DH:VALUE_COLS], lo, vals[:, b, u, DH:VALUE_COLS],
                                                 start=False, stop=u == T - 1, skip_group_check=True)
                        last_one.then_inc(k.astep.sem, 1)

            for u in range(LEAD):
                scores(0, u, 0, u)
            with pe.Fori(0, pairs - 1) as g:
                pair(g, False)
            pair(pairs - 1, True)

        @block.scalar
        def _(act):

            def exponential(g, n):
                u = n % T
                act.wait_ge(k.full.sem, g * (2 * T) + k.full.count(n + 1))
                low = k.lo if u in on_vector else k.aux2
                act.wait_ge(low.sem, g * T + low.count(n // T * T // 2 + lows(u)))
                act.activation(exact[u % 8], k.bank[u % RING], ACT.Exp).then_inc(k.valued.sem, 1)

            def pair(g, last):
                for n in range(2 * T):
                    if n + 2 < 2 * T or not last:
                        exponential(g, n + 2)
                    act.wait_ge(k.aux.sem, g * (2 * T) + k.aux.count(n + 1))
                    act.wait_ge(k.astep.sem, g * (2 * T) + k.astep.count(2 * T + n - 3))
                    act.activation(probs[:, n % RING, 0, :], exact[n % 8], ACT.Copy).then_inc(k.hi.sem, 1)

            for n in range(2):
                exponential(0, n)
            with act.Fori(0, pairs - 1) as g:
                pair(g, False)
            pair(pairs - 1, True)

        @block.vector
        def _(dve):
            dve.sem_inc(k.stat.sem, 2)
            for b in range(2):
                dve.memset(keys[64:96, b, 1, :], 1.0).then_inc(k.loaded.sem, 1)
                dve.memset(vals[:, b, :, 2 * DH:], 1.0).then_inc(k.loaded.sem, 1)

            def read_out(g, b, s):
                if s == 0:
                    dve.wait_ge(k.astep.sem, g * (2 * T) + k.astep.count(2 * T + (b + 1) * T))
                    dve.tensor_scalar(rsum, acc[b][:, :, 2 * DH:VALUE_COLS], 1e-16, None, ALU.add
                                      ).then_inc(k.step.sem, 1)
                    dve.tensor_copy(summed, acc[b][:, :, 0:DH]).then_inc(k.step.sem, 1)
                elif s == 1:
                    dve.wait_ge(k.step.sem, g * 8 + k.step.count(b * 4 + 2))
                    dve.reciprocal(rsum, rsum).then_inc(k.step.sem, 1)
                    dve.tensor_tensor(summed, acc[b][:, :, DH:2 * DH], summed, ALU.add).then_inc(k.step.sem, 1)
                else:
                    dve.wait_ge(k.step.sem, g * 8 + k.step.count(b * 4 + 4))
                    dve.tensor_tensor(out[:, bass.ds(g * 2 + b, 1), :, :].rearrange("p h t d -> p (h t) d"), summed,
                                      rsum.to_broadcast([P, 4, DH]), ALU.mult).then_inc(k.stat.sem, 1)

            def pair(i, hp, first=False):
                g = i * (HEADS // 2) + hp
                for b in range(2):
                    for u in range(T):
                        if b == 0 and u % 4 == 0:
                            dve.wait_ge(k.atg[u // 4].sem, i * 16 + k.atg[u // 4].count(16))
                        dve.wait_ge(k.valued.sem, g * (2 * T) + k.valued.count(RING + b * T + u + 1))
                        tile = exact[u % 8]
                        dve.scalar_tensor_tensor(tile, tile, 1e30, at[:, u, :], ALU.min, ALU.mult
                                                 ).then_inc(k.aux.sem, 1)
                        v = u - 1
                        if v in on_vector:
                            dve.wait_ge(k.hi.sem, g * (2 * T) + k.hi.count(b * T + v + 1))
                            dve.tensor_tensor(probs[:, v % RING, 1, :], exact[v % 8],
                                              probs[:, v % RING, 0, :], ALU.subtract).then_inc(k.lo.sem, 1)
                        if u in (6, 7, 8) and not (first and b == 0):
                            if b == 1:
                                read_out(g, 0, u - 6)
                            else:
                                read_out(g - 1, 1, u - 6)

            pair(0, 0, first=True)
            with dve.Fori(1, HEADS // 2) as hp:
                pair(0, hp)
            with dve.Fori(1, NC) as i:
                with dve.Fori(0, HEADS // 2) as hp:
                    pair(i, hp)
            for s in range(3):
                read_out(pairs - 1, 1, s)

    n = pairs * 2 * T
    done(k, full=n, valued=n, lo=n // 2, aux2=n // 2 + 4, aux=n, hi=n, astep=n + 2 * T, stat=2 * pairs + 2,
         step=8 * pairs, loaded=4)
    for b in range(2):
        k.ring[b].base += 128 * pairs
    for g in range(4):
        k.atg[g].base += 16 * NC


def batch_norm_stage(k, x, gain, bias, eps):
    nc = k.nc
    stats = k.moments[:, :, :]
    mv, sc = k.small[:, 4, 0:8].rearrange("p (b s) -> p b s", b=KC), k.small[:, 5, 0:KC]
    with nc.Block() as block:

        @block.vector
        def _(dve):
            n = [0]

            def do(ins, wait=True):
                ins.then_inc(k.step.sem, 1)
                n[0] += 1
                if wait:
                    dve.wait_ge(k.step.sem, k.step.count(n[0]))

            for b in range(KC):
                for c in range(NC):
                    do(dve.bn_stats(stats[:, b * NC + c, :], x[:, b, c * CH:(c + 1) * CH]), c == NC - 1)
                do(dve.bn_aggr(mv[:, b, :], stats[:, b * NC:(b + 1) * NC, :].rearrange("p a s -> p (a s)")))
            do(dve.tensor_scalar(sc, mv[:, :, 1], eps, None, ALU.add))
            dve.wait_ge(k.hi.sem, k.hi.count(1))
            do(dve.reciprocal(sc, sc))
            do(dve.tensor_tensor(sc, sc, gain, ALU.mult))
            for b in range(KC):
                do(dve.tensor_scalar(x[:, b, :], x[:, b, :], mv[:, b, 0:1], sc[:, b:b + 1], ALU.subtract, ALU.mult))
                do(dve.tensor_scalar(x[:, b, :], x[:, b, :], bias[:, b:b + 1], None, ALU.add))
            assert n[0] == KC * (NC + 1) + 3 + 2 * KC

        @block.scalar
        def _(act):
            act.wait_ge(k.step.sem, k.step.count(KC * (NC + 1) + 1))
            act.activation(sc, sc, ACT.Sqrt).then_inc(k.hi.sem, 1)

    done(k, step=KC * (NC + 1) + 3 + 2 * KC, hi=1)


def halves_stage(k, src, dst):
    nc = k.nc
    with nc.Block() as block:

        @block.scalar
        def _(act):
            for b in range(KC):
                act.activation(dst[:, b, :], src[:, b, :], ACT.Copy).then_inc(k.hi.sem, 1)

        @block.vector
        def _(dve):
            for b in range(KC):
                dve.wait_ge(k.hi.sem, k.hi.count(b + 1))
                dve.tensor_tensor(dst[:, KC + b, :], src[:, b, :], dst[:, b, :], ALU.subtract).then_inc(k.step.sem, 1)

    done(k, hi=KC, step=KC)


def layer1_graph(k):
    ins = k.ins
    x, a, res = k.F(0), k.F(2), k.F32v(1)
    heads_out = k.big[1][:, :].rearrange("p (h t d) -> p h t d", t=4, d=DH)

    def attended_tile(dve, i, j, y, chain):
        return dve.tensor_copy(y.rearrange("p (h d) -> p h d", h=HEADS),
                               heads_out[:, bass.ts(i, HEADS), j, :])

    q_dram, k_dram, v_dram, m_dram = (ins[n] for n in ("q_dram", "k_dram", "v_dram", "m_dram"))
    top = k.small_top
    for layer in range(2):
        col = lambda n, width=KC: k.cols[:, ins["col_index"][n] + width * layer:][:, 0:width]
        wq = use_weight(k)
        bq = col("L1_gnn_bq")
        product_stage(k, lambda i, j: features_out(x, wq, j, i), lambda dve, i, j, ps, y, chain:
                      dve.tensor_scalar(y, ps, bq[:, j:j + 1], DH ** -0.5, ALU.add, ALU.mult), f_halves(k.F(1)))
        wk = use_weight(k)
        kf = k.F(2)
        product_stage(k, lambda i, j: features_out(x, wk, j, i), as_is, f_halves(kf), value_on="scalar",
                      copies=[(q_dram.rearrange("h (b p) n -> p (h b) n", p=P), k.F(1))])
        wv = use_weight(k)
        v = k.TH(3)

        def store_values(i):
            return [(v_dram[:, :, bass.ds(i * RING + j, 1), (1 - a_) * DH:(2 - a_) * DH].rearrange("h p s d -> p h (s d)"),
                     v[:, bass.ds(i * RING + j, 1), a_, :].rearrange("p s (h d) -> p (s h) d", h=HEADS))
                    for j in range(RING) for a_ in range(2)]

        product_stage(k, lambda i, j: tokens_out(x, wv, tile_of(i, j)), as_is, t_halves(v), value_on="scalar",
                      copies=[(k_dram.rearrange("h (b p) n -> p (h b) n", p=P), kf)], trip_store=store_values)
        edge_max_stage(k, q_dram, k_dram, top)
        edge_max_out_stage(k, top, m_dram)
        edge_attention_stage(k, q_dram, k_dram, v_dram, m_dram, heads_out)
        transpose_stage(k, attended_tile, a)
        wo = use_weight(k)
        bo = col("L1_gnn_bo")

        def attended(dve, i, j, ps, y, chain):
            chain(dve.tensor_scalar(y, ps, bo[:, j:j + 1], None, ALU.add), 1)
            chain(dve.tensor_tensor(y, y, x[:, KC + j, bass.ts(i, CH)], ALU.add), 2)
            return dve.tensor_tensor(res[:, j, bass.ts(i, CH)], y, x[:, j, bass.ts(i, CH)], ALU.add)

        product_stage(k, lambda i, j: features_out(a, wo, j, i), attended, steps=3)
        batch_norm_stage(k, res, col("L1_gnn_g1"), col("L1_gnn_beta1"), EPS)
        halves_stage(k, res, x)
        w1 = use_weight(k)
        f1 = k.F(2)
        product_stage(k, lambda i, j: features_out(x, w1, 0, i), plus_col(col("L1_gnn_b1", 1), relu=True),
                      lambda i, j: (f1[:, 0, bass.ts(i, CH)], f1[:, KC, bass.ts(i, CH)]), width=1)
        w2 = use_weight(k)
        b2 = col("L1_gnn_b2")

        def fed(dve, i, j, ps, y, chain):
            chain(dve.tensor_scalar(y, ps, b2[:, j:j + 1], None, ALU.add), 1)
            r = res[:, j, bass.ts(i, CH)]
            return dve.tensor_tensor(r, y, r, ALU.add)

        def from_f1(i, j):
            hi, lo = f1[:, 0, bass.ts(i, CH)], f1[:, KC, bass.ts(i, CH)]
            whi, wlo = (w2[:, h, 0, j * P:(j + 1) * P] for h in range(2))
            return [(whi, hi), (whi, lo), (wlo, hi)]

        product_stage(k, from_f1, fed, steps=2)
        batch_norm_stage(k, res, col("L1_gnn_g2"), col("L1_gnn_beta2"), EPS)
        if layer == 0:
            halves_stage(k, res, x)
    t32 = k.T32(2)
    turn_to_tokens_stage(k, res, t32)
    moments_stage(k, t32, EPS, row_loads(k, "L1_gnn_ln_g", "L1_gnn_ln_b"))
    norm_add_stage(k, t32, k.rows[:, 0, :], k.rows[:, 1, :])


def turn_to_tokens_stage(k, src, dst):
    nc = k.nc
    with nc.Block() as block:

        @block.tensor
        def _(pe):
            for t in range(T):
                pe.wait_ge(k.valued.sem, k.valued.count(t + 1))
                for c in range(KC):
                    last = pe.transpose(k.bank[t % RING][:, c * P:(c + 1) * P], src[:, c, t * P:(t + 1) * P],
                                        k.identf[:, :])
                last.then_inc(k.full.sem, 1)

        @block.vector
        def _(dve):
            for t in range(T):
                dve.wait_ge(k.full.sem, k.full.count(t + 1))
                dve.tensor_copy(dst[:, t, :], k.bank[t % RING]).then_inc(k.valued.sem, 1)

    done(k, full=T, valued=T)



def weights_of(part):
    return {
        "L0_mix": ["L0_mix_Wq", "L0_mix_Wk", "L0_mix_Wv", "L0_mix_Wo", "L0_mix_W1", "L0_mix_W2"],
        "L0_gnn": ["L0_gnn_W_rel1", "L0_gnn_W_root1", "L0_gnn_W_lin1", "L0_gnn_W_rel2", "L0_gnn_W_root2",
                   "L0_gnn_W_lin2"],
        "L0_ffn": ["L0_ffn_Wr", "L0_ffn_W1", "L0_ffn_W2", "L0_ffn_W3"],
        "L1_mix": ["L1_mix_Wk", "L1_mix_Wv", "L1_mix_Wq", "L1_mix_W1", "L1_mix_W2"],
        "L2_gnn": ["L2_gnn_W1", "L2_gnn_W2"],
        "L2_mix": ["L2_mix_Wq", "L2_mix_Wk", "L2_mix_Wv", "L2_mix_out_w"],
        "L3_gnn": ["L3_gnn_W_l", "L3_gnn_W_r"],
        "L3_ffn": [f"L3_ffn_{n}{g}" for g in range(3) for n in ("gate", "up", "down")],
        "L3_mix": ["L3_mix_Wq", "L3_mix_Wk", "L3_mix_Wv", "L3_mix_proj", "L3_mix_Wo", "L3_mix_W1a", "L3_mix_W1b",
                   "L3_mix_W2a", "L3_mix_W2b"],
        "L1_gnn": [f"L1_gnn_{n}{l}" for l in range(2) for n in ("Wq", "Wk", "Wv", "Wo", "W1", "W2")],
        "L1_ffn": ["L1_ffn_W_router", "L1_ffn_W1", "L1_ffn_b2", "L1_ffn_W2"],
        "L2_ffn": ["L2_ffn_w1", "L2_ffn_w2"],
    }.get(part, [])


STAGES = {"graph": graph_stages,
          "L0_mix": layer0_mix, "L0_gnn": layer0_graph, "L0_ffn": layer0_experts,
          "L1_mix": layer1_mix, "L1_gnn": layer1_graph, "L1_ffn": layer1_experts,
          "L2_gnn": layer2_graph, "L2_mix": layer2_mix, "L2_ffn": layer2_experts,
          "L3_mix": layer3_mix, "L3_gnn": layer3_graph, "L3_ffn": layer3_ffn}

PARTS = ["graph",
         "norm", "L0_mix", "L0_gnn", "norm", "L0_ffn",
         "norm", "L1_mix", "L1_gnn", "norm", "L1_ffn",
         "norm", "L2_gnn", "L2_mix", "norm", "L2_ffn",
         "norm", "L3_mix", "L3_gnn", "norm", "L3_ffn"]

STATS_TAKEN = {"L0_gnn": 0, "L0_ffn": 0, "L1_ffn": 0, "L2_mix": 0, "L2_ffn": 1}


def entry_copies(k, part):
    if part == "L2_ffn":
        return [*zip(assignments(k), (k.ins["expert_idx"], k.ins["expert_w"]))]
    rows = {"L0_mix": ("L0_mix_bk", "L0_mix_bv", "L0_mix_bo"), "L0_ffn": ("L0_ffn_br",), "L1_ffn": ("L1_ffn_b1",),
            "L2_gnn": ("L2_gnn_b1",)}
    return row_loads(k, *rows.get(part, ()))


def build(nc, ins, out, parts):
    with ExitStack() as ctx:
        k = Core(ctx, nc, ins)
        k.queue = [weight(ins[n], ins[n].shape[0] // P, n.startswith("L3_ffn")) for p in parts for n in weights_of(p)]
        setup_stage(k)
        for n, part in enumerate(parts):
            if part == "norm":
                input_norm(k, STATS_TAKEN.get(parts[n - 1], T), entry_copies(k, parts[n + 1]))
            else:
                STAGES[part](k)
        with nc.Block() as block:

            @block.sync
            def _(sp):
                sp.dma_start(out.rearrange("(t p) d -> p t d", p=P), k.x[:, :, :]).then_inc(k.loaded.sem, 16)
                sp.wait_ge(k.loaded.sem, k.loaded.count(16))



ROWS = ["L0_mix_bk", "L0_mix_bv", "L0_mix_bo", "L0_mix_ln1_scale", "L0_mix_ln1_bias", "L0_mix_b2",
        "L0_mix_ln2_scale", "L0_mix_ln2_bias", "L0_gnn_b_lin2", "L0_ffn_br", "L1_ffn_b1", "L2_gnn_b1", "L2_mix_ln_gamma",
        "L2_mix_ln_beta", "L2_mix_bk", "L2_mix_bv", "L2_mix_out_b", "L3_gnn_gamma", "L3_gnn_beta", "L3_gnn_b_l", "L3_mix_bo", "L3_mix_ln0_g",
        "L3_mix_ln0_b", "L3_mix_b2", "L3_mix_ln1_g", "L3_mix_ln1_b", "L1_gnn_ln_g", "L1_gnn_ln_b"]
COLS = ["L0_mix_bq", "L0_mix_b1", "L0_gnn_b_rel1", "L0_gnn_b_lin1", "L0_gnn_b_rel2", "L2_mix_bq", "L3_mix_b1"] + [
    "L1_gnn_" + n for n in ("bq", "bo", "b1", "b2", "g1", "beta1", "g2", "beta2")]


def lay_out(inputs):
    a = {n: np.asarray(v) for n, v in inputs.items()}
    f32 = np.float32

    def wide(w):
        return np.concatenate([w, np.zeros((w.shape[0], P - w.shape[1]), f32)], 1)

    def tall(w):
        return np.concatenate([w, np.zeros((P - w.shape[0], w.shape[1]), f32)], 0)

    o = {"x": a["x"]}
    for n in ("Wq", "Wk", "Wv"):
        o["L0_mix_" + n] = a["L0_mix_" + n].reshape(D, D)
    o["L0_mix_Wo"] = a["L0_mix_Wo"].reshape(D, D)
    o["L0_mix_W1"] = wide(a["L0_mix_W1"])
    o["L0_mix_W2"] = tall(a["L0_mix_W2"])
    for n in ("rel1", "root1", "lin1", "rel2", "root2", "lin2"):
        o["L0_gnn_W_" + n] = a["L0_gnn_W_" + n].T

    def experts_in(w):
        return w.transpose(1, 0, 2).reshape(D, D)

    o["L0_ffn_Wr"] = a["L0_ffn_Wr"]
    o["L0_ffn_W1"], o["L0_ffn_W2"] = experts_in(a["L0_ffn_W1"]), experts_in(a["L0_ffn_W2"])
    o["L0_ffn_W3"] = a["L0_ffn_W3"].reshape(D, D)
    o["L1_ffn_W_router"] = a["L1_ffn_W_router"]
    o["L1_ffn_W1"], o["L1_ffn_W2"] = experts_in(a["L1_ffn_W1"]), a["L1_ffn_W2"].reshape(D, D)
    o["L1_ffn_b2"] = tall(a["L1_ffn_b2"])
    o["L2_ffn_w1"], o["L2_ffn_w2"] = experts_in(a["L2_ffn_w1"]), a["L2_ffn_w2"].reshape(D, D)
    o["expert_idx"], o["expert_w"] = a["L2_ffn_expert_indices"], a["L2_ffn_expert_weights"]

    for n in ("Wq", "Wk", "Wv", "W1", "W2"):
        o["L1_mix_" + n] = a["L1_mix_" + n].T
    o["L2_gnn_W1"] = wide(a["L2_gnn_W1"])
    o["L2_gnn_W2"] = tall(np.concatenate([a["L2_gnn_W2"], a["L2_gnn_b2"][None]], 0))
    a["L2_gnn_b1"] = np.concatenate([a["L2_gnn_b1"], np.ones(1, f32)])
    for n, part in enumerate("qkv"):
        o["L2_mix_W" + part] = a["L2_mix_qkv_w"][n * D:(n + 1) * D].T
        a["L2_mix_b" + part] = a["L2_mix_qkv_b"][n * D:(n + 1) * D]
    o["L2_mix_out_w"] = a["L2_mix_out_w"].T
    for n in ("W_l", "W_r"):
        o["L3_gnn_" + n] = a["L3_gnn_" + n].T
    for g in range(3):
        f = slice(g * D, min(g * D + D, 1408))
        o[f"L3_ffn_gate{g}"], o[f"L3_ffn_up{g}"] = a["L3_ffn_w_gate"][f].T, a["L3_ffn_w_up"][f].T
        o[f"L3_ffn_down{g}"] = a["L3_ffn_w_down"][:, f].T

    for n in ("Wq", "Wk", "Wv", "Wo"):
        o["L3_mix_" + n] = a["L3_mix_" + n]
    o["L3_mix_W1a"], o["L3_mix_W1b"] = a["L3_mix_W1"][:, :D], a["L3_mix_W1"][:, D:]
    o["L3_mix_W2a"], o["L3_mix_W2b"] = a["L3_mix_W2"][:D], a["L3_mix_W2"][D:]
    pj = np.zeros((2, 2, 64, 266), f32)
    pj[0, 0] = pj[1, 1] = a["L3_mix_proj"].T
    o["L3_mix_proj"] = pj.reshape(2 * P, 266)

    for l in range(2):
        for n in ("Wq", "Wk", "Wv", "Wo"):
            o[f"L1_gnn_{n}{l}"] = a["L1_gnn_" + n][l].T
        o[f"L1_gnn_W1{l}"] = wide(a["L1_gnn_W1"][l].T)
        o[f"L1_gnn_W2{l}"] = tall(a["L1_gnn_W2"][l].T)
    a["L1_gnn_b1"] = np.concatenate([a["L1_gnn_b1"], np.zeros((2, 64), f32)], 1)

    def row(v):
        v = v.reshape(-1)
        return np.concatenate([v, np.zeros(D - v.size, f32)])

    def col(v):
        v = v.reshape(-1)
        v = np.concatenate([v, np.zeros(-v.size % P, f32)])
        return v.reshape(-1, P).T

    o["src"], o["dst"] = (a[n].reshape(E // P, P).T for n in ("src", "dst"))
    tile = np.arange(3)[None] * P + np.arange(P)[:, None]
    pair = np.minimum(tile // 2, PAIRS - 1)
    block = np.broadcast_to(np.arange(T)[None] * P, (P, T))
    o["edge_consts"] = np.concatenate([pair, pair - NOWHERE, block, block + P], 1).astype(f32)
    o["iota"] = np.arange(N)[None].astype(np.float16)
    o["rows"] = np.stack([row(a[n]) for n in ROWS])
    cols = [col(a[n]) for n in COLS]
    o["cols"] = np.concatenate(cols, 1)
    at = np.cumsum([0] + [c.shape[1] for c in cols])
    return {n: np.ascontiguousarray(v) for n, v in o.items()}, {n: int(at[i]) for i, n in enumerate(COLS)}


def program(nc, arrays, col_index, parts):
    ins = {n: nc.dram_tensor(f"in_{n}", a.shape, mybir.dt.from_np(a.dtype), kind="ExternalInput").ap()
           for n, a in arrays.items()}
    ins["col_index"] = col_index
    ins["row_index"] = {n: i for i, n in enumerate(ROWS)}
    for n, shape, dt in (("xn_dram", [T, P, D], F32), ("at_dram", [T, P, N], BF16),
                         ("a_dram", [T, P, N], BF16), ("q_dram", [2, D, N], BF16), ("k_dram", [2, D, N], BF16),
                         ("v_dram", [HEADS, P, T, 2 * DH], BF16), ("m_dram", [3, 8, N], BF16)):
        if n not in ins:
            ins[n] = nc.dram_tensor(n, shape, dt, kind="Internal").ap()
    out = nc.dram_tensor("out_0_dram", (N, D), F32, kind="ExternalOutput").ap()
    build(nc, ins, out, parts)


def kernel(**inputs):
    import concourse.bacc as bacc
    from concourse.bass_utils import run_bass_kernel_spmd

    arrays, col_index = lay_out(inputs)
    nc = bacc.Bacc("TRN2", target_bir_lowering=False, num_devices=1)
    program(nc, arrays, col_index, PARTS)
    inputs = {f"in_{n}": a for n, a in arrays.items()}
    return run_bass_kernel_spmd(nc, [inputs], core_ids=[0]).results[0]["out_0_dram"]
```

```python
from contextlib import ExitStack

import numpy as np
import concourse.bass as bass
from concourse import mybir

ALU = mybir.AluOpType
ACT = mybir.ActivationFunctionType
F32 = mybir.dt.float32
BF16 = mybir.dt.bfloat16
F16 = mybir.dt.float16
I32 = mybir.dt.int32
AX = mybir.AxisListType

P = 128
N = 2048
D = 512
T = N // P
KC = D // P
CH = 512
NC = N // CH
RING = 4
LOOPS = 4
E = 34816
EPS = 1e-5



class Signal:

    def __init__(self, ctx, nc, name):
        self.sem = ctx.enter_context(nc.semaphore(name))
        self.base = 0

    def count(self, n):
        return self.base + n


class Core:

    def __init__(self, ctx, nc, ins):
        self.nc, self.ins = nc, ins

        def sb(name, shape, dt):
            return ctx.enter_context(nc.sbuf_tensor(name, shape, dt))

        self.x = sb("x_tokens", [P, T, D], F32)
        self.store = sb("store", [P, 4 * T * D], F32)
        self.big = [self.store[:, i * T * D:(i + 1) * T * D] for i in range(4)]
        self.weights = [sb(f"weights{i}", [P, 2, KC, D], BF16) for i in range(2)]
        self.staging = sb("staging", [P, KC, D], F32)
        self.tmp = sb("tmp", [P, RING, D], F32)
        self.rows = sb("rows", [P, 3, D], F32)
        self.cols = sb("cols", [P, ins["cols"].shape[1]], F32)
        self.zeros = sb("zeros", [P, 512], BF16)
        self.ones = sb("ones", [P, 2], BF16)
        self.headmask = sb("headmask", [P, P], F32)
        self.kv = sb("kv", [P, 2, 2, KC, P], BF16)
        self.small = sb("small", [P, 9, T], F32)
        self.xweight = sb("xweight", [P, T], F32)
        self.counts = sb("counts", [P, 2, EXPERTS], F32)
        self.hots = sb("hots", [P, 2, T, EXPERTS], BF16)
        self.ones128 = sb("ones128", [P, P], BF16)
        self.small_top = sb("edge_top", [P, T, 8], F32)
        self.table = self.hots[0:1, :, :, :].rearrange("p a t e -> p (a t e)").bitcast(I32)[:, 0:3 * T].rearrange(
            "p (a b) -> p a b", a=3)
        self.iota = self.rows[:, :, :].rearrange("p a d -> p (a d)").bitcast(F16)[:, 0:N]
        self.rdegree = sb("rdegree", [P, T], F32)
        self.onesf = sb("onesf", [P, P], F32)
        self.ident = sb("ident", [P, P], BF16)
        self.identf = sb("identf", [P, P], F32)
        self.moments = sb("moments", [P, T, 6], F32)
        self.tile_top = self.moments[:, :, :].rearrange("p t s -> p (t s)")[:, 0:HEADS]
        self.meanvar = sb("meanvar", [P, T, 2], F32)
        self.rstd = sb("rstd", [P, T], F32)
        self.psum = ctx.enter_context(nc.psum_tensor("banks", [P, 8, 512], F32))
        self.bank = [self.psum[:, i, :] for i in range(8)]

        def sig(name):
            return Signal(ctx, nc, name)

        self.full = sig("bank_full")
        self.valued = sig("value_ready")
        self.hi = sig("hi_ready")
        self.lo = sig("lo_ready")
        self.step = sig("vector_step")
        self.astep = sig("scalar_step")
        self.staged = sig("weight_staged")
        self.whi = sig("weight_hi")
        self.wlo = sig("weight_lo")
        self.loaded = sig("params_loaded")
        self.ring = [sig(f"ring_dma{j}") for j in range(RING)]
        self.atg = [sig(f"group_dma{g}") for g in range(4)]
        self.stat = sig("row_statistics")
        self.magnitude = sig("weight_magnitudes")
        self.group_sum = sig("weight_group_sums")
        self.quantum = sig("quantize_steps")
        self.upper = sig("upper_half_by_vector")
        self.squared = sig("squares_ready")
        self.peak = sig("unit_maxima")
        self.biased = sig("exponent_bias")
        self.turned = sig("unit_turned")
        self.weighed = sig("products_with_context")
        self.inverse = sig("inverse_sums")
        self.out = sig("unit_out")
        self.peak_rest = sig("unit_maxima_rest")
        self.biased_rest = sig("exponent_bias_rest")
        self.half_full = sig("unit_half_full")
        self.half_used = sig("unit_half_used")
        self.aux = sig("aux")
        self.aux2 = sig("aux2")
        self.hot_ready = sig("one_hots_ready")
        self.hot_used = sig("one_hots_used")
        self.queue = []
        self.slot = 0
        self.staged_spec = None
        self.slot_ready = False

    def big_pair(self, i):
        return self.store[:, i * T * D:(i + 2) * T * D].bitcast(BF16).rearrange("p (t n) -> p t n", t=T)

    def F(self, i):
        return self.big[i][:, :].bitcast(BF16).rearrange("p (b n) -> p b n", b=2 * KC)

    def TH(self, i):
        return self.big[i][:, :].bitcast(BF16).rearrange("p (t h d) -> p t h d", t=T, h=2)

    def T32(self, i):
        return self.big[i][:, :].rearrange("p (t d) -> p t d", t=T)

    def F32v(self, i):
        return self.big[i][:, :].rearrange("p (b n) -> p b n", b=KC)

    def col(self, name, width=1):
        c = self.ins["col_index"][name]
        return self.cols[:, c:c + width]


def done(k, **counts):
    signals = {"full": k.full, "valued": k.valued, "hi": k.hi, "lo": k.lo, "step": k.step, "astep": k.astep,
               "staged": k.staged, "whi": k.whi, "wlo": k.wlo, "loaded": k.loaded, "stat": k.stat,
               "aux": k.aux, "aux2": k.aux2, "magnitude": k.magnitude, "upper": k.upper, "group_sum": k.group_sum,
               "quantum": k.quantum, "squared": k.squared, "peak": k.peak, "biased": k.biased,
               "turned": k.turned, "weighed": k.weighed, "inverse": k.inverse, "out": k.out,
               "peak_rest": k.peak_rest, "biased_rest": k.biased_rest, "half_full": k.half_full, "half_used": k.half_used}
    for name, n in counts.items():
        signals[name].base += n



QUANTIZE_STEPS = 6
MAGIC = 1.5 * 2.0 ** 23


class WeightTurn:

    def __init__(self, k):
        self.k = k
        self.split = None if k.slot_ready else k.staged_spec
        self.slot = 1 - k.slot
        self.next = None
        if self.split is not None:
            k.slot_ready, k.staged_spec = True, None
        if k.staged_spec is None and k.queue:
            self.next = k.staged_spec = k.queue.pop(0)
        self.by_trips = self.split is not None and self.split[4] == "by trips"
        self.parts = 0 if self.split is None else KC if self.by_trips else 1

    def scalar(self, act):
        k = self.k
        if self.split is not None:
            _, p, c, n, _ = self.split
            act.wait_ge(k.staged.sem, k.staged.count(0))
            if not self.by_trips:
                k.nc.scalar.activation(k.weights[self.slot][0:p, 0, 0:c, 0:n], k.staging[0:p, 0:c, 0:n],
                                       ACT.Copy).then_inc(k.whi.sem, 1)

    def vector(self, dve):
        k = self.k
        if self.split is not None and not self.by_trips:
            _, p, c, n, _ = self.split
            dve.wait_ge(k.whi.sem, k.whi.count(1))
            k.nc.vector.tensor_tensor(k.weights[self.slot][0:p, 1, 0:c, 0:n], k.staging[0:p, 0:c, 0:n],
                                      k.weights[self.slot][0:p, 0, 0:c, 0:n],
                                      ALU.subtract).then_inc(k.wlo.sem, 1)

    def block(self, buf, i):
        return buf[:, bass.ds(i, 1), 0:self.split[3]].rearrange("p a n -> p (a n)")

    def magnitudes(self, act, i):
        k = self.k
        act.wait_ge(k.wlo.sem, i + k.wlo.count(0))
        act.activation(k.rows[:, 0, 0:self.split[3]], self.block(k.staging, i), ACT.Abs).then_inc(k.magnitude.sem, 1)

    def sums(self, pe, i):
        k = self.k
        n = self.split[3]
        pe.wait_ge(k.magnitude.sem, i + k.magnitude.count(1))
        pe.matmul(k.bank[RING][:, 0:n], k.onesf[:, :], k.rows[:, 0, 0:n], start=True,
                  stop=True).then_inc(k.group_sum.sem, 1)

    def quantize(self, dve, i):
        k = self.k
        n = self.split[3]
        y, scale = k.rows[:, 0, 0:n], k.rows[:, 1, 0:n]
        dve.wait_ge(k.group_sum.sem, i + k.group_sum.count(1))
        for step in range(QUANTIZE_STEPS):
            if step:
                dve.wait_ge(k.quantum.sem, i * QUANTIZE_STEPS + k.quantum.count(step))
            (dve.tensor_scalar(scale, k.bank[RING][:, 0:n], 1.0 / P, EPS, ALU.mult, ALU.add) if step == 0 else
             dve.reciprocal(y, scale) if step == 1 else
             dve.tensor_tensor(y, self.block(k.staging, i), y, ALU.mult) if step == 2 else
             dve.tensor_scalar(y, y, MAGIC, MAGIC, ALU.add, ALU.subtract) if step == 3 else
             dve.tensor_scalar(y, y, -1.0, 1.0, ALU.max, ALU.min) if step == 4 else
             dve.tensor_tensor(y, y, scale, ALU.mult)).then_inc(k.quantum.sem, 1)

    def upper(self, act, i):
        k = self.k
        act.wait_ge(k.quantum.sem, i * QUANTIZE_STEPS + k.quantum.count(QUANTIZE_STEPS))
        act.activation(self.block(k.weights[self.slot][:, 0, :, :], i), k.rows[:, 0, 0:self.split[3]],
                       ACT.Copy).then_inc(k.whi.sem, 1)

    def lower(self, dve, i):
        k = self.k
        dve.wait_ge(k.whi.sem, i + k.whi.count(1))
        dve.tensor_tensor(self.block(k.weights[self.slot][:, 1, :, :], i), k.rows[:, 0, 0:self.split[3]],
                          self.block(k.weights[self.slot][:, 0, :, :], i), ALU.subtract).then_inc(k.wlo.sem, 1)

    def sync(self, sp):
        k = self.k
        if self.next is not None:
            if self.split is not None:
                sp.wait_ge(k.wlo.sem, k.wlo.count(self.parts))
            ap, p, c, n, _ = self.next
            sp.dma_start(k.staging[0:p, 0:c, 0:n], ap).then_inc(k.staged.sem, 16)

    def finish(self):
        k = self.k
        done(k, whi=self.parts, wlo=self.parts, staged=16 * int(self.next is not None))
        if self.by_trips:
            done(k, magnitude=KC, group_sum=KC, quantum=KC * QUANTIZE_STEPS)
        if self.next is not None and self.next[4] == "before":
            quantize_stage(k)


def use_weight(k):
    assert k.slot_ready
    k.slot_ready = False
    k.slot = 1 - k.slot
    return k.weights[k.slot]



def accumulate(pe, out, pairs, start=True, stop=True):
    last = None
    for n, (stationary, moving) in enumerate(pairs):
        last = pe.matmul(out, stationary, moving, start=start and n == 0, stop=stop and n == len(pairs) - 1,
                         skip_group_check=True)
    return last


def start_copies(k, sp, copies):
    for dst, src in copies:
        sp.dma_start(dst, src).then_inc(k.loaded.sem, 16)


def end_copies(k, sp, copies):
    if copies:
        sp.wait_ge(k.loaded.sem, k.loaded.count(16 * len(copies)))


def tokens_out(act_f, w, i_tile, blocks=KC, n=D):
    out = []
    for c in range(blocks):
        hi = act_f[:, c, bass.ts(i_tile, P)]
        lo = act_f[:, KC + c, bass.ts(i_tile, P)]
        out += [(hi, w[:, 0, c, 0:n]), (hi, w[:, 1, c, 0:n]), (lo, w[:, 0, c, 0:n])]
    return out


def features_out(act_f, w, f, i_chunk, m=P, chunk=CH):
    out = []
    for c in range(KC):
        hi = act_f[:, c, bass.ts(i_chunk, chunk)]
        lo = act_f[:, KC + c, bass.ts(i_chunk, chunk)]
        whi, wlo = w[:, 0, c, f * P:f * P + m], w[:, 1, c, f * P:f * P + m]
        out += [(whi, hi), (whi, lo), (wlo, hi)]
    return out


def product_stage(k, pairs, value, halves=None, in_place=False, value_on="vector", steps=1, rows_out=P, width=RING,
                  trips=LOOPS, turn=True, cols_out=D, pairs2=None, pre=None, copies=(), needs_copies=False,
                  stats=None, trip_store=None, split=None, after=None):
    assert not (after and (halves or pre or value_on == "scalar"))
    assert not (split and (halves or value_on == "vector" or stats))
    nc = k.nc
    turn = WeightTurn(k) if turn else None
    quantizes = turn is not None and turn.by_trips
    stores = trips * len(trip_store(0)) if trip_store else 0
    with nc.Block() as block:

        @block.sync
        def _(sp):
            if turn:
                turn.sync(sp)
            start_copies(k, sp, copies)
            if trip_store:
                with sp.Fori(0, trips) as i:
                    sp.wait_ge(k.lo.sem, i * width + k.lo.count(RING + width))
                    for dst, src in trip_store(i):
                        sp.dma_start(dst, src).then_inc(k.aux2.sem, 16)
                sp.wait_ge(k.aux2.sem, k.aux2.count(16 * stores))
            end_copies(k, sp, copies)

        @block.tensor
        def _(pe):
            with pe.Fori(0, trips) as i:
                for j in range(width):
                    pe.wait_ge(k.valued.sem, i * width + k.valued.count(j + 1 + RING - width))
                    if pairs2:
                        accumulate(pe, k.bank[RING + j][0:rows_out, 0:cols_out], pairs2(i, j))
                    accumulate(pe, k.bank[j][0:rows_out, 0:cols_out], pairs(i, j)).then_inc(k.full.sem, 1)
                    if quantizes and j == 1:
                        turn.sums(pe, i)

        def value_program(eng):
            if needs_copies:
                eng.wait_ge(k.loaded.sem, k.loaded.count(16 * len(copies)))
            vector = value_on == "vector"
            with eng.Fori(0, trips) as i:
                if quantizes and not vector:
                    turn.magnitudes(eng, i)
                for j in range(width):
                    if quantizes and j == 2:
                        (turn.quantize if vector else turn.upper)(eng, i)
                    if quantizes and vector and j == 3:
                        turn.lower(eng, i)
                    n = i * width + j
                    eng.wait_ge(k.full.sem, i * width + k.full.count(j + 1))
                    if pre:
                        eng.wait_ge(k.aux.sem, i * width + k.aux.count(j + 1))
                    if halves:
                        eng.wait_ge(k.lo.sem, i * width + k.lo.count(j + 1 + RING - width))
                    sig = k.step if eng is nc.vector or value_on == "vector" else k.astep

                    def chain(ins, s, n=n, sig=sig):
                        ins.then_inc(sig.sem, 1)
                        eng.wait_ge(sig.sem, i * (width * (steps - 1)) + sig.count(j * (steps - 1) + s))

                    value(eng, i, j, k.bank[j][0:rows_out, 0:cols_out], k.tmp[0:rows_out, j, 0:cols_out],
                          chain).then_inc(k.valued.sem, 1)
                    if stats is not None:
                        eng.wait_ge(k.valued.sem, i * width + k.valued.count(RING + j + 1))
                        slot, row = stats(i, j)
                        eng.bn_stats(k.moments[:, bass.ds(slot, 1), :].rearrange("p a s -> p (a s)"),
                                     row).then_inc(k.stat.sem, 1)
                if quantizes and vector and width < 4:
                    turn.lower(eng, i)

        def hi_program(eng, copy):
            with eng.Fori(0, trips) as i:
                if quantizes:
                    turn.magnitudes(eng, i)
                for j in range(width):
                    if quantizes and j == 2:
                        turn.upper(eng, i)
                    eng.wait_ge(k.valued.sem, i * width + k.valued.count(RING + j + 1))
                    if in_place and j == 0:
                        eng.wait_ge(k.full.sem, i * width + k.full.count(width))
                    copy(halves(i, j)[0], k.tmp[0:rows_out, j, 0:cols_out]).then_inc(k.hi.sem, 1)

        @block.vector
        def _(dve):
            if turn:
                turn.vector(dve)
            if value_on == "vector":
                value_program(dve)
            elif halves:
                hi_program(dve, lambda o, a: dve.tensor_copy(o, a))
            elif pre:
                with dve.Fori(0, trips) as i:
                    for j in range(width):
                        dve.wait_ge(k.full.sem, i * width + k.full.count(j + 1))
                        pre(dve, i, j, k.bank[j][0:rows_out, 0:cols_out]).then_inc(k.aux.sem, 1)
                        if split and j == 2:
                            dve.wait_ge(k.loaded.sem, k.loaded.count(16 * len(copies)))
                            dve.tensor_copy(split[0][:, bass.ts(i, RING), 0, :],
                                            split[1][:, bass.ts(i, RING), :]).then_inc(k.hi.sem, 1)
            elif quantizes:
                with dve.Fori(0, trips) as i:
                    turn.quantize(dve, i)
                    turn.lower(dve, i)

        @block.scalar
        def _(act):
            if turn:
                turn.scalar(act)
            if value_on == "scalar":
                value_program(act)
            elif pre and value_on == "vector":
                with act.Fori(0, trips) as i:
                    for j in range(width):
                        act.wait_ge(k.full.sem, i * width + k.full.count(j + 1))
                        act.wait_ge(k.lo.sem, i * width + k.lo.count(j + 1 + RING - width))
                        pre(act, i, j, k.bank[j][0:rows_out, 0:cols_out]).then_inc(k.aux.sem, 1)
                    for j in range(width if halves else 0):
                        act.wait_ge(k.valued.sem, i * width + k.valued.count(RING + j + 1))
                        act.activation(halves(i, j)[0], k.tmp[0:rows_out, j, 0:cols_out],
                                       ACT.Copy).then_inc(k.hi.sem, 1)
            elif halves:
                hi_program(act, lambda o, a: act.activation(o, a, ACT.Copy))
            elif after:
                with act.Fori(0, trips) as i:
                    for j in range(width):
                        act.wait_ge(k.valued.sem, i * width + k.valued.count(RING + j + 1))
                        after(act, i, j).then_inc(k.hi.sem, 1)
            elif quantizes:
                with act.Fori(0, trips) as i:
                    turn.magnitudes(act, i)
                    turn.upper(act, i)

        @block.gpsimd
        def _(pool):
            if split:
                with pool.Fori(0, trips) as i:
                    tiles = bass.ts(i, RING)
                    pool.wait_ge(k.hi.sem, i + k.hi.count(1))
                    pool.tensor_tensor(split[0][:, tiles, 1, :], split[1][:, tiles, :], split[0][:, tiles, 0, :],
                                       ALU.subtract).then_inc(k.lo.sem, 1)
            if halves:
                with pool.Fori(0, trips) as i:
                    for j in range(width):
                        pool.wait_ge(k.hi.sem, i * width + k.hi.count(j + 1))
                        hi, lo = halves(i, j)
                        pool.tensor_tensor(lo, k.tmp[0:rows_out, j, 0:cols_out], hi,
                                           ALU.subtract).then_inc(k.lo.sem, 1)

    n = trips * width
    done(k, full=n, valued=n)
    if steps > 1:
        done(k, **{"step" if value_on == "vector" else "astep": n * (steps - 1)})
    if halves:
        done(k, hi=n, lo=n)
    if split:
        done(k, hi=T // RING, lo=T // RING)
    if after:
        done(k, hi=n)
    if pre:
        done(k, aux=n)
    done(k, loaded=16 * len(copies), stat=n if stats is not None else 0, aux2=16 * stores)
    if turn:
        turn.finish()


def moments_stage(k, src, eps, copies=(), tiles=T):
    nc = k.nc
    with nc.Block() as block:

        @block.sync
        def _(sp):
            start_copies(k, sp, copies)
            end_copies(k, sp, copies)

        @block.vector
        def _(dve):
            for t in range(tiles):
                dve.bn_stats(k.moments[:, t, :], src[:, t, :]).then_inc(k.step.sem, 1)
            for t in range(T):
                if t < tiles:
                    dve.wait_ge(k.step.sem, k.step.count(t + 1))
                dve.bn_aggr(k.meanvar[:, t, :], k.moments[:, t, :]).then_inc(k.aux.sem, 1)
            dve.wait_ge(k.aux.sem, k.aux.count(T))
            dve.tensor_scalar(k.rstd[:, :], k.meanvar[:, :, 1], eps, None, ALU.add).then_inc(k.step.sem, 1)
            dve.wait_ge(k.hi.sem, k.hi.count(1))
            dve.reciprocal(k.rstd[:, :], k.rstd[:, :]).then_inc(k.step.sem, 1)

        @block.scalar
        def _(act):
            act.wait_ge(k.step.sem, k.step.count(tiles + 1))
            act.activation(k.rstd[:, :], k.rstd[:, :], ACT.Sqrt).then_inc(k.hi.sem, 1)

    done(k, step=tiles + 2, aux=T, hi=1, loaded=16 * len(copies))


def transpose_stage(k, make, dst, steps=1, turn=False, store=None, trips=LOOPS, width=RING,
                    copies=()):
    nc = k.nc
    turn = WeightTurn(k) if turn else None
    with nc.Block() as block:

        @block.vector
        def _(dve):
            if turn:
                turn.vector(dve)
            lag = min(2, width)

            def tile(i, j):
                if store is not None:
                    dve.wait_ge(k.ring[j].sem, i * 16 + k.ring[j].count(16))

                def chain(ins, s):
                    ins.then_inc(k.step.sem, 1)
                    dve.wait_ge(k.step.sem, i * (width * (steps - 1)) + k.step.count(j * (steps - 1) + s))

                make(dve, i, j, k.tmp[:, j, :], chain).then_inc(k.aux.sem, 1)

            def lower(i, j):
                dve.wait_ge(k.hi.sem, i * width + k.hi.count(j + 1))
                dve.tensor_tensor(dst[:, KC:2 * KC, bass.ts(i * width + j, P)],
                                  k.bank[j][:, :].rearrange("p (c n) -> p c n", c=KC),
                                  dst[:, 0:KC, bass.ts(i * width + j, P)], ALU.subtract).then_inc(k.valued.sem, 1)

            def trip(i, first):
                for j in range(width):
                    tile(i, j)
                    if j >= lag:
                        lower(i, j - lag)
                    elif not first:
                        lower(i - 1, width + j - lag)

            trip(0, True)
            if trips > 1:
                with dve.Fori(1, trips) as i:
                    trip(i, False)
            for j in range(width - lag, width):
                lower(trips - 1, j)

        @block.tensor
        def _(pe):
            with pe.Fori(0, trips) as i:
                for j in range(width):
                    pe.wait_ge(k.aux.sem, i * width + k.aux.count(j + 1))
                    pe.wait_ge(k.valued.sem, i * width + k.valued.count(j + 1 + RING - width))
                    for c in range(KC):
                        last = pe.transpose(k.bank[j][:, c * P:(c + 1) * P], k.tmp[:, j, c * P:(c + 1) * P],
                                            k.identf[:, :])
                    last.then_inc(k.full.sem, 1)

        @block.scalar
        def _(act):
            if turn:
                turn.scalar(act)
            with act.Fori(0, trips) as i:
                for j in range(width):
                    act.wait_ge(k.full.sem, i * width + k.full.count(j + 1))
                    act.activation(dst[:, 0:KC, bass.ts(i * width + j, P)],
                                   k.bank[j][:, :].rearrange("p (c n) -> p c n", c=KC),
                                   ACT.Copy).then_inc(k.hi.sem, 1)

        @block.sync
        def _(sp):
            if turn:
                turn.sync(sp)
            start_copies(k, sp, copies)
            if store is not None:
                with sp.Fori(0, trips) as i:
                    for j in range(width):
                        sp.wait_ge(k.aux.sem, i * width + k.aux.count(j + 1))
                        sp.dma_start(store(i * width + j), k.tmp[:, j, :]).then_inc(k.ring[j].sem, 16)
                for j in range(width):
                    sp.wait_ge(k.ring[j].sem, k.ring[j].count(16 * (trips + 1)))
            end_copies(k, sp, copies)

    n = trips * width
    done(k, aux=n, hi=n, full=n, valued=n, step=n * (steps - 1), loaded=16 * len(copies))
    if store is not None:
        for j in range(width):
            k.ring[j].base += 16 * trips
    if turn:
        turn.finish()


def tile_of(i, j):
    return i * RING + j


def rows_of(buf):
    return lambda i, j: (tile_of(i, j), buf[:, tile_of(i, j), :])



def setup_stage(k):
    nc, ins = k.nc, k.ins
    turn = WeightTurn(k)
    with nc.Block() as block:

        @block.gpsimd
        def _(pool):
            pool.memset(k.zeros[:, :], 0.0).then_inc(k.aux.sem, 1)
            pool.memset(k.ones[:, :], 1.0).then_inc(k.aux.sem, 1)
            pool.memset(k.identf[:, :], 0.0).then_inc(k.aux.sem, 1)
            pool.wait_ge(k.aux.sem, 3)
            pool.affine_select(out=k.identf[:, :], in_=k.identf[:, :], compare_op=ALU.not_equal, fill=1.0,
                               base=0, pattern=[[-1, P]], channel_multiplier=1).then_inc(k.aux.sem, 1)
            pool.wait_ge(k.aux.sem, 4)
            pool.tensor_copy(k.ident[:, :], k.identf[:, :]).then_inc(k.aux.sem, 1)
            pool.memset(k.headmask[:, :], 0.0).then_inc(k.aux.sem, 1)
            pool.wait_ge(k.aux.sem, 6)
            pool.memset(k.ones128[:, :], 1.0).then_inc(k.aux.sem, 1)
            pool.memset(k.onesf[:, :], 1.0).then_inc(k.aux.sem, 1)

        @block.sync
        def _(sp):
            turn.sync(sp)
            sp.dma_start(k.cols[:, :], ins["cols"]).then_inc(k.ring[0].sem, 16)
            sp.wait_ge(k.ring[0].sem, 16)

        @block.vector
        def _(dve):
            dve.sem_inc(k.valued.sem, RING)
            dve.sem_inc(k.lo.sem, RING)
            dve.wait_ge(k.ring[0].sem, 16)
            for j in range(1, RING):
                dve.sem_inc(k.ring[j].sem, 16)
            dve.wait_ge(k.aux.sem, 7)
            for h in range(2):
                dve.memset(k.headmask[64 * h:64 * h + 64, 64 * h:64 * h + 64], 1.0).then_inc(k.aux.sem, 1)

    done(k, aux=10)
    turn.finish()


def row_loads(k, *names, **last):
    slots = [*enumerate(names), *((2, n) for n in last.values())]
    return [(k.rows[:, s, :], k.ins["rows"][r:r + 1, :].rearrange("a d -> (a d)").partition_broadcast(P))
            for s, r in ((s, k.ins["row_index"][n]) for s, n in slots)]


def tile_in(buf):
    return lambda t: buf[:, bass.ds(t, 1), :].rearrange("p a d -> p (a d)")


def norm_add_stage(k, src, gain, bias):
    nc = k.nc
    order = [(0, 0), (0, 1), (1, 0), (0, 2), (1, 1), (0, 3), (1, 2), (1, 3)]
    with nc.Block() as block:

        @block.vector
        def _(dve):
            with dve.Fori(0, LOOPS) as i:
                for s, j in order:
                    t = tile_of(i, j)
                    y = k.tmp[:, j, :]
                    if s == 0:
                        dve.wait_ge(k.lo.sem, i * RING + k.lo.count(j + 1))
                        ins = dve.scalar_tensor_tensor(y, src[:, t, :], k.meanvar[:, t, 0:1], gain, ALU.subtract,
                                                       ALU.mult)
                    else:
                        dve.wait_ge(k.step.sem, i * (2 * RING) + k.step.count(1 + order.index((0, j))))
                        ins = dve.scalar_tensor_tensor(y, y, k.rstd[:, bass.ds(t, 1)], bias, ALU.mult, ALU.add)
                    ins.then_inc(k.step.sem, 1)

        @block.gpsimd
        def _(pool):
            with pool.Fori(0, LOOPS) as i:
                for j in range(RING):
                    x = k.x[:, tile_of(i, j), :]
                    pool.wait_ge(k.step.sem, i * (2 * RING) + k.step.count(1 + order.index((1, j))))
                    pool.tensor_tensor(x, x, k.tmp[:, j, :], ALU.add).then_inc(k.lo.sem, 1)

    done(k, step=2 * T, lo=T)


def normalise(k, src, gain=None, bias=None):

    def make(dve, i, j, y, chain):
        t = tile_of(i, j)
        if gain is None:
            return dve.tensor_scalar(y, src[:, t, :], k.meanvar[:, t, 0:1], k.rstd[:, bass.ds(t, 1)],
                                     ALU.subtract, ALU.mult)
        chain(dve.scalar_tensor_tensor(y, src[:, t, :], k.meanvar[:, t, 0:1], gain, ALU.subtract, ALU.mult), 1)
        return dve.scalar_tensor_tensor(y, y, k.rstd[:, bass.ds(t, 1)], bias, ALU.mult, ALU.add)

    return make


def key_value_stage(k, kp, v, kv):
    nc = k.nc
    with nc.Block() as block:

        @block.tensor
        def _(pe):
            for b in range(2):
                pe.matmul(k.bank[b][:, :], k.zeros[:, 0:P], k.zeros[:, :], start=True, stop=False,
                          skip_group_check=True)
            with pe.Fori(0, LOOPS) as i:
                for j in range(RING):
                    t = tile_of(i, j)
                    for p in range(KC):
                        f = slice(p * P, p * P + P)
                        hi, lo = kp[:, t, 0, f], kp[:, t, 1, f]
                        for s, m in ((hi, v[:, t, 0, f]), (hi, v[:, t, 1, f]), (lo, v[:, t, 0, f])):
                            pe.matmul(k.bank[0][:, f], s, m, start=False, stop=False, skip_group_check=True)
                        for s in (hi, lo):
                            pe.matmul(k.bank[1][:, p:p + 1], s, k.ones[:, 0:1], start=False, stop=False,
                                      skip_group_check=True)
            pe.matmul(k.bank[1][:, :], k.zeros[:, 0:P], k.zeros[:, :], start=False, stop=True,
                      skip_group_check=True).then_inc(k.full.sem, 1)

        @block.vector
        def _(dve):
            dve.wait_ge(k.full.sem, k.full.count(1))
            n = 0
            for p in range(KC):
                f = slice(p * P, p * P + P)
                dve.tensor_tensor(k.tmp[:, 0, f], k.bank[0][:, f], k.headmask[:, :], ALU.mult).then_inc(k.step.sem, 1)
                dve.tensor_scalar(k.tmp[:, 1, f], k.headmask[:, :], k.bank[1][:, p:p + 1], None,
                                  ALU.mult).then_inc(k.step.sem, 1)
            dve.wait_ge(k.step.sem, k.step.count(2 * KC))
            for b in range(2):
                hi = kv[:, b, 0, :, :].rearrange("p a d -> p (a d)")
                dve.tensor_copy(hi, k.tmp[:, b, :]).then_inc(k.step.sem, 1)
            dve.wait_ge(k.step.sem, k.step.count(2 * KC + 2))
            for b in range(2):
                hi = kv[:, b, 0, :, :].rearrange("p a d -> p (a d)")
                lo = kv[:, b, 1, :, :].rearrange("p a d -> p (a d)")
                dve.tensor_tensor(lo, k.tmp[:, b, :], hi, ALU.subtract).then_inc(k.step.sem, 1)

    done(k, full=1, step=2 * KC + 4)


def aggregate_stage(k, u, at_ring, at_dram, root, w, value, halves, in_place):
    nc = k.nc
    turn = WeightTurn(k)
    with nc.Block() as block:

        @block.sync
        def _(sp):
            turn.sync(sp)
            with sp.Fori(0, NC) as i:
                for g in range(RING):
                    sp.wait_ge(k.aux2.sem, i * RING + k.aux2.count(g + 1))
                    sp.dma_start(at_ring[:, g, :, :],
                                 at_dram[4 * g:4 * g + 4, :, bass.ts(i, CH)].rearrange("s p n -> p s n")
                                 ).then_inc(k.ring[g].sem, 16)

        @block.tensor
        def _(pe):
            pe.sem_inc(k.aux2.sem, RING)
            with pe.Fori(0, NC) as i:
                for g in range(RING):
                    pe.wait_ge(k.ring[g].sem, i * 16 + k.ring[g].count(32))
                    for f in range(KC):
                        if g == 0:
                            pe.wait_ge(k.valued.sem, i * KC + k.valued.count(f + 1))
                        pairs = [(u[:, 4 * g + s, h, f * P:f * P + P], at_ring[:, g, s, :])
                                 for s in range(4) for h in range(2)]
                        last = accumulate(pe, k.bank[f][:, :], pairs, start=g == 0, stop=False)
                    last.then_inc(k.aux2.sem, 1)
                for f in range(KC):
                    accumulate(pe, k.bank[f][:, :], features_out(root, w, f, i), start=False).then_inc(k.full.sem, 1)

        @block.vector
        def _(dve):
            turn.vector(dve)
            with dve.Fori(0, NC) as i:
                for f in range(KC):
                    dve.wait_ge(k.full.sem, i * KC + k.full.count(f + 1))
                    dve.wait_ge(k.lo.sem, i * KC + k.lo.count(f + 1))
                    value(dve, i, f, k.bank[f][:, :], k.tmp[:, f, :]).then_inc(k.valued.sem, 1)

        @block.scalar
        def _(act):
            turn.scalar(act)
            with act.Fori(0, NC) as i:
                for f in range(KC):
                    act.wait_ge(k.valued.sem, i * KC + k.valued.count(RING + f + 1))
                    if in_place and f == 0:
                        act.wait_ge(k.full.sem, i * KC + k.full.count(KC))
                    act.activation(halves(i, f)[0], k.tmp[:, f, :], ACT.Copy).then_inc(k.hi.sem, 1)

        @block.gpsimd
        def _(pool):
            with pool.Fori(0, NC) as i:
                for f in range(KC):
                    pool.wait_ge(k.hi.sem, i * KC + k.hi.count(f + 1))
                    pool.tensor_tensor(halves(i, f)[1], k.tmp[:, f, :], halves(i, f)[0],
                                       ALU.subtract).then_inc(k.lo.sem, 1)

    n = NC * KC
    done(k, full=n, valued=n, hi=n, lo=n, aux2=n + RING)
    for g in range(RING):
        k.ring[g].base += 16 * NC
    turn.finish()



def all_tiles(dram):
    return dram.rearrange("t p d -> p t d")


def f_halves(buf):
    return lambda i, j: (buf[:, j, bass.ts(i, CH)], buf[:, KC + j, bass.ts(i, CH)])


def t_halves(buf):
    return lambda i, j: (buf[:, tile_of(i, j), 0, :], buf[:, tile_of(i, j), 1, :])


def plus_col(col, relu=False):
    def value(dve, i, j, ps, y, chain=None):
        return dve.tensor_scalar(y, ps, col[:, j:j + 1], 0.0 if relu else None, ALU.add,
                                 *([ALU.max] if relu else []))
    return value


def plus_row(row):
    return lambda dve, i, j, ps, y, chain: dve.tensor_tensor(y, ps, row, ALU.add)


def as_is(eng, i, j, ps, y, chain):
    return eng.activation(y, ps, ACT.Copy)


def weight(ap, c=KC, quantized=None):
    return ap.rearrange("(c p) n -> p c n", p=P), P, c, ap.shape[1], quantized



def layer0_mix(k):
    xn, q, f1 = k.F(0), k.F(1), k.F(2)
    kp, v, t32 = k.TH(2), k.TH(3), k.T32(3)
    kv = k.big[2][:, 0:1024].bitcast(BF16).rearrange("p (b h a d) -> p b h a d", b=2, h=2, a=KC)
    keps = 0.001
    bq = k.col("L0_mix_bq", KC)

    def relu_col(dve, i, j, ps, y, chain):
        chain(dve.tensor_scalar(y, ps, bq[:, j:j + 1], 0.0, ALU.add, ALU.max), 1)
        return dve.tensor_scalar(y, y, keps, None, ALU.add)

    def relu_row(dve, i, j, ps, y, chain):
        chain(dve.tensor_tensor(y, ps, k.rows[:, 0, :], ALU.add), 1)
        return dve.tensor_scalar(y, y, 0.0, keps, ALU.max, ALU.add)

    wq = use_weight(k)
    product_stage(k, lambda i, j: features_out(xn, wq, j, i), relu_col, f_halves(q), steps=2)
    wk = use_weight(k)
    product_stage(k, lambda i, j: tokens_out(xn, wk, tile_of(i, j)), relu_row, t_halves(kp), steps=2)
    wv = use_weight(k)
    product_stage(k, lambda i, j: tokens_out(xn, wv, tile_of(i, j)), plus_row(k.rows[:, 1, :]), t_halves(v))
    key_value_stage(k, kp, v, k.kv)
    linear_attention(k, q, k.kv, 0.0, [(t32, all_tiles(k.ins["xn_dram"])),
                                       *row_loads(k, "L0_mix_ln1_scale", "L0_mix_ln1_bias")])
    wo = use_weight(k)

    def residual(row):
        def value(dve, i, j, ps, y, chain):
            chain(dve.tensor_tensor(y, ps, row, ALU.add), 1)
            return dve.tensor_tensor(t32[:, tile_of(i, j), :], y, t32[:, tile_of(i, j), :], ALU.add)
        return value

    product_stage(k, lambda i, j: tokens_out(q, wo, tile_of(i, j)), residual(k.rows[:, 2, :]), steps=2,
                  stats=rows_of(t32))
    moments_stage(k, t32, 1e-6, tiles=0)
    transpose_stage(k, normalise(k, t32, k.rows[:, 0, :], k.rows[:, 1, :]), q, steps=2, store=tile_in(t32),
                    copies=row_loads(k, b2="L0_mix_b2"))
    w1 = use_weight(k)
    product_stage(k, lambda i, j: features_out(q, w1, 0, i), plus_col(k.col("L0_mix_b1"), relu=True),
                  lambda i, j: (f1[:, 0, bass.ts(i, CH)], f1[:, KC, bass.ts(i, CH)]), width=1,
                  copies=row_loads(k, "L0_mix_ln2_scale", "L0_mix_ln2_bias"))
    w2 = use_weight(k)
    product_stage(k, lambda i, j: tokens_out(f1, w2, tile_of(i, j), blocks=1), residual(k.rows[:, 2, :]), steps=2,
                  stats=rows_of(t32))
    moments_stage(k, t32, 1e-6, tiles=0)
    norm_add_stage(k, t32, k.rows[:, 0, :], k.rows[:, 1, :])


def linear_attention(k, q, kv, eps, copies):
    nc = k.nc
    spare = k.big[2]
    pick = spare[:, 0:KC * P].rearrange("p (b s m) -> p b s m", b=KC, s=2)
    inverse = spare[:, KC * P:KC * P + CH]
    sums = spare[:, KC * P + CH:2 * KC * P + CH].bitcast(BF16).rearrange("p (h b m) -> p h b m", h=2, b=KC)

    def products(w, i, j):
        hi, lo = q[:, j, bass.ts(i, CH)], q[:, KC + j, bass.ts(i, CH)]
        a, b = (w[:, h, j, :] for h in range(2))
        return [(a, hi), (a, lo), (b, hi)]

    with nc.Block() as block:

        @block.sync
        def _(sp):
            start_copies(k, sp, copies)
            end_copies(k, sp, copies)

        @block.tensor
        def _(pe):
            pe.wait_ge(k.aux2.sem, k.aux2.count(KC + 1 + KC))
            with pe.Fori(0, NC) as i:
                pe.wait_ge(k.valued.sem, i * KC + k.valued.count(1))
                accumulate(pe, k.bank[RING], [x for j in range(KC) for x in products(sums, i, j)]
                           ).then_inc(k.weighed.sem, 1)
                for j in range(KC):
                    pe.wait_ge(k.valued.sem, i * KC + k.valued.count(j + 1))
                    accumulate(pe, k.bank[j], products(kv[:, 0, :, :, :], i, j)).then_inc(k.full.sem, 1)
                pe.wait_ge(k.inverse.sem, i + k.inverse.count(1))
                for j in range(KC):
                    pe.matmul(k.bank[RING + j], pick[:, j, :, :].rearrange("p s m -> p (s m)"), inverse,
                              start=True, stop=True).then_inc(k.turned.sem, 1)

        @block.vector
        def _(dve):
            for j in range(KC):
                dve.tensor_copy(pick[:, j, :, :], k.identf[:, 32 * j:32 * j + 32:16].unsqueeze(2).to_broadcast(
                    [P, 2, DH])).then_inc(k.aux2.sem, 1)
            dve.memset(sums, 0.0).then_inc(k.aux2.sem, 1)
            dve.wait_ge(k.aux2.sem, k.aux2.count(KC + 1))
            for j in range(KC):
                dve.tensor_copy(sums[:, :, j, 32 * j:32 * j + 32], kv[:, 1, :, j, 0:P:4]).then_inc(k.aux2.sem, 1)
            with dve.Fori(0, NC) as i:
                dve.wait_ge(k.weighed.sem, i + k.weighed.count(1))
                dve.tensor_scalar(inverse, k.bank[RING], eps, None, ALU.add).then_inc(k.step.sem, 1)
                dve.wait_ge(k.step.sem, i + k.step.count(1))
                dve.reciprocal(inverse, inverse).then_inc(k.inverse.sem, 1)
                for j in range(KC):
                    dve.wait_ge(k.turned.sem, i * KC + k.turned.count(j + 1))
                    dve.wait_ge(k.aux.sem, i * KC + k.aux.count(j + 1))
                    dve.tensor_tensor(k.tmp[:, j, :], k.bank[RING + j], k.tmp[:, j, :], ALU.mult
                                      ).then_inc(k.valued.sem, 1)

        @block.scalar
        def _(act):
            with act.Fori(0, NC) as i:
                for j in range(KC):
                    act.wait_ge(k.full.sem, i * KC + k.full.count(j + 1))
                    act.wait_ge(k.lo.sem, i * KC + k.lo.count(j + 1))
                    act.activation(k.tmp[:, j, :], k.bank[j], ACT.Copy).then_inc(k.aux.sem, 1)
                for j in range(KC):
                    act.wait_ge(k.valued.sem, i * KC + k.valued.count(RING + j + 1))
                    act.activation(q[:, j, bass.ts(i, CH)], k.tmp[:, j, :], ACT.Copy).then_inc(k.hi.sem, 1)

        @block.gpsimd
        def _(pool):
            with pool.Fori(0, NC) as i:
                for j in range(KC):
                    pool.wait_ge(k.hi.sem, i * KC + k.hi.count(j + 1))
                    pool.tensor_tensor(q[:, KC + j, bass.ts(i, CH)], k.tmp[:, j, :], q[:, j, bass.ts(i, CH)],
                                       ALU.subtract).then_inc(k.lo.sem, 1)

    n = NC * KC
    done(k, weighed=NC, full=n, inverse=NC, turned=n, aux=n, aux2=2 * KC + 1, step=NC, valued=n, hi=n, lo=n,
         loaded=16 * len(copies))


def layer0_graph(k):
    xn, a, b = k.F(0), k.F(1), k.F(2)
    at_ring = k.big[3][:, 0:RING * 1024].bitcast(BF16).rearrange("p (g s n) -> p g s n", g=RING, s=4)
    at_dram = k.ins["at_dram"]
    root, u = xn, k.TH(1)
    for layer in (1, 2):
        ub, cb = ((1, 2), (2, 1))[layer - 1]
        u = k.TH(ub)
        w = use_weight(k)
        product_stage(k, lambda i, j, w=w, root=root: tokens_out(root, w, tile_of(i, j)), as_is, t_halves(u),
                      value_on="scalar", copies=row_loads(k, "L0_gnn_b_lin2") if layer == 1 else ())
        w = use_weight(k)
        c = k.F(cb)
        aggregate_stage(k, u, at_ring, at_dram, root, w, plus_col(k.col(f"L0_gnn_b_rel{layer}", KC)), f_halves(c),
                        in_place=layer == 2)
        w = use_weight(k)
        if layer == 1:
            h = k.F(1)
            product_stage(k, lambda i, j, w=w, c=c: features_out(c, w, j, i),
                          plus_col(k.col("L0_gnn_b_lin1", KC), relu=True), f_halves(h))
            root = h
        else:

            def value(dve, i, j, ps, y, chain):
                chain(dve.tensor_tensor(y, ps, k.rows[:, 0, :], ALU.add), 1)
                return dve.scalar_tensor_tensor(k.x[:, tile_of(i, j), :], y, 0.0, k.x[:, tile_of(i, j), :],
                                                ALU.max, ALU.add)

            product_stage(k, lambda i, j, w=w, c=c: tokens_out(c, w, tile_of(i, j)), value, steps=2,
                          stats=rows_of(k.x))


def input_norm(k, tiles, copies):
    moments_stage(k, k.x, EPS, tiles=tiles)
    xn = k.ins["xn_dram"]
    transpose_stage(k, normalise(k, k.x), k.F(0), turn=True, copies=copies,
                    store=lambda t: xn[bass.ds(t, 1), :, :].rearrange("a p d -> p (a d)"))



EXPERTS = 8


def routes(k):
    r = k.kv[:, :, :, :, :].rearrange("p a b c d -> p (a b c d)").bitcast(F32)
    return [r[:, n * P:(n + 1) * P].rearrange("p (t e) -> p t e", e=EXPERTS) for n in range(8)]


def router_stage(k, logits, bias=None):
    w = use_weight(k)
    xn = k.F(0)

    def value(dve, i, j, ps, y, chain):
        if bias is None:
            return dve.tensor_copy(logits[:, tile_of(i, j), :], ps)
        return dve.tensor_tensor(logits[:, tile_of(i, j), :], ps, bias, ALU.add)

    product_stage(k, lambda i, j: tokens_out(xn, w, tile_of(i, j), n=EXPERTS), value, cols_out=EXPERTS)


def top2_stage(k, capacity):
    nc = k.nc
    logits, key, hot0, hot1, work, iota, down, coef = routes(k)
    one = k.small
    m0, m1, s0, s1, keep0, keep1, idx0, idx1, last = (one[:, n, :] for n in range(9))
    counts = k.counts
    steps = [0]

    def wide(a):
        return a.unsqueeze(2).to_broadcast([P, T, EXPERTS])

    def over_tokens(a):
        return a.unsqueeze(1).to_broadcast([P, T, EXPERTS])

    with nc.Block() as block:

        @block.gpsimd
        def _(pool):
            pool.iota(iota, pattern=[[0, T], [1, EXPERTS]], base=0, channel_multiplier=0,
                      allow_small_or_imprecise_dtypes=True).then_inc(k.aux.sem, 1)
            pool.iota(down, pattern=[[0, T], [-1, EXPERTS]], base=EXPERTS, channel_multiplier=0,
                      allow_small_or_imprecise_dtypes=True).then_inc(k.aux.sem, 1)
            pool.memset(last, 0.0).then_inc(k.aux.sem, 1)
            pool.wait_ge(k.aux.sem, k.aux.count(3))
            pool.affine_select(out=last, in_=last, compare_op=ALU.not_equal, fill=1.0, base=-(N - 1),
                               pattern=[[P, T]], channel_multiplier=1).then_inc(k.aux.sem, 1)

        @block.vector
        def _(dve):

            def do(ins):
                ins.then_inc(k.step.sem, 1)
                steps[0] += 1
                dve.wait_ge(k.step.sem, k.step.count(steps[0]))

            def best(scores, m, hot):
                do(dve.tensor_reduce(m, scores, AX.X, ALU.max))
                do(dve.tensor_tensor(key, scores, wide(m), ALU.is_equal))
                do(dve.tensor_tensor(key, key, down, ALU.mult))
                do(dve.tensor_reduce(s0, key, AX.X, ALU.max))
                do(dve.tensor_tensor(hot, key, wide(s0), ALU.is_equal))

            dve.wait_ge(k.aux.sem, k.aux.count(4))
            best(logits, m0, hot0)
            do(dve.scalar_tensor_tensor(work, hot0, -1e30, logits, ALU.mult, ALU.add))
            best(work, m1, hot1)
            do(dve.tensor_tensor(s1, m1, m0, ALU.subtract))
            dve.wait_ge(k.hi.sem, k.hi.count(1))
            do(dve.tensor_scalar(s0, s1, 1.0, None, ALU.add))
            do(dve.reciprocal(s0, s0))
            do(dve.tensor_tensor(s1, s1, s0, ALU.mult))
            if not capacity:
                do(dve.tensor_tensor(hot0, hot0, wide(s0), ALU.mult))
                do(dve.tensor_tensor(hot1, hot1, wide(s1), ALU.mult))
                do(dve.tensor_tensor(coef, hot0, hot1, ALU.add))
                return
            do(dve.tensor_copy(k.hots[:, 0, :, :], hot0))
            do(dve.tensor_tensor(k.hots[:, 1, :, :], hot0, hot1, ALU.add))
            dve.wait_ge(k.full.sem, k.full.count(1))
            for n, (hot, keep, idx) in enumerate(((hot0, keep0, idx0), (hot1, keep1, idx1))):
                do(dve.tensor_reduce(counts[:, n, :], k.bank[0][:, n * P:(n + 1) * P]
                                     .rearrange("p (t e) -> p e t", e=EXPERTS), AX.X, ALU.add))
                do(dve.tensor_scalar(counts[:, n, :], counts[:, n, :], float(N), None, ALU.is_ge))
                do(dve.tensor_tensor(work, hot, over_tokens(counts[:, n, :]), ALU.mult))
                do(dve.tensor_reduce(keep, work, AX.X, ALU.add))
                do(dve.tensor_tensor(keep, keep, last, ALU.mult))
                do(dve.tensor_scalar(keep, keep, -1.0, 1.0, ALU.mult, ALU.add))
                do(dve.tensor_tensor(work, hot, iota, ALU.mult))
                do(dve.tensor_reduce(idx, work, AX.X, ALU.add))
                do(dve.tensor_tensor(idx, idx, keep, ALU.mult))
            do(dve.tensor_tensor(idx0, idx0, idx1, ALU.max))
            do(dve.tensor_tensor(m0, s0, s1, ALU.add))
            do(dve.tensor_tensor(s0, s0, keep0, ALU.mult))
            do(dve.tensor_tensor(s1, s1, keep1, ALU.mult))
            do(dve.tensor_tensor(s0, s0, s1, ALU.add))
            do(dve.tensor_tensor(k.xweight[:, :], m0, s0, ALU.subtract))
            do(dve.tensor_tensor(hot0, iota, wide(idx0), ALU.is_equal))
            do(dve.tensor_tensor(coef, hot0, wide(s0), ALU.mult))

        before_exp = 12

        @block.scalar
        def _(act):
            act.wait_ge(k.step.sem, k.step.count(before_exp))
            act.activation(s1, s1, ACT.Exp).then_inc(k.hi.sem, 1)

        if capacity:

            @block.tensor
            def _(pe):
                pe.wait_ge(k.step.sem, k.step.count(before_exp + 5))
                pe.matmul(k.bank[0][:, 0:2 * P], k.ones128[:, :], k.hots[:, :, :, :].rearrange("p a t e -> p (a t e)"),
                          start=True, stop=True).then_inc(k.full.sem, 1)

    done(k, aux=4, step=steps[0], hi=1, full=int(capacity))


def weigh_experts(a32, coef):
    def make(dve, i, j, y, chain):
        t = tile_of(i, j)
        return dve.tensor_tensor(y.rearrange("p (e h) -> p e h", e=EXPERTS),
                                 a32[:, t, :].rearrange("p (e h) -> p e h", e=EXPERTS),
                                 coef[:, t, :].unsqueeze(2).to_broadcast([P, EXPERTS, D // EXPERTS]), ALU.mult)
    return make


def layer0_experts(k):
    xn, a32, hidden, t32 = k.F(0), k.T32(1), k.F(2), k.T32(3)
    logits, coef = routes(k)[0], routes(k)[7]
    router_stage(k, logits, k.rows[:, 0, 0:EXPERTS])
    top2_stage(k, capacity=True)
    w1 = use_weight(k)
    product_stage(k, lambda i, j: tokens_out(xn, w1, tile_of(i, j)),
                  lambda act, i, j, ps, y, chain: act.activation(a32[:, tile_of(i, j), :], ps, ACT.Copy),
                  value_on="scalar", copies=[(t32, all_tiles(k.ins["xn_dram"]))])
    w2 = use_weight(k)
    product_stage(k, lambda i, j: tokens_out(xn, w2, tile_of(i, j)),
                  lambda dve, i, j, ps, y, chain: dve.tensor_tensor(a32[:, tile_of(i, j), :], ps,
                                                                    a32[:, tile_of(i, j), :], ALU.mult),
                  after=lambda act, i, j: act.activation(a32[:, tile_of(i, j), :], a32[:, tile_of(i, j), :],
                                                         ACT.Gelu))
    transpose_stage(k, weigh_experts(a32, coef), hidden)

    def value(dve, i, j, ps, y, chain):
        t = tile_of(i, j)
        chain(dve.tensor_tensor(k.x[:, t, :], ps, k.x[:, t, :], ALU.add), 1)
        return dve.scalar_tensor_tensor(k.x[:, t, :], t32[:, t, :], k.xweight[:, bass.ds(t, 1)], k.x[:, t, :],
                                        ALU.mult, ALU.add)

    w3 = use_weight(k)
    product_stage(k, lambda i, j: tokens_out(hidden, w3, tile_of(i, j)), value, steps=2, stats=rows_of(k.x))


def layer1_experts(k):
    xn, a32, hidden, comb = k.F(0), k.T32(1), k.F(2), k.F(3)
    logits, coef = routes(k)[0], routes(k)[7]
    router_stage(k, logits)
    top2_stage(k, capacity=False)
    combine_stage(k, coef, comb)
    w1 = use_weight(k)

    def relu_row(dve, i, j, ps, y, chain):
        chain(dve.tensor_tensor(y, ps, k.rows[:, 0, :], ALU.add), 1)
        return dve.tensor_scalar(a32[:, tile_of(i, j), :], y, 0.0, None, ALU.max)

    product_stage(k, lambda i, j: tokens_out(xn, w1, tile_of(i, j)), relu_row, steps=2)
    transpose_stage(k, weigh_experts(a32, coef), hidden)
    add = lambda dve, i, j, ps, y, chain: dve.tensor_tensor(k.x[:, tile_of(i, j), :], ps, k.x[:, tile_of(i, j), :],
                                                            ALU.add)
    b2 = use_weight(k)
    product_stage(k, lambda i, j: tokens_out(comb, b2, tile_of(i, j), blocks=1), add)
    w2 = use_weight(k)
    product_stage(k, lambda i, j: tokens_out(hidden, w2, tile_of(i, j)), add, stats=rows_of(k.x))


def combine_stage(k, coef, comb):
    nc = k.nc
    with nc.Block() as block:

        @block.gpsimd
        def _(pool):
            for h in range(2):
                pool.memset(comb[:, h * KC, :], 0.0).then_inc(k.aux.sem, 1)

        @block.tensor
        def _(pe):
            for t in range(T):
                last = pe.transpose(k.bank[t // 4][0:EXPERTS, t % 4 * P:(t % 4 + 1) * P], coef[:, t, :],
                                    k.identf[:, :])
                if t % 4 == 3:
                    last.then_inc(k.full.sem, 1)

        @block.vector
        def _(dve):
            dve.wait_ge(k.aux.sem, k.aux.count(2))
            for b in range(4):
                dve.wait_ge(k.full.sem, k.full.count(b + 1))
                hi = comb[0:EXPERTS, 0, b * CH:(b + 1) * CH]
                lo = comb[0:EXPERTS, KC, b * CH:(b + 1) * CH]
                ps = k.bank[b][0:EXPERTS, :]
                dve.tensor_copy(hi, ps).then_inc(k.step.sem, 1)
                dve.wait_ge(k.step.sem, k.step.count(2 * b + 1))
                dve.tensor_tensor(lo, ps, hi, ALU.subtract).then_inc(k.step.sem, 1)

    done(k, aux=2, full=4, step=8)


def assignments(k):
    return k.small[:, 0, 0:2].bitcast(I32), k.small[:, 1, 0:2]


def layer2_experts(k):
    nc, ins = k.nc, k.ins
    xn, a32, hidden = k.F(0), k.T32(1), k.F(2)
    _, key, _, _, idxf, iota, _, coef = routes(k)
    idx, ew = assignments(k)
    with nc.Block() as block:

        @block.gpsimd
        def _(pool):
            pool.iota(iota[:, 0, :], pattern=[[1, EXPERTS]], base=0, channel_multiplier=0,
                      allow_small_or_imprecise_dtypes=True).then_inc(k.aux.sem, 1)

        @block.vector
        def _(dve):
            n = [0]

            def do(ins):
                ins.then_inc(k.step.sem, 1)
                n[0] += 1
                dve.wait_ge(k.step.sem, k.step.count(n[0]))

            dve.wait_ge(k.aux.sem, k.aux.count(1))
            do(dve.tensor_copy(idxf[:, 0, 0:2], idx))
            for c in range(2):
                do(dve.tensor_scalar(key[:, c, :], iota[:, 0, :], idxf[:, 0, c:c + 1], ew[:, c:c + 1],
                                     ALU.is_equal, ALU.mult))
            do(dve.tensor_tensor(coef[:, 0, :], key[:, 0, :], key[:, 1, :], ALU.add))

    done(k, aux=1, step=4)
    w1 = use_weight(k)
    product_stage(k, lambda i, j: tokens_out(xn, w1, 0), lambda act, i, j, ps, y, chain:
                  act.activation(a32[:, 0, :], ps, ACT.Gelu), value_on="scalar", trips=1, width=1)
    tile0 = weigh_experts(a32, coef)
    transpose_stage(k, lambda dve, i, j, y, chain: tile0(dve, 0, 0, y, chain), hidden, trips=1, width=1)
    w2 = use_weight(k)
    product_stage(k, lambda i, j: tokens_out(hidden, w2, 0), lambda dve, i, j, ps, y, chain:
                  dve.tensor_tensor(k.x[:, 0, :], ps, k.x[:, 0, :], ALU.add), trips=1, width=1)



def whole_stage(k, vector=None, scalar=None, pool=None, sync=None):
    with k.nc.Block() as block:
        for eng, prog in ((block.vector, vector), (block.scalar, scalar), (block.gpsimd, pool), (block.sync, sync)):
            if prog is not None:
                eng(prog)


def turn_back_stage(k, make, dst):
    nc = k.nc
    with nc.Block() as block:

        @block.scalar
        def _(act):
            with act.Fori(0, LOOPS) as i:
                for j in range(RING):
                    act.wait_ge(k.valued.sem, i * RING + k.valued.count(j + 1))
                    make(act, i, j, k.tmp[:, j, :]).then_inc(k.aux.sem, 1)

        @block.tensor
        def _(pe):
            with pe.Fori(0, LOOPS) as i:
                for j in range(RING):
                    pe.wait_ge(k.aux.sem, i * RING + k.aux.count(j + 1))
                    for c in range(KC):
                        last = pe.transpose(k.bank[j][:, c * P:(c + 1) * P], k.tmp[:, j, c * P:(c + 1) * P],
                                            k.identf[:, :])
                    last.then_inc(k.full.sem, 1)

        @block.vector
        def _(dve):
            with dve.Fori(0, LOOPS) as i:
                for j in range(RING):
                    hi, lo = dst(i, j)
                    dve.wait_ge(k.full.sem, i * RING + k.full.count(j + 1))
                    dve.tensor_copy(hi, k.bank[j][:, :]).then_inc(k.hi.sem, 1)
                    dve.wait_ge(k.hi.sem, i * RING + k.hi.count(j + 1))
                    dve.tensor_tensor(lo, k.bank[j][:, :], hi, ALU.subtract).then_inc(k.valued.sem, 1)

    done(k, aux=T, hi=T, full=T, valued=T)


def key_sums_stage(k, kt, xn_t, sums, inverse):
    nc = k.nc
    with nc.Block() as block:

        @block.tensor
        def _(pe):
            for b in range(KC + 1):
                pe.matmul(k.bank[b][:, :], k.zeros[:, 0:P], k.zeros[:, :], start=True, stop=False,
                          skip_group_check=True)
            with pe.Fori(0, LOOPS) as i:
                for j in range(RING):
                    t = tile_of(i, j)
                    for f in range(KC):
                        block_f = slice(f * P, (f + 1) * P)
                        accumulate(pe, k.bank[f][:, :],
                                   [(xn_t[:, t, 0, block_f], kt[:, t, 0, :]), (xn_t[:, t, 0, block_f], kt[:, t, 1, :]),
                                    (xn_t[:, t, 1, block_f], kt[:, t, 0, :])], start=False, stop=False)
                        accumulate(pe, k.bank[KC][:, f:f + 1],
                                   [(kt[:, t, 0, block_f], k.ones[:, 0:1]), (kt[:, t, 1, block_f], k.ones[:, 0:1])],
                                   start=False, stop=False)
            for b in range(KC + 1):
                last = pe.matmul(k.bank[b][:, :], k.zeros[:, 0:P], k.zeros[:, :], start=False, stop=True,
                                 skip_group_check=True)
            last.then_inc(k.full.sem, 1)

        @block.vector
        def _(dve):
            dve.wait_ge(k.full.sem, k.full.count(1))
            dve.reciprocal(inverse, k.bank[KC][:, 0:KC]).then_inc(k.step.sem, 1)
            for f in range(KC):
                dve.tensor_copy(sums[:, 0, f, :], k.bank[f][:, :]).then_inc(k.step.sem, 1)
            for f in range(KC):
                dve.wait_ge(k.step.sem, k.step.count(2 + f))
                dve.tensor_tensor(sums[:, 1, f, :], k.bank[f][:, :], sums[:, 0, f, :],
                                  ALU.subtract).then_inc(k.step.sem, 1)

    done(k, full=1, step=2 * KC + 1)


def layer1_mix(k):
    xn = k.F(0)
    kf32, kt, xn_t = k.F32v(1), k.TH(2), k.TH(3)
    sums, ctx = [k.big[2][:, n * 2048:(n + 1) * 2048].bitcast(BF16).rearrange("p (h c n) -> p h c n", h=2, c=KC)
                 for n in range(2)]
    wk = use_weight(k)
    xn32 = k.T32(2)
    chunk_top = k.small[:, 2, 0:KC * NC].rearrange("p (c n) -> p c n", c=KC)
    product_stage(k, lambda i, j: features_out(xn, wk, j, i),
                  lambda act, i, j, ps, y, chain: act.activation(kf32[:, j, bass.ts(i, CH)], ps, ACT.Copy),
                  value_on="scalar", copies=[(xn32, all_tiles(k.ins["xn_dram"]))], split=(xn_t, xn32),
                  pre=lambda dve, i, j, ps: dve.tensor_reduce(chunk_top[:, j, bass.ds(i, 1)], ps, AX.X, ALU.max))
    top = k.small[:, 1, 0:KC]

    def key_max(dve):
        dve.tensor_reduce(top, chunk_top, AX.X, ALU.max, negate=True).then_inc(k.step.sem, 1)

    whole_stage(k, vector=key_max)
    done(k, step=1)

    def exp_keys(act, i, j, y):
        for c in range(KC):
            last = act.activation(y[:, c * P:(c + 1) * P], kf32[:, c, bass.ts(tile_of(i, j), P)], ACT.Exp,
                                  bias=top[:, c:c + 1])
        return last

    turn_back_stage(k, exp_keys, t_halves(kt))
    inverse = k.small[:, 0, 0:KC]
    key_sums_stage(k, kt, xn_t, sums, inverse)
    wv = use_weight(k)
    product_stage(k, lambda i, j: [x for c in range(KC) for x in (
        (sums[:, 0, c, j * P:(j + 1) * P], wv[:, 0, c, :]), (sums[:, 0, c, j * P:(j + 1) * P], wv[:, 1, c, :]),
        (sums[:, 1, c, j * P:(j + 1) * P], wv[:, 0, c, :]))],
                  lambda dve, i, j, ps, y, chain: dve.tensor_scalar(y, ps, inverse[:, j:j + 1], None, ALU.mult),
                  lambda i, j: (ctx[:, 0, j, :], ctx[:, 1, j, :]), trips=1)
    wq = use_weight(k)
    q32, qf, t32 = k.T32(1), k.F(3), k.T32(1)
    qtop, qsum = k.small[:, 2, :], k.small[:, 3, :]
    product_stage(k, lambda i, j: tokens_out(xn, wq, tile_of(i, j)),
                  lambda act, i, j, ps, y, chain: act.activation(
                      q32[:, tile_of(i, j), :], ps, ACT.Exp, bias=qtop[:, bass.ds(tile_of(i, j), 1)],
                      accum_out=qsum[:, bass.ds(tile_of(i, j), 1)]),
                  value_on="scalar",
                  pre=lambda dve, i, j, ps: dve.tensor_reduce(qtop[:, bass.ds(tile_of(i, j), 1)], ps, AX.X, ALU.max,
                                                              negate=True))

    def query_sums(dve):
        dve.reciprocal(qsum, qsum).then_inc(k.step.sem, 1)
        dve.wait_ge(k.step.sem, k.step.count(1))
        dve.tensor_scalar(qsum, qsum, D ** -0.5, None, ALU.mult).then_inc(k.step.sem, 1)

    whole_stage(k, vector=query_sums)
    done(k, step=2)
    w1 = use_weight(k)
    transpose_stage(k, lambda dve, i, j, y, chain: dve.tensor_scalar(
        y, q32[:, tile_of(i, j), :], qsum[:, bass.ds(tile_of(i, j), 1)], None, ALU.mult), qf, turn=True)
    w12 = join_weights(k, w1, use_weight(k))
    product_stage(k, lambda i, j: tokens_out(qf, ctx, tile_of(i, j)),
                  lambda dve, i, j, ps, y, chain: dve.tensor_tensor(t32[:, tile_of(i, j), :], ps,
                                                                    t32[:, tile_of(i, j), :], ALU.add), turn=False,
                  copies=[(t32, all_tiles(k.ins["xn_dram"]))], needs_copies=True)
    x2f = k.F(2)
    transpose_stage(k, lambda dve, i, j, y, chain: dve.tensor_copy(y, t32[:, tile_of(i, j), :]), x2f)
    product_stage(k, lambda i, j: tokens_out(x2f, w12, tile_of(i, j)), add_to_x(k, t32), steps=2)


def join_weights(k, w1, w2):

    def products(i, j):
        f = slice(j * P, (j + 1) * P)
        return [x for c in range(KC) for x in ((w1[:, 0, c, f], w2[:, 0, c, :]), (w1[:, 0, c, f], w2[:, 1, c, :]),
                                               (w1[:, 1, c, f], w2[:, 0, c, :]))]

    product_stage(k, products, as_is, lambda i, j: (w1[:, 0, j, :], w1[:, 1, j, :]), in_place=True,
                  value_on="scalar", trips=1, turn=False)
    k.slot = 1 - k.slot
    return w1


def add_to_x(k, t32, row=None):
    def value(dve, i, j, ps, y, chain):
        x = k.x[:, tile_of(i, j), :]
        if row is not None:
            chain(dve.tensor_tensor(y, ps, row, ALU.add), 1)
            chain(dve.tensor_tensor(x, x, y, ALU.add), 2)
        else:
            chain(dve.tensor_tensor(x, ps, x, ALU.add), 1)
        return dve.tensor_tensor(x, x, t32[:, tile_of(i, j), :], ALU.add)
    return value



def layer2_graph(k):
    nc = k.nc
    xn, z = k.F(0), k.F(2)
    tt = k.big[1][:, 0:2048].bitcast(BF16).rearrange("p (t h m) -> p t h m", t=T, h=2)
    ring = k.big[3][:, 0:RING * 1024].bitcast(BF16).rearrange("p (g s n) -> p g s n", g=RING, s=4)
    w1 = use_weight(k)

    def relu_row(dve, i, j, ps, y, chain):
        chain(dve.tensor_tensor(y, ps, k.rows[:, 0, 0:P], ALU.add), 1)
        return dve.tensor_scalar(y, y, 0.0, None, ALU.max)

    product_stage(k, lambda i, j: tokens_out(xn, w1, tile_of(i, j), n=P), relu_row,
                  lambda i, j: (tt[:, tile_of(i, j), 0, :], tt[:, tile_of(i, j), 1, :]), steps=2, cols_out=P)
    with nc.Block() as block:

        @block.sync
        def _(sp):
            with sp.Fori(0, NC) as i:
                for g in range(RING):
                    sp.wait_ge(k.aux2.sem, i * RING + k.aux2.count(g + 1))
                    sp.dma_start(ring[:, g, :, :], k.ins["a_dram"][4 * g:4 * g + 4, :, bass.ts(i, CH)]
                                 .rearrange("s p n -> p s n")).then_inc(k.ring[g].sem, 16)

        @block.tensor
        def _(pe):
            pe.sem_inc(k.aux2.sem, RING)
            with pe.Fori(0, NC) as i:
                pe.wait_ge(k.valued.sem, i + k.valued.count(RING))
                for g in range(RING):
                    pe.wait_ge(k.ring[g].sem, i * 16 + k.ring[g].count(32))
                    pairs = [(tt[:, 4 * g + s, h, :], ring[:, g, s, :]) for s in range(4) for h in range(2)]
                    accumulate(pe, k.bank[0][:, :], pairs, start=g == 0, stop=False).then_inc(k.aux2.sem, 1)
                for s in range(4):
                    pairs = [(tt[:, i * 4 + s, h, :], k.ident[:, :]) for h in range(2)]
                    last = accumulate(pe, k.bank[0][:, s * P:(s + 1) * P], pairs, start=False, stop=s == 3)
                last.then_inc(k.full.sem, 1)

        @block.vector
        def _(dve):
            with dve.Fori(0, NC) as i:
                hi, lo = z[:, 0, bass.ts(i, CH)], z[:, KC, bass.ts(i, CH)]
                dve.wait_ge(k.full.sem, i + k.full.count(1))
                dve.tensor_copy(hi, k.bank[0][:, :]).then_inc(k.step.sem, 1)
                dve.wait_ge(k.step.sem, i + k.step.count(1))
                dve.tensor_tensor(lo, k.bank[0][:, :], hi, ALU.subtract).then_inc(k.valued.sem, 1)

    done(k, aux2=RING * NC + RING, full=NC, valued=NC, step=NC)
    for g in range(RING):
        k.ring[g].base += 16 * NC
    w2 = use_weight(k)
    product_stage(k, lambda i, j: tokens_out(z, w2, tile_of(i, j), blocks=1),
                  lambda dve, i, j, ps, y, chain: dve.tensor_tensor(k.x[:, tile_of(i, j), :], ps,
                                                                    k.x[:, tile_of(i, j), :], ALU.add),
                  copies=[(k.T32(1), all_tiles(k.ins["xn_dram"])), *row_loads(k, "L2_mix_ln_gamma", "L2_mix_ln_beta")])


def layer2_mix(k):
    x2, q = k.F(0), k.F(1)
    kp, v, t32 = k.TH(2), k.TH(3), k.T32(1)
    ebuf = k.big[3][:, 0:RING * D].rearrange("p (r d) -> p r d", r=RING)
    moments_stage(k, t32, EPS)
    transpose_stage(k, normalise(k, t32, k.rows[:, 0, :], k.rows[:, 1, :]), x2, steps=2)
    bq = k.col("L2_mix_bq", KC)

    def elu(dve, y, e, j):
        return dve.scalar_tensor_tensor(y, e, 1.0, y, ALU.min, ALU.add)

    def q_value(dve, i, j, ps, y, chain):
        chain(dve.tensor_scalar(y, ps, bq[:, j:j + 1], 0.0, ALU.add, ALU.max), 1)
        return elu(dve, y, ebuf[:, j, :], j)

    wq = use_weight(k)
    product_stage(k, lambda i, j: features_out(x2, wq, j, i), q_value, f_halves(q), steps=2,
                  pre=lambda act, i, j, ps: act.activation(ebuf[:, j, :], ps, ACT.Exp, bias=bq[:, j:j + 1]),
                  copies=row_loads(k, "L2_mix_bk", "L2_mix_bv", "L2_mix_out_b"))
    wk = use_weight(k)
    t2 = k.T32(3)
    bias = k.big[3][:, RING * D:(RING + 1) * D].bitcast(BF16).rearrange("p (h d) -> p h d", h=2)

    def bias_halves(dve):
        dve.tensor_copy(bias[:, 0, :], k.rows[:, 0, :]).then_inc(k.step.sem, 1)
        dve.wait_ge(k.step.sem, k.step.count(1))
        dve.tensor_tensor(bias[:, 1, :], k.rows[:, 0, :], bias[:, 0, :], ALU.subtract).then_inc(k.step.sem, 1)

    whole_stage(k, vector=bias_halves)
    done(k, step=2)

    def k_value(dve, i, j, ps, y, chain):
        chain(dve.tensor_scalar(y, ps, 0.0, None, ALU.max), 1)
        return elu(dve, y, ebuf[:, j, :], j)

    product_stage(k, lambda i, j: [(k.ident[:, :], bias[:, 0, :]), (k.ident[:, :], bias[:, 1, :]),
                                   *tokens_out(x2, wk, tile_of(i, j))],
                  k_value, t_halves(kp), steps=2,
                  pre=lambda act, i, j, ps: act.activation(ebuf[:, j, :], ps, ACT.Exp))
    wv = use_weight(k)
    product_stage(k, lambda i, j: tokens_out(x2, wv, tile_of(i, j)), plus_row(k.rows[:, 1, :]), t_halves(v))
    key_value_stage(k, kp, v, k.kv)
    linear_attention(k, q, k.kv, 1e-8, [(t2, all_tiles(k.ins["xn_dram"]))])
    wo = use_weight(k)
    product_stage(k, lambda i, j: tokens_out(q, wo, tile_of(i, j)), add_to_x(k, t2, k.rows[:, 2, :]), steps=3,
                  stats=rows_of(k.x))



def layer3_graph(k):
    nc, ins = k.nc, k.ins
    t32, h, u, xn32 = k.T32(1), k.F(2), k.TH(1), k.T32(0)
    ring = k.big[3][:, 0:RING * 1024].bitcast(BF16).rearrange("p (g s n) -> p g s n", g=RING, s=4)
    moments_stage(k, t32, EPS, row_loads(k, "L3_gnn_gamma", "L3_gnn_beta", "L3_gnn_b_l"))
    transpose_stage(k, normalise(k, t32, k.rows[:, 0, :], k.rows[:, 1, :]), h, steps=2)
    wl = use_weight(k)
    product_stage(k, lambda i, j: tokens_out(h, wl, tile_of(i, j)), as_is, t_halves(u), value_on="scalar")
    wr = use_weight(k)
    turn = WeightTurn(k)
    with nc.Block() as block:

        @block.sync
        def _(sp):
            turn.sync(sp)
            with sp.Fori(0, NC) as i:
                for g in range(RING):
                    sp.wait_ge(k.aux2.sem, i * RING + k.aux2.count(g + 1))
                    sp.dma_start(ring[:, g, :, :], ins["at_dram"][4 * g:4 * g + 4, :, bass.ts(i, CH)]
                                 .rearrange("s p n -> p s n")).then_inc(k.ring[g].sem, 16)

        @block.tensor
        def _(pe):
            pe.sem_inc(k.aux2.sem, RING)
            with pe.Fori(0, NC) as i:
                for g in range(RING):
                    pe.wait_ge(k.ring[g].sem, i * 16 + k.ring[g].count(32))
                    for j in range(4):
                        if g == 0:
                            pe.wait_ge(k.valued.sem, i * RING + k.valued.count(j + 1))
                        pairs = [(ring[:, g, s, j * P:(j + 1) * P], u[:, 4 * g + s, h_, :])
                                 for s in range(4) for h_ in range(2)]
                        last = accumulate(pe, k.bank[j][:, :], pairs, start=g == 0, stop=g == RING - 1)
                    last.then_inc(k.aux2.sem, 1)
                for j in range(4):
                    accumulate(pe, k.bank[RING + j][:, :], tokens_out(h, wr, tile_of(i, j))).then_inc(k.full.sem, 1)

        @block.vector
        def _(dve):
            turn.vector(dve)
            with dve.Fori(0, NC) as i:
                for j in range(4):
                    t, y = tile_of(i, j), k.tmp[:, j, :]
                    n = 0
                    dve.wait_ge(k.full.sem, i * RING + k.full.count(j + 1))

                    def do(ins_):
                        nonlocal n
                        ins_.then_inc(k.step.sem, 1)
                        n += 1
                        dve.wait_ge(k.step.sem, i * (RING * 4) + k.step.count(j * 4 + n))

                    do(dve.tensor_scalar(y, k.bank[j][:, :], k.rdegree[:, bass.ds(t, 1)], None, ALU.mult))
                    do(dve.tensor_tensor(y, y, k.rows[:, 2, :], ALU.add))
                    do(dve.tensor_tensor(y, k.bank[RING + j][:, :], y, ALU.add))
                    do(dve.scalar_tensor_tensor(y, y, 0.0, xn32[:, t, :], ALU.max, ALU.add))
                    dve.tensor_tensor(k.x[:, t, :], k.x[:, t, :], y, ALU.add).then_inc(k.valued.sem, 1)
                    dve.wait_ge(k.valued.sem, i * RING + k.valued.count(RING + j + 1))
                    dve.bn_stats(k.moments[:, bass.ds(t, 1), :].rearrange("p a s -> p (a s)"),
                                 k.x[:, t, :]).then_inc(k.stat.sem, 1)

        @block.scalar
        def _(act):
            turn.scalar(act)

    done(k, aux2=RING * NC + RING, full=T, valued=T, step=4 * T, stat=T)
    for g in range(RING):
        k.ring[g].base += 16 * NC
    turn.finish()


def quantize_stage(k):
    nc = k.nc
    _, p, blocks, n, _ = k.staged_spec
    with nc.Block() as block:

        @block.scalar
        def _(act):
            act.wait_ge(k.staged.sem, k.staged.count(0))
            for c in range(blocks):
                act.activation(k.tmp[:, c, 0:n], k.staging[:, c, 0:n], ACT.Abs).then_inc(k.hi.sem, 1)

        @block.tensor
        def _(pe):
            for c in range(blocks):
                pe.wait_ge(k.hi.sem, k.hi.count(c + 1))
                pe.matmul(k.bank[c][:, 0:n], k.onesf[:, :], k.tmp[:, c, 0:n], start=True,
                          stop=True).then_inc(k.full.sem, 1)

        @block.vector
        def _(dve):
            count = 0
            for s in range(6):
                for c in range(blocks):
                    w, scale, y = k.staging[:, c, 0:n], k.bank[RING + c][:, 0:n], k.tmp[:, c, 0:n]
                    if s == 0:
                        dve.wait_ge(k.full.sem, k.full.count(c + 1))
                        ins = dve.tensor_scalar(scale, k.bank[c][:, 0:n], 1.0 / P, EPS, ALU.mult, ALU.add)
                    else:
                        dve.wait_ge(k.step.sem, k.step.count((s - 1) * blocks + c + 1))
                        if s == 1:
                            ins = dve.reciprocal(y, scale)
                        elif s == 2:
                            ins = dve.tensor_tensor(y, w, y, ALU.mult)
                        elif s == 3:
                            ins = dve.tensor_scalar(y, y, MAGIC, MAGIC, ALU.add, ALU.subtract)
                        elif s == 4:
                            ins = dve.tensor_scalar(y, y, -1.0, 1.0, ALU.max, ALU.min)
                        else:
                            ins = dve.tensor_tensor(w, y, scale, ALU.mult)
                    ins.then_inc(k.step.sem, 1)

    done(k, hi=blocks, full=blocks, step=6 * blocks)


def layer3_ffn(k):
    xn, gate, hidden = k.F(0), k.F32v(1), k.F(2)
    for n in (4, 4, 3):
        wg = use_weight(k)
        product_stage(k, lambda i, j: features_out(xn, wg, j, i),
                      lambda act, i, j, ps, y, chain: act.activation(gate[:, j, bass.ts(i, CH)], ps, ACT.Silu),
                      value_on="scalar", width=n)
        wu = use_weight(k)
        product_stage(k, lambda i, j: features_out(xn, wu, j, i),
                      lambda dve, i, j, ps, y, chain: dve.tensor_tensor(y, ps, gate[:, j, bass.ts(i, CH)], ALU.mult),
                      f_halves(hidden), width=n)
        wd = use_weight(k)
        product_stage(k, lambda i, j: tokens_out(hidden, wd, tile_of(i, j), blocks=n),
                      lambda dve, i, j, ps, y, chain: dve.tensor_tensor(k.x[:, tile_of(i, j), :], ps,
                                                                        k.x[:, tile_of(i, j), :], ALU.add))



HEADS, DH = 8, 64
FEATS = 266
R_CHUNKS = [(0, 128), (128, 128), (256, 10)]
KERNEL_EPS = 1e-4
UNIT = 4


class Performer:

    def __init__(self, k):
        w = k.big[0]
        n = UNIT * FEATS
        self.e = [w[:, g * n:(g + 1) * n].rearrange("p (h r) -> p h r", h=UNIT) for g in range(2)]
        self.kh = [w[:, (2 + g) * n:(3 + g) * n].bitcast(BF16).rearrange("p (a h r) -> p a h r", a=2, h=UNIT)
                   for g in range(2)]
        self.ctx = w[:, 4 * n:4 * n + 1584].bitcast(BF16).rearrange("p (c a h d) -> p c a h d", c=3, a=2, h=HEADS)
        w = k.kv[:, :, :, :, :].rearrange("p a b c d -> p (a b c d)").bitcast(F32)
        self.tops = w[:, 0:T * HEADS].rearrange("p (t h) -> p t h", t=T)
        self.stab = w[:, 128:130]
        self.halfsel = w[:, 130:132]
        self.bias = w[:, 132:140].rearrange("p (g h) -> p g h", g=2)
        self.top = w[:, 140:148].rearrange("p (g h) -> p g h", g=2)
        self.rden = w[:, 148:156].rearrange("p (g h) -> p g h", g=2)


def features_of(src, pj, t, g, bank):
    out = []
    for hh in range(UNIT):
        b = 2 * g + hh // 2
        hi, lo = src[:, b, bass.ts(t, P)], src[:, KC + b, bass.ts(t, P)]
        whi, wlo = pj[:, 0, hh % 2, 0:FEATS], pj[:, 1, hh % 2, 0:FEATS]
        out.append((bank[hh][:, 0:FEATS], [(hi, whi), (hi, wlo), (lo, whi)]))
    return out


def key_top_stage(k, pf, src, pj):
    nc = k.nc
    with nc.Block() as block:

        @block.tensor
        def _(pe):
            with pe.Fori(0, T) as t:
                for g in range(2):
                    pe.wait_ge(k.aux.sem, t * 2 + k.aux.count(g + 1))
                    for out, pairs in features_of(src, pj, t, g, k.bank[4 * g:4 * g + 4]):
                        last = accumulate(pe, out, pairs)
                    last.then_inc(k.full.sem, 1)

        @block.vector
        def _(dve):
            dve.sem_inc(k.aux.sem, 2)
            dve.tensor_scalar(pf.halfsel, k.headmask[:, 0:P:DH], 0.5, None, ALU.mult).then_inc(k.step.sem, 1)
            with dve.Fori(0, T) as t:
                for g in range(2):
                    dve.wait_ge(k.full.sem, t * 2 + k.full.count(g + 1))
                    dve.tensor_reduce(pf.tops[:, t, UNIT * g:UNIT * (g + 1)],
                                      k.psum[:, UNIT * g:UNIT * (g + 1), 0:FEATS], AX.X,
                                      ALU.max).then_inc(k.aux.sem, 1)
            dve.wait_ge(k.aux.sem, k.aux.count(2 * T + 2))
            dve.tensor_reduce(pf.stab[:, 1:2], pf.tops, AX.XY, ALU.max).then_inc(k.step.sem, 1)
            dve.wait_ge(k.aux2.sem, k.aux2.count(1))
            dve.tensor_scalar(pf.stab[:, 0:1], pf.stab[:, 0:1], -1.0, None, ALU.mult).then_inc(k.step.sem, 1)

        @block.gpsimd
        def _(pool):
            pool.wait_ge(k.step.sem, k.step.count(2))
            pool.partition_all_reduce(pf.stab[:, 0:1], pf.stab[:, 1:2], P,
                                      bass.bass_isa.ReduceOp.max).then_inc(k.aux2.sem, 1)

    done(k, aux=2 * T + 2, full=2 * T, step=3, aux2=1)



def unit_wait(eng, sig, t, n, each=1):
    if isinstance(t, int) and t * 2 + n <= 0:
        return
    eng.wait_ge(sig.sem, t * (2 * each) + sig.count(each * n))


def squares(eng, k, src, t, g):
    y = k.tmp[:, g, 0:2 * P].rearrange("p (b n) -> p b n", b=2)
    eng.tensor_tensor(y, src[:, 2 * g:2 * g + 2, bass.ts(t, P)], src[:, KC + 2 * g:KC + 2 * g + 2, bass.ts(t, P)],
                      ALU.add).then_inc(k.step.sem, 1)
    unit_wait(eng, k.step, t, g + 1)
    eng.tensor_tensor(y, y, y, ALU.mult).then_inc(k.squared.sem, 1)


def unit_products(pe, k, pf, src, pj, t, g):
    unit_wait(pe, k.squared, t, g + 1)
    unit_wait(pe, k.half_used, t, g + 1)
    for b in range(2):
        pe.matmul(k.bank[4][:, 300 + 2 * b:302 + 2 * b], k.tmp[:, g, b * P:(b + 1) * P], pf.halfsel,
                  start=True, stop=True, skip_group_check=True)
    for hh, (out, pairs) in enumerate(features_of(src, pj, t, g, k.bank[4:8])):
        if hh == UNIT // 2:
            last.then_inc(k.half_full.sem, 1)
            unit_wait(pe, k.valued, t, g + RING)
        last = accumulate(pe, out, pairs)
    last.then_inc(k.full.sem, 1)


def unit_exponentials(act, k, pf, t, g, rest):
    for hh in range(UNIT):
        if hh == UNIT // 2:
            last.then_inc(k.half_used.sem, 1)
            unit_wait(act, rest, t, g + 1)
        last = act.activation(pf.e[g][:, hh, :], k.bank[4 + hh][:, 0:FEATS], ACT.Exp, bias=pf.bias[:, g, hh:hh + 1])
    last.then_inc(k.valued.sem, 1)


def key_features_stage(k, pf, src, v, pj):
    nc = k.nc
    ratio = FEATS ** -0.5
    with nc.Block() as block:

        @block.tensor
        def _(pe):
            for b in range(4):
                pe.matmul(k.bank[b][:, :], k.zeros[:, 0:P], k.zeros[:, :], start=True, stop=False,
                          skip_group_check=True)

            def context(t, g):
                unit_wait(pe, k.lo, t, g + 1 + RING)
                for hh in range(UNIT):
                    h = UNIT * g + hh
                    for c, (r0, m) in enumerate(R_CHUNKS):
                        hi, lo = (pf.kh[g][:, a, hh, r0:r0 + m] for a in range(2))
                        vh, vl = (v[:, t, a, h * DH:(h + 1) * DH] for a in range(2))
                        accumulate(pe, k.bank[c][0:m, h * DH:(h + 1) * DH], [(hi, vh), (hi, vl), (lo, vh)],
                                   start=False, stop=False)
                        last = accumulate(pe, k.bank[3][0:m, 8 * c + h:8 * c + h + 1],
                                          [(hi, k.ones[:, 0:1]), (lo, k.ones[:, 0:1])], start=False, stop=False)
                last.then_inc(k.aux2.sem, 1)

            for g in range(2):
                unit_products(pe, k, pf, src, pj, 0, g)
            with pe.Fori(0, T - 1) as t:
                for g in range(2):
                    unit_products(pe, k, pf, src, pj, t + 1, g)
                    context(t, g)
            for g in range(2):
                context(T - 1, g)
            for b in range(4):
                last = pe.matmul(k.bank[b][:, :], k.zeros[:, 0:P], k.zeros[:, :], start=False, stop=True,
                                 skip_group_check=True)
            last.then_inc(k.full.sem, 1)

        @block.vector
        def _(dve):

            def bias(t, g):
                unit_wait(dve, k.half_full, t, g + 1)
                unit_wait(dve, k.valued, t, g - 1 + RING)
                dve.tensor_scalar(pf.bias[:, g, :], k.bank[4][:, 300:304], -1.0, pf.stab[:, 0:1], ALU.mult,
                                  ALU.add).then_inc(k.biased.sem, 1)

            def step(t, g, follows, second):
                if follows:
                    bias(*((t, 1) if g == 0 else (t + 1, 0)))
                unit_wait(dve, k.valued, t, g + 1 + RING)
                dve.tensor_scalar(pf.e[g], pf.e[g], KERNEL_EPS, ratio, ALU.add, ALU.mult).then_inc(k.astep.sem, 1)
                unit_wait(dve, k.astep, t, g + 1)
                unit_wait(dve, k.aux2, t, g + 1)
                dve.tensor_copy(pf.kh[g][:, 0, :, :], pf.e[g]).then_inc(k.hi.sem, 1)
                if second:
                    squares(dve, k, src, t + 1, g)

            for g in range(2):
                squares(dve, k, src, 0, g)
            bias(0, 0)
            with dve.Fori(0, T - 1) as t:
                for g in range(2):
                    step(t, g, True, True)
            step(T - 1, 0, True, False)
            step(T - 1, 1, False, False)

        @block.scalar
        def _(act):
            act.sem_inc(k.half_used.sem, 1)
            with act.Fori(0, T) as t:
                for g in range(2):
                    unit_wait(act, k.biased, t, g + 1)
                    unit_wait(act, k.lo, t, g - 1 + RING)
                    unit_exponentials(act, k, pf, t, g, k.full)

        @block.gpsimd
        def _(pool):
            pool.sem_inc(k.aux2.sem, 2)
            with pool.Fori(0, T) as t:
                for g in range(2):
                    unit_wait(pool, k.hi, t, g + 1)
                    pool.tensor_tensor(pf.kh[g][:, 1, :, :], pf.e[g], pf.kh[g][:, 0, :, :],
                                       ALU.subtract).then_inc(k.lo.sem, 1)

    n = 2 * T
    done(k, squared=n, full=n + 1, valued=n, step=n, biased=n, astep=n, hi=n, lo=n, aux2=n + 2,
         half_full=n, half_used=n + 1)


def performer_context_stage(k, pf):
    with k.nc.Block() as block:

        @block.vector
        def _(dve):
            for s in range(2):
                for c, (_, m) in enumerate(R_CHUNKS):
                    for ps, d in ((k.bank[c][0:m, :].rearrange("p (h d) -> p h d", h=HEADS), slice(0, DH)),
                                  (k.bank[3][0:m, 8 * c:8 * c + 8].unsqueeze(2), slice(DH, DH + 1))):
                        hi, lo = (pf.ctx[0:m, c, a, :, d] for a in range(2))
                        if s == 0:
                            dve.tensor_copy(hi, ps).then_inc(k.step.sem, 1)
                        else:
                            dve.wait_ge(k.step.sem, k.step.count(6))
                            dve.tensor_tensor(lo, ps, hi, ALU.subtract).then_inc(k.step.sem, 1)

    done(k, step=12)


def query_features_stage(k, pf, src, pj, qt, out):
    nc = k.nc
    ratio = FEATS ** -0.5
    ncol = DH + 1

    def run(eng, step):
        step(0, 0, True, False, True)
        step(0, 1, True, True, True)
        with eng.Fori(1, T - 1) as t:
            for g in range(2):
                step(t, g, True, True, True)
        step(T - 1, 0, True, True, False)
        step(T - 1, 1, False, True, False)

    def after(t, g):
        return (t, 1) if g == 0 else (t + 1, 0)

    def before(t, g):
        return (t, 0) if g == 1 else (t - 1, 1)

    with nc.Block() as block:

        @block.tensor
        def _(pe):

            def multiply(t, g):
                unit_wait(pe, k.lo, t, g + 1 + RING)
                unit_wait(pe, k.out, t, g + 1)
                for hh in range(UNIT):
                    pairs = []
                    for c, (r0, m) in enumerate(R_CHUNKS):
                        qh, ql = (qt[0:m, g, c, a, hh * P:(hh + 1) * P] for a in range(2))
                        ch, cl = (pf.ctx[0:m, c, a, UNIT * g + hh, 0:ncol] for a in range(2))
                        pairs += [(qh, ch), (qh, cl), (ql, ch)]
                    last = accumulate(pe, k.bank[3][:, hh * ncol:(hh + 1) * ncol], pairs)
                last.then_inc(k.weighed.sem, 1)

            def step(t, g, follows, precedes, _):
                if follows:
                    unit_products(pe, k, pf, src, pj, *after(t, g))
                unit_wait(pe, k.astep, t, g + 1)
                unit_wait(pe, k.lo, t, g + RING)
                for c, (r0, m) in enumerate(R_CHUNKS):
                    for hh in range(UNIT):
                        last = pe.transpose(k.bank[c][0:m, hh * P:(hh + 1) * P], pf.e[g][:, hh, r0:r0 + m],
                                            k.identf[:, :])
                last.then_inc(k.turned.sem, 1)
                if precedes:
                    multiply(*before(t, g))

            unit_products(pe, k, pf, src, pj, 0, 0)
            run(pe, step)
            multiply(T - 1, 1)

        @block.vector
        def _(dve):
            dve.sem_inc(k.out.sem, 1)

            def peak(t, g):
                unit_wait(dve, k.half_full, t, g + 1)
                unit_wait(dve, k.valued, t, g - 1 + RING)
                top, bias, half_lengths = pf.top[:, g, :], pf.bias[:, g, :], k.bank[4][:, 300:304]
                dve.tensor_reduce(top[:, 0:2], k.psum[:, 4:6, 0:FEATS], AX.X, ALU.max).then_inc(k.peak.sem, 1)
                unit_wait(dve, k.peak, t, g + 1)
                dve.scalar_tensor_tensor(bias[:, 0:2], half_lengths[:, 0:2], -1.0, top[:, 0:2], ALU.mult,
                                         ALU.subtract)
                dve.tensor_scalar(bias[:, 2:4], half_lengths[:, 2:4], -1.0, None, ALU.mult).then_inc(k.biased.sem, 1)
                unit_wait(dve, k.full, t, g + 1)
                dve.tensor_reduce(top[:, 2:4], k.psum[:, 6:8, 0:FEATS], AX.X, ALU.max).then_inc(k.peak_rest.sem, 1)
                unit_wait(dve, k.biased, t, g + 1)
                unit_wait(dve, k.peak_rest, t, g + 1)
                dve.tensor_tensor(bias[:, 2:4], bias[:, 2:4], top[:, 2:4], ALU.subtract).then_inc(k.biased_rest.sem, 1)

            def plus_eps(t, g):
                unit_wait(dve, k.valued, t, g + 1 + RING)
                dve.tensor_scalar(pf.e[g], pf.e[g], KERNEL_EPS, ratio, ALU.add, ALU.mult).then_inc(k.astep.sem, 1)

            def divide(t, g):
                num = k.bank[3][:, 0:UNIT * ncol].rearrange("p (h d) -> p h d", h=UNIT)
                unit_wait(dve, k.weighed, t, g + 1)
                dve.reciprocal(pf.rden[:, g, :].unsqueeze(2), num[:, :, DH:ncol]).then_inc(k.inverse.sem, 1)
                unit_wait(dve, k.inverse, t, g + 1)
                dve.tensor_tensor(out[:, t, UNIT * g * DH:UNIT * (g + 1) * DH].rearrange("p (h d) -> p h d", h=UNIT),
                                  num[:, :, 0:DH], pf.rden[:, g, :].unsqueeze(2).to_broadcast([P, UNIT, DH]),
                                  ALU.mult).then_inc(k.out.sem, 1)

            def step(t, g, follows, precedes, _):
                if follows:
                    peak(*after(t, g))
                if precedes:
                    divide(*before(t, g))
                if follows:
                    plus_eps(*after(t, g))
                unit_wait(dve, k.hi, t, g + 1)
                for c, (_, m) in enumerate(R_CHUNKS):
                    last = dve.tensor_tensor(qt[0:m, g, c, 1, :], k.bank[c][0:m, :], qt[0:m, g, c, 0, :],
                                             ALU.subtract)
                last.then_inc(k.lo.sem, 1)

            peak(0, 0)
            plus_eps(0, 0)
            run(dve, step)
            divide(T - 1, 1)

        @block.scalar
        def _(act):

            def exponential(t, g):
                unit_wait(act, k.biased, t, g + 1)
                unit_wait(act, k.turned, t, g - 1)
                unit_exponentials(act, k, pf, t, g, k.biased_rest)

            def step(t, g, follows, precedes, _):
                if follows:
                    exponential(*after(t, g))
                unit_wait(act, k.turned, t, g + 1)
                unit_wait(act, k.weighed, t, g - 1)
                for c, (_, m) in enumerate(R_CHUNKS):
                    last = act.activation(qt[0:m, g, c, 0, :], k.bank[c][0:m, :], ACT.Copy)
                last.then_inc(k.hi.sem, 1)

            act.sem_inc(k.half_used.sem, 1)
            exponential(0, 0)
            run(act, step)

        @block.gpsimd
        def _(pool):
            for g in range(2):
                squares(pool, k, src, 0, g)
            with pool.Fori(0, T - 1) as t:
                for g in range(2):
                    unit_wait(pool, k.full, t, g + 1)
                    squares(pool, k, src, t + 1, g)

    n = 2 * T
    done(k, squared=n, full=n, valued=n, step=n, peak=n, biased=n, astep=n, hi=n, lo=n, turned=n, weighed=n,
         inverse=n, out=n + 1, half_full=n, half_used=n + 1, peak_rest=n, biased_rest=n)


def layer3_mix(k):
    xn, kf, v, qf = k.F(0), k.F(1), k.TH(2), k.F(3)
    norm = float(DH) ** -0.25
    scaled = lambda act, i, j, ps, y, chain: act.activation(y, ps, ACT.Copy, scale=norm)
    wq = use_weight(k)
    product_stage(k, lambda i, j: features_out(xn, wq, j, i), scaled, f_halves(qf), value_on="scalar")
    wk = use_weight(k)
    product_stage(k, lambda i, j: features_out(xn, wk, j, i), scaled, f_halves(kf), value_on="scalar")
    wv = use_weight(k)
    product_stage(k, lambda i, j: tokens_out(xn, wv, tile_of(i, j)), as_is, t_halves(v), value_on="scalar")
    pj = use_weight(k)
    pf = Performer(k)
    key_top_stage(k, pf, kf, pj)
    key_features_stage(k, pf, kf, v, pj)
    performer_context_stage(k, pf)
    qt = k.big[1][:, 0:2 * 1536].bitcast(BF16).rearrange("p (g c a n) -> p g c a n", g=2, c=3, a=2)
    attn = k.T32(2)
    query_features_stage(k, pf, qf, pj, qt, attn)
    af, t32 = k.F(1), k.T32(2)
    transpose_stage(k, lambda dve, i, j, y, chain: dve.tensor_copy(y, attn[:, tile_of(i, j), :]), af, turn=True)

    def add_t32(row):
        def value(dve, i, j, ps, y, chain):
            t = t32[:, tile_of(i, j), :]
            if row is None:
                return dve.tensor_tensor(t, ps, t, ALU.add)
            chain(dve.tensor_tensor(y, ps, row, ALU.add), 1)
            return dve.tensor_tensor(t, y, t, ALU.add)
        return value

    wo = use_weight(k)
    product_stage(k, lambda i, j: tokens_out(af, wo, tile_of(i, j)), add_t32(k.rows[:, 0, :]), steps=2,
                  copies=[*row_loads(k, "L3_mix_bo", "L3_mix_ln0_g", "L3_mix_ln0_b"),
                          (t32, all_tiles(k.ins["xn_dram"]))], needs_copies=True, stats=rows_of(t32))
    moments_stage(k, t32, EPS, tiles=0)
    h = k.F(0)
    transpose_stage(k, normalise(k, t32, k.rows[:, 1, :], k.rows[:, 2, :]), h, steps=2, store=tile_in(t32))
    for part, dst in enumerate((k.F(1), k.F(3))):
        w1 = use_weight(k)
        b1 = k.cols[:, k.ins["col_index"]["L3_mix_b1"] + KC * part:][:, 0:KC]
        product_stage(k, lambda i, j: features_out(h, w1, j, i), lambda act, i, j, ps, y, chain:
                      act.activation(y, ps, ACT.Gelu, bias=b1[:, j:j + 1]), f_halves(dst), value_on="scalar",
                      copies=() if part else row_loads(k, "L3_mix_b2", "L3_mix_ln1_g", "L3_mix_ln1_b"))
    xn_dram = all_tiles(k.ins["xn_dram"])
    for part, src in enumerate((k.F(1), k.F(3))):
        w2 = use_weight(k)
        product_stage(k, lambda i, j: tokens_out(src, w2, tile_of(i, j)), add_t32(None if part else k.rows[:, 0, :]),
                      steps=1 if part else 2, stats=rows_of(t32) if part else None,
                      copies=[(k.T32(1), xn_dram), (k.T32(0), xn_dram)] if part else ())
    moments_stage(k, t32, EPS, tiles=0)
    norm_add_stage(k, t32, k.rows[:, 1, :], k.rows[:, 2, :])



TILES = E // P
TAKEN = 4
GROUPS = TILES // TAKEN
NOWHERE = 4096.0


def edge_range_stage(k, dst_f, src_f, table):
    nc, ins = k.nc, k.ins
    w = k.big[3]
    raw = w[:, 0:2 * TILES].bitcast(I32).rearrange("p (a t) -> p a t", a=2)
    consts = w[:, 600:600 + 6 + 2 * T]
    reach = w[:, 700:706]
    near = w[:, 710:710 + T]
    cand = w[:, 800:800 + 6 * T].rearrange("p (g a b) -> p g a b", g=3, a=2)
    ends = w[0:T, 1000:1002]
    row = w[0:1, 1010:1010 + 5 * T].rearrange("p (a b) -> p a b", a=5)
    groups = [min(P, TILES - g * P) for g in range(3)]
    with nc.Block() as block:

        @block.sync
        def _(sp):
            sp.dma_start(raw[:, 0, :], ins["dst"]).then_inc(k.loaded.sem, 16)
            sp.dma_start(raw[:, 1, :], ins["src"]).then_inc(k.loaded.sem, 16)
            sp.dma_start(consts, ins["edge_consts"]).then_inc(k.loaded.sem, 16)
            sp.dma_start(k.iota, ins["iota"].rearrange("a n -> (a n)").partition_broadcast(P)
                         ).then_inc(k.loaded.sem, 16)

        @block.tensor
        def _(pe):
            pe.wait_ge(k.aux.sem, k.aux.count(1))
            for g, n in enumerate(groups):
                last = pe.transpose(k.bank[g][0:n, 0:P], dst_f[:, g * P:g * P + n], k.identf[:, :])
            last.then_inc(k.full.sem, 1)
            pe.wait_ge(k.aux.sem, k.aux.count(2))
            for a in range(2):
                for g in range(3):
                    last = pe.transpose(k.bank[4 + a][0:T, g * P:(g + 1) * P], cand[:, g, a, :], k.identf[:, :])
            last.then_inc(k.full.sem, 1)
            pe.wait_ge(k.aux.sem, k.aux.count(3))
            for a in range(2):
                last = pe.transpose(k.bank[6][0:1, a * T:(a + 1) * T], ends[:, a:a + 1], k.identf[0:T, 0:T])
            last.then_inc(k.full.sem, 1)

        @block.vector
        def _(dve):
            n = [0]

            def do(x, sig=None):
                if sig is not None:
                    x.then_inc(sig.sem, 1)
                    return
                x.then_inc(k.step.sem, 1)
                n[0] += 1
                dve.wait_ge(k.step.sem, k.step.count(n[0]))

            dve.wait_ge(k.loaded.sem, k.loaded.count(64))
            do(dve.tensor_copy(dst_f, raw[:, 0, :]), k.aux)
            do(dve.tensor_copy(src_f, raw[:, 1, :]))
            do(dve.memset(reach[:, 0:3], NOWHERE))
            do(dve.memset(reach[:, 3:6], -1.0))
            dve.wait_ge(k.full.sem, k.full.count(1))
            for g, m in enumerate(groups):
                do(dve.tensor_reduce(reach[0:m, g:g + 1], k.bank[g][0:m, 0:P], AX.X, ALU.min))
                do(dve.tensor_reduce(reach[0:m, 3 + g:4 + g], k.bank[g][0:m, 0:P], AX.X, ALU.max))
            start, end = consts[:, 6:6 + T], consts[:, 6 + T:6 + 2 * T]
            for g in range(3):
                do(dve.tensor_scalar(near, end, reach[:, g:g + 1], None, ALU.is_gt))
                do(dve.scalar_tensor_tensor(near, start, reach[:, 3 + g:4 + g], near, ALU.is_le, ALU.mult))
                do(dve.tensor_scalar(cand[:, g, 0, :], near, consts[:, 3 + g:4 + g], NOWHERE, ALU.mult, ALU.add))
                do(dve.tensor_scalar(cand[:, g, 1, :], near, consts[:, g:g + 1], None, ALU.mult))
            dve.sem_inc(k.aux.sem, 1)
            dve.wait_ge(k.full.sem, k.full.count(2))
            do(dve.tensor_reduce(ends[:, 0:1], k.bank[4][0:T, 0:3 * P], AX.X, ALU.min))
            do(dve.tensor_reduce(ends[:, 1:2], k.bank[5][0:T, 0:3 * P], AX.X, ALU.max))
            do(dve.tensor_tensor(ends[:, 0:1], ends[:, 0:1], ends[:, 1:2], ALU.min))
            dve.sem_inc(k.aux.sem, 1)
            dve.wait_ge(k.full.sem, k.full.count(3))
            do(dve.tensor_copy(row[:, 0:2, :], k.bank[6][0:1, 0:2 * T].rearrange("p (a b) -> p a b", a=2)))
            do(dve.tensor_scalar(row[:, 1, :], row[:, 1, :], 1.0, None, ALU.add))
            do(dve.tensor_tensor(row[:, 2, :], row[:, 1, :], row[:, 0, :], ALU.subtract))
            do(dve.tensor_copy(row[:, 3, :], row[:, 2, :]))
            a, b = 3, 4
            for s in (1, 2, 4, 8):
                do(dve.tensor_copy(row[:, b, 0:s], row[:, a, 0:s]))
                do(dve.tensor_tensor(row[:, b, s:T], row[:, a, s:T], row[:, a, 0:T - s], ALU.add))
                a, b = b, a
            do(dve.tensor_tensor(row[:, 1, :], row[:, a, :], row[:, 2, :], ALU.subtract))
            do(dve.tensor_copy(row[:, 2, :], row[:, a, :]))
            do(dve.tensor_copy(table, row[:, 0:3, :]))
            k.range_steps = n[0]

    done(k, loaded=64, aux=3, full=3, step=k.range_steps)


def adjacency_stage(k, dst_f, src_f, table, a):
    nc = k.nc
    hot_src = k.big[3][:, 0:TAKEN * N // 2].bitcast(BF16).rearrange("p (s n) -> p s n", s=TAKEN)
    hot_dst = k.kv[:, 0, 0, :, :]
    with nc.Block() as block:

        def block_range(eng, b, *names):
            top = (GROUPS - 1, T * GROUPS, T * GROUPS)
            return [eng.value_load(table[0:1, n, bass.ds(b, 1)], min_val=0, max_val=top[n]) for n in names]

        @block.sync
        def _(sp):
            copies = [(k.x[:, :, :], k.ins["x"].rearrange("(t p) d -> p t d", p=P))]
            start_copies(k, sp, copies)
            end_copies(k, sp, copies)

        @block.vector
        def _(dve):
            dve.sem_inc(k.hot_used.sem, TAKEN)
            with dve.Fori(0, T) as b:
                first, before, end = block_range(dve, b, 0, 1, 2)
                with dve.Fori(before, end) as q:
                    group = nc.s_assert_within(q + first - before, 0, GROUPS - 1, skip_runtime_bounds_check_because=(
                        "q runs over as many groups as the block's range has, and the range lies within all groups"))
                    for s in range(TAKEN):
                        e = group * TAKEN + s
                        dve.wait_ge(k.hot_used.sem, q * TAKEN + (s + 1))
                        dve.tensor_scalar(hot_dst[:, s, :], k.iota[:, bass.ts(b, P)], dst_f[:, bass.ds(e, 1)], None,
                                          ALU.is_equal).then_inc(k.hot_ready.sem, 1)
                        dve.tensor_scalar(hot_src[:, s, :], k.iota, src_f[:, bass.ds(e, 1)], None,
                                          ALU.is_equal).then_inc(k.hot_ready.sem, 1)

        @block.tensor
        def _(pe):
            with pe.Fori(0, T // 2) as i:
                for h in range(2):
                    b = i * 2 + h
                    before, end = block_range(pe, b, 1, 2)
                    pe.wait_ge(k.step.sem, b + k.step.count(1))
                    for c in range(NC):
                        pe.matmul(k.bank[4 * h + c], k.zeros[:, 0:P], k.zeros[:, :], start=True, stop=False,
                                  skip_group_check=True)
                    with pe.Fori(before, end) as q:
                        for s in range(TAKEN):
                            pe.wait_ge(k.hot_ready.sem, q * (2 * TAKEN) + (2 * s + 2))
                            for c in range(NC):
                                m = pe.matmul(k.bank[4 * h + c], hot_dst[:, s, :],
                                              hot_src[:, s, c * CH:(c + 1) * CH], start=False, stop=False,
                                              skip_group_check=True)
                            m.then_inc(k.hot_used.sem, 1)
                    pe.matmul(k.bank[4 * h + NC - 1], k.zeros[:, 0:P], k.zeros[:, :], start=False, stop=True,
                              skip_group_check=True).then_inc(k.full.sem, 1)

        @block.scalar
        def _(act):
            act.sem_inc(k.step.sem, 2)
            with act.Fori(0, T // 2) as i:
                for h in range(2):
                    act.wait_ge(k.full.sem, i * 2 + k.full.count(h + 1))
                    act.activation(a[:, bass.ds(i * 2 + h, 1), :].rearrange("p a n -> p (a n)"),
                                   k.psum[:, 4 * h:4 * h + 4, :].rearrange("p a n -> p (a n)"),
                                   ACT.Copy).then_inc(k.step.sem, 1)

    done(k, full=T, step=T + 2, loaded=16)


def adjacency_out_stage(k, a, at):
    nc, ins = k.nc, k.ins
    with nc.Block() as block:

        @block.tensor
        def _(pe):
            with pe.Fori(0, T) as s:
                for c in range(NC):
                    pe.wait_ge(k.valued.sem, s * NC + k.valued.count(c + 1))
                    for d in range(4):
                        last = pe.matmul(k.bank[c][:, d * P:(d + 1) * P], a[:, 4 * c + d, bass.ts(s, P)],
                                         k.ident[:, :], start=True, stop=True)
                    last.then_inc(k.full.sem, 1)

        @block.scalar
        def _(act):
            with act.Fori(0, T) as s:
                for c in range(NC):
                    act.wait_ge(k.full.sem, s * NC + k.full.count(c + 1))
                    act.activation(at[:, bass.ds(s, 1), c * CH:(c + 1) * CH].rearrange("p a n -> p (a n)"),
                                   k.bank[c], ACT.Copy).then_inc(k.valued.sem, 1)

        @block.vector
        def _(dve):
            for b in range(T):
                dve.tensor_reduce(k.rdegree[:, b:b + 1], a[:, b, :], AX.X, ALU.add).then_inc(k.step.sem, 1)
            dve.wait_ge(k.step.sem, k.step.count(T))
            dve.tensor_scalar(k.rdegree[:, :], k.rdegree[:, :], 1.0, None, ALU.max).then_inc(k.step.sem, 1)
            dve.wait_ge(k.step.sem, k.step.count(T + 1))
            dve.reciprocal(k.rdegree[:, :], k.rdegree[:, :]).then_inc(k.step.sem, 1)

        @block.sync
        def _(sp):
            sp.dma_start(ins["a_dram"].rearrange("t p n -> p t n"), a).then_inc(k.loaded.sem, 16)
            for s in range(T):
                sp.wait_ge(k.valued.sem, k.valued.count(RING + NC * (s + 1)))
                sp.dma_start(ins["at_dram"][s], at[:, s, :]).then_inc(k.aux.sem, 16)
            sp.wait_ge(k.aux.sem, k.aux.count(16 * T))
            sp.wait_ge(k.loaded.sem, k.loaded.count(16))

    done(k, full=T * NC, valued=T * NC, step=T + 2, loaded=16, aux=16 * T)


def graph_stages(k):
    whole = k.big_pair(0)
    dst_f, src_f = k.big[2][:, 0:TILES], k.big[2][:, TILES:2 * TILES]
    edge_range_stage(k, dst_f, src_f, k.table[:, :, :])
    adjacency_stage(k, dst_f, src_f, k.table, whole)
    adjacency_out_stage(k, whole, k.big_pair(2))



NEVER = -1e30


def edge_max_stage(k, q_dram, k_dram, top):
    nc, ins = k.nc, k.ins
    keys = [k.big[2 + a][:, :].bitcast(BF16).rearrange("p (h n) -> p h n", h=HEADS) for a in range(2)]
    w = k.big[1][:, :].bitcast(BF16)
    counts = w[:, 0:2 * N].rearrange("p (b n) -> p b n", b=2)
    mask = w[:, 2 * N:4 * N].rearrange("p (b n) -> p b n", b=2)
    qa = w[:, 4 * N:4 * N + 2 * HEADS * P].rearrange("p (b h n) -> p b h n", b=2, h=HEADS)
    scratch = w[:, 5 * N:7 * N].rearrange("p (b n) -> p b n", b=2)
    with nc.Block() as block:

        @block.scalar
        def _(act):
            for h in range(0, HEADS, 2):
                for a in range(2):
                    for r in range(2):
                        act.dma_start(keys[a][r * DH:(r + 1) * DH, h:h + 2, :],
                                      k_dram[a, h * DH:(h + 2) * DH, :].rearrange("(h d) n -> d h n", d=DH)
                                      ).then_inc(k.atg[h // 2].sem, 16)

        @block.sync
        def _(sp):
            with sp.Fori(0, T // 2) as i:
                for b in range(2):
                    t = i * 2 + b
                    sp.wait_ge(k.aux.sem, t + k.aux.count(1))
                    sp.dma_start(counts[:, b, :], ins["a_dram"][bass.ds(t, 1), :, :].rearrange("a p n -> p (a n)")
                                 ).then_inc(k.ring[b].sem, 16)
                    sp.wait_ge(k.valued.sem, t * HEADS + k.valued.count(RING - HEADS))
                    for a in range(2):
                        sp.dma_start(qa[a * DH:(a + 1) * DH, b, :, :],
                                     q_dram[a, :, bass.ts(t, P)].rearrange("(h d) n -> d h n", d=DH)
                                     ).then_inc(k.ring[2 + b].sem, 16)

        @block.tensor
        def _(pe):
            with pe.Fori(0, T // 2) as i:
                for b in range(2):
                    pe.wait_ge(k.ring[2 + b].sem, i * 32 + k.ring[2 + b].count(16 + 32))
                    for h in range(HEADS):
                        if b == 0 and h % 2 == 0:
                            pe.wait_ge(k.atg[h // 2].sem, k.atg[h // 2].count(64))
                        pe.wait_ge(k.valued.sem, i * (2 * HEADS) + k.valued.count(RING - 1 + b * HEADS + h))
                        for c in range(NC):
                            pairs = [(qa[:, b, h, :], keys[a][:, h, c * CH:(c + 1) * CH]) for a in range(2)]
                            last = accumulate(pe, k.bank[4 * (h % 2) + c], pairs)
                        last.then_inc(k.full.sem, 1)

        @block.vector
        def _(dve):
            with dve.Fori(0, T // 2) as i:
                for b in range(2):
                    t = i * 2 + b
                    dve.wait_ge(k.aux.sem, t + k.aux.count(3))
                    dve.wait_ge(k.step.sem, t + k.step.count(0))
                    for h in range(HEADS):
                        dve.wait_ge(k.full.sem, i * (2 * HEADS) + k.full.count(b * HEADS + h + 1))
                        dve.wait_ge(k.valued.sem, i * (2 * HEADS) + k.valued.count(RING - 1 + b * HEADS + h))
                        g = 4 * (h % 2)
                        dve.nop(nofuse=True)
                        dve.tensor_tensor_reduce(
                            scratch[:, h % 2, :], k.psum[:, g:g + 4, :].rearrange("p a n -> p (a n)"), mask[:, b, :],
                            1.0, -3e38, ALU.add, ALU.max, k.tile_top[:, h:h + 1]).then_inc(k.valued.sem, 1)
                    dve.wait_ge(k.valued.sem, t * HEADS + k.valued.count(RING + HEADS))
                    dve.tensor_copy(top[:, bass.ds(t, 1), :].rearrange("p a b -> p (a b)"),
                                    k.tile_top[:, :]).then_inc(k.step.sem, 1)

        @block.gpsimd
        def _(pool):
            pool.sem_inc(k.aux.sem, 2)
            with pool.Fori(0, T // 2) as i:
                for b in range(2):
                    pool.wait_ge(k.ring[b].sem, i * 16 + k.ring[b].count(32))
                    pool.wait_ge(k.step.sem, i * 2 + k.step.count(b - 1))
                    pool.nop(nofuse=True)
                    pool.tensor_scalar(mask[:, b, :], counts[:, b, :], 0.0, NEVER, ALU.is_equal,
                                       ALU.mult).then_inc(k.aux.sem, 1)

    done(k, aux=T + 2, full=T * HEADS, valued=T * HEADS, step=T)
    for b in range(2):
        k.ring[b].base += 16 * (T // 2)
        k.ring[2 + b].base += 32 * (T // 2)
    for g in range(4):
        k.atg[g].base += 64


def edge_max_out_stage(k, top, m_dram):
    nc = k.nc
    w = k.big[1]
    m32 = w[0:HEADS, 0:N]
    parts = w[0:HEADS, N:N + 3 * N // 2].bitcast(BF16).rearrange("p (a n) -> p a n", a=3)
    with nc.Block() as block:

        @block.tensor
        def _(pe):
            for t in range(T):
                last = pe.transpose(k.bank[t // 4][0:HEADS, t % 4 * P:(t % 4 + 1) * P], top[:, t, :], k.identf[:, :])
            last.then_inc(k.full.sem, 1)

        @block.vector
        def _(dve):
            dve.wait_ge(k.full.sem, k.full.count(1))
            n = [0]

            def do(ins):
                ins.then_inc(k.step.sem, 1)
                n[0] += 1
                dve.wait_ge(k.step.sem, k.step.count(n[0]))

            do(dve.tensor_scalar(m32, k.psum[0:HEADS, 0:4, :].rearrange("p a n -> p (a n)"), -1.0, None, ALU.mult))
            for a in range(3):
                do(dve.tensor_copy(parts[:, a, :], m32))
                if a < 2:
                    do(dve.tensor_tensor(m32, m32, parts[:, a, :], ALU.subtract))

        @block.sync
        def _(sp):
            sp.wait_ge(k.step.sem, k.step.count(6))
            sp.dma_start(m_dram.rearrange("a h n -> h a n"), parts).then_inc(k.loaded.sem, 16)
            sp.wait_ge(k.loaded.sem, k.loaded.count(16))

    done(k, full=1, step=6, loaded=16)


VALUE_COLS = 2 * DH + 1
BEHIND = 1
LEAD = 5


def edge_attention_stage(k, q_dram, k_dram, v_dram, m_dram, out):
    nc, ins = k.nc, k.ins
    w2 = k.big[2][:, :].bitcast(BF16)
    at = w2[:, 0:T * CH].rearrange("p (s n) -> p s n", s=T)
    keys = w2[:, T * CH:T * CH + 4 * N].rearrange("p (b a n) -> p b a n", b=2, a=2)
    w3 = k.big[3]
    vals = w3[:, 0:2080].bitcast(BF16).rearrange("p (b s d) -> p b s d", b=2, s=T)
    probs = w3[:, 2080:2080 + RING * CH].bitcast(BF16).rearrange("p (r a n) -> p r a n", r=RING, a=2)
    qs = w3[:, 4128:4128 + 1024].bitcast(BF16).rearrange("p (b a n) -> p b a n", b=2, a=2)
    summed = w3[:, 5152:5152 + 4 * DH].rearrange("p (t d) -> p t d", t=4)
    rsum = w3[:, 5408:5412].rearrange("p (t a) -> p t a", t=4)
    more = w3[:, 5632:5632 + RING * CH].rearrange("p (r n) -> p r n", r=RING)
    exact = [k.tmp[:, n, :] if n < RING else more[:, n - RING, :] for n in range(2 * RING)]
    acc = [k.psum[:, 4 + 2 * b:6 + 2 * b, :].rearrange("p k (q c) -> p (k q) c", c=CH // 2) for b in range(2)]
    pairs = NC * HEADS // 2
    on_vector = [u for u in range(T) if u % 8 in (0, 4)]
    on_pool = [u for u in range(T) if u not in on_vector]

    def wait_low(eng, g, n, made):
        sig, own, start = (k.lo, on_vector, RING) if n % T in on_vector else (k.aux2, on_pool, 8)
        before = n // T * len(own) + sum(u <= n % T for u in own)
        eng.wait_ge(sig.sem, g * (2 * len(own)) + sig.count(start + before - made))

    with nc.Block() as block:

        @block.gpsimd
        def _(pool):
            pool.sem_inc(k.aux2.sem, 8)
            with pool.Fori(0, pairs) as g:
                for b in range(2):
                    for u in range(T):
                        if u in on_pool:
                            pool.wait_ge(k.hi.sem, g * (2 * len(on_pool)) +
                                         k.hi.count(b * len(on_pool) + on_pool.index(u) + 1))
                            pool.tensor_tensor(probs[:, u % RING, 1, :], exact[u % 8],
                                               probs[:, u % RING, 0, :], ALU.subtract).then_inc(k.aux2.sem, 1)

        @block.sync
        def _(sp):

            def load_counts(i, g):
                sp.dma_start(at[:, 4 * g:4 * g + 4, :], ins["at_dram"][4 * g:4 * g + 4, :, bass.ts(i, CH)]
                             .rearrange("s p n -> p s n")).then_inc(k.atg[g].sem, 16)

            def load_head(i, hp, b):
                sp.wait_ge(k.astep.sem, i * (HEADS * T) + hp * (2 * T) + k.astep.count((b + 1) * T))
                s = k.ring[b].sem
                row = hp * P + b * DH
                kh, kl = (k_dram[a, bass.ds(row, DH), :] for a in range(2))
                sp.dma_start(keys[0:DH, b, 0, :], kh).then_inc(s, 16)
                sp.dma_start(keys[DH:P, b, 0, :], kl).then_inc(s, 16)
                sp.dma_start(keys[0:DH, b, 1, :], kh).then_inc(s, 16)
                qh, ql = (q_dram[a, bass.ds(row, DH), bass.ts(i, CH)] for a in range(2))
                sp.dma_start(qs[0:DH, b, 0, :], qh).then_inc(s, 16)
                sp.dma_start(qs[DH:P, b, 0, :], qh).then_inc(s, 16)
                sp.dma_start(qs[0:DH, b, 1, :], ql).then_inc(s, 16)
                sp.dma_start(qs[DH:DH + 3, b, 1, :], m_dram[:, bass.ds(hp * 2 + b, 1), bass.ts(i, CH)]
                             .rearrange("a h n -> (a h) n")).then_inc(s, 16)
                sp.dma_start(vals[:, b, :, 0:2 * DH], v_dram[bass.ds(hp * 2 + b, 1), :, :, :]
                             .rearrange("h p s d -> p (h s) d")).then_inc(s, 16)

            sp.wait_ge(k.loaded.sem, k.loaded.count(4))
            for b in range(2):
                load_head(0, 0, b)
            for g in range(4):
                load_counts(0, g)

            def other_heads(i):
                with sp.Fori(1, HEADS // 2) as hp:
                    for b in range(2):
                        load_head(i, hp, b)

            with sp.Fori(0, NC - 1) as i:
                other_heads(i)
                for b in range(2):
                    load_head(i + 1, 0, b)
                for g in range(4):
                    sp.wait_ge(k.aux.sem, i * (HEADS * T) + k.aux.count(HEADS * T - T + 4 * g + 4))
                    load_counts(i + 1, g)
            other_heads(NC - 1)

        @block.tensor
        def _(pe):
            pe.sem_inc(k.astep.sem, 2 * T)

            def scores(g, n, b, u):
                if u == 0:
                    pe.wait_ge(k.ring[b].sem, g * 128 + k.ring[b].count(16 + 128 * (1 + n // (2 * T))))
                pe.wait_ge(k.valued.sem, g * (2 * T) + k.valued.count(n + 1))
                pe.matmul(k.bank[u % RING], keys[:, b, 0, u * P:(u + 1) * P], qs[:, b, 0, :], start=True, stop=False)
                pe.matmul(k.bank[u % RING], keys[0:DH + 3, b, 1, u * P:(u + 1) * P], qs[0:DH + 3, b, 1, :],
                          start=False, stop=True).then_inc(k.full.sem, 1)

            def pair(g, last):
                for b in range(2):
                    for u in range(T):
                        n = b * T + u + LEAD
                        if n < 2 * T or not last:
                            scores(g, n, n // T % 2, n % T)
                        if u == 0:
                            pe.wait_ge(k.stat.sem, g * 2 + k.stat.count(b + 1))
                        wait_low(pe, g, b * T + u, 0)
                        for t in range(4):
                            hi, lo = (probs[:, u % RING, a, t * P:(t + 1) * P] for a in range(2))
                            pe.matmul(acc[b][:, t, 0:VALUE_COLS], hi, vals[:, b, u, 0:VALUE_COLS],
                                      start=u == 0 and t % 2 == 0, stop=False, skip_group_check=True)
                            last_one = pe.matmul(acc[b][:, t, DH:VALUE_COLS], lo, vals[:, b, u, DH:VALUE_COLS],
                                                 start=False, stop=u == T - 1, skip_group_check=True)
                        last_one.then_inc(k.astep.sem, 1)

            for u in range(LEAD):
                scores(0, u, 0, u)
            with pe.Fori(0, pairs - 1) as g:
                pair(g, False)
            pair(pairs - 1, True)

        @block.scalar
        def _(act):

            def exponential(g, n):
                u = n % T
                act.wait_ge(k.full.sem, g * (2 * T) + k.full.count(n + 1))
                wait_low(act, g, n, sum((n - s) % T in on_vector for s in range(8)) if u in on_vector else
                         sum((n - s) % T in on_pool for s in range(8)))
                act.activation(exact[u % 8], k.bank[u % RING], ACT.Exp).then_inc(k.valued.sem, 1)

            def pair(g, last):
                for n in range(2 * T):
                    if n + 2 < 2 * T or not last:
                        exponential(g, n + 2)
                    if n % T in on_vector:
                        continue
                    act.wait_ge(k.aux.sem, g * (2 * T) + k.aux.count(n + 1))
                    act.wait_ge(k.astep.sem, g * (2 * T) + k.astep.count(2 * T + n - 3))
                    act.activation(probs[:, n % RING, 0, :], exact[n % 8], ACT.Copy).then_inc(k.hi.sem, 1)

            for n in range(2):
                exponential(0, n)
            with act.Fori(0, pairs - 1) as g:
                pair(g, False)
            pair(pairs - 1, True)

        @block.vector
        def _(dve):
            dve.sem_inc(k.stat.sem, 2)
            for b in range(2):
                dve.memset(keys[64:96, b, 1, :], 1.0).then_inc(k.loaded.sem, 1)
                dve.memset(vals[:, b, :, 2 * DH:], 1.0).then_inc(k.loaded.sem, 1)

            def read_out(g, b, s):
                if s == 0:
                    dve.wait_ge(k.astep.sem, g * (2 * T) + k.astep.count(2 * T + (b + 1) * T))
                    dve.tensor_scalar(rsum, acc[b][:, :, 2 * DH:VALUE_COLS], 1e-16, None, ALU.add
                                      ).then_inc(k.step.sem, 1)
                    dve.tensor_copy(summed, acc[b][:, :, 0:DH]).then_inc(k.step.sem, 1)
                elif s == 1:
                    dve.wait_ge(k.step.sem, g * 8 + k.step.count(b * 4 + 2))
                    dve.reciprocal(rsum, rsum).then_inc(k.step.sem, 1)
                    dve.tensor_tensor(summed, acc[b][:, :, DH:2 * DH], summed, ALU.add).then_inc(k.step.sem, 1)
                else:
                    dve.wait_ge(k.step.sem, g * 8 + k.step.count(b * 4 + 4))
                    dve.tensor_tensor(out[:, bass.ds(g * 2 + b, 1), :, :].rearrange("p h t d -> p (h t) d"), summed,
                                      rsum.to_broadcast([P, 4, DH]), ALU.mult).then_inc(k.stat.sem, 1)

            def pair(i, hp, first=False):
                g = i * (HEADS // 2) + hp
                for b in range(2):
                    for u in range(T):
                        if b == 0 and u % 4 == 0:
                            dve.wait_ge(k.atg[u // 4].sem, i * 16 + k.atg[u // 4].count(16))
                        dve.wait_ge(k.valued.sem, g * (2 * T) + k.valued.count(RING + b * T + u + 1))
                        tile = exact[u % 8]
                        dve.scalar_tensor_tensor(tile, tile, 1e30, at[:, u, :], ALU.min, ALU.mult
                                                 ).then_inc(k.aux.sem, 1)
                        v = u - BEHIND
                        if v in on_vector:
                            dve.wait_ge(k.astep.sem, g * (2 * T) + k.astep.count(2 * T + b * T + v - 3))
                            dve.wait_ge(k.aux.sem, g * (2 * T) + k.aux.count(b * T + v + 1))
                            dve.tensor_copy(probs[:, v % RING, 0, :], exact[v % 8]).then_inc(k.upper.sem, 1)
                            dve.wait_ge(k.upper.sem, g * (2 * len(on_vector)) +
                                        k.upper.count(b * len(on_vector) + on_vector.index(v) + 1))
                            dve.tensor_tensor(probs[:, v % RING, 1, :], exact[v % 8],
                                              probs[:, v % RING, 0, :], ALU.subtract).then_inc(k.lo.sem, 1)
                        if u in (6, 7, 8) and not (first and b == 0):
                            if b == 1:
                                read_out(g, 0, u - 6)
                            else:
                                read_out(g - 1, 1, u - 6)

            pair(0, 0, first=True)
            with dve.Fori(1, HEADS // 2) as hp:
                pair(0, hp)
            with dve.Fori(1, NC) as i:
                with dve.Fori(0, HEADS // 2) as hp:
                    pair(i, hp)
            for s in range(3):
                read_out(pairs - 1, 1, s)

    n = pairs * 2 * T
    done(k, full=n, valued=n, lo=2 * pairs * len(on_vector), aux2=2 * pairs * len(on_pool) + 8, aux=n,
         upper=2 * pairs * len(on_vector), hi=2 * pairs * len(on_pool), astep=n + 2 * T, stat=2 * pairs + 2,
         step=8 * pairs, loaded=4)
    for b in range(2):
        k.ring[b].base += 128 * pairs
    for g in range(4):
        k.atg[g].base += 16 * NC


def batch_norm_stage(k, x, gain, bias, eps, dst=None):
    nc = k.nc
    mv = k.small[:, 4, 0:8].rearrange("p (b s) -> p b s", b=KC)
    scale, shift = k.small[:, 5, 0:KC], k.small[:, 5, KC:2 * KC]
    with nc.Block() as block:

        @block.vector
        def _(dve):
            n = [0]

            def do(ins, wait=True):
                ins.then_inc(k.step.sem, 1)
                n[0] += 1
                if wait:
                    dve.wait_ge(k.step.sem, k.step.count(n[0]))

            for b in range(KC):
                do(dve.bn_aggr(mv[:, b, :], k.moments[:, b * NC:(b + 1) * NC, :].rearrange("p a s -> p (a s)")),
                   b == KC - 1)
            do(dve.tensor_scalar(scale, mv[:, :, 1], eps, None, ALU.add))
            dve.wait_ge(k.hi.sem, k.hi.count(1))
            do(dve.reciprocal(scale, scale))
            do(dve.tensor_tensor(scale, scale, gain, ALU.mult))
            do(dve.tensor_tensor(shift, mv[:, :, 0], scale, ALU.mult))
            do(dve.tensor_tensor(shift, bias, shift, ALU.subtract))
            if dst is not None:
                for b in range(KC):
                    dve.wait_ge(k.valued.sem, k.valued.count(RING + b + 1))
                    dve.tensor_copy(dst[:, b, :], x[:, b, :]).then_inc(k.astep.sem, 1)
                    if b % 2 == 1:
                        dve.wait_ge(k.astep.sem, k.astep.count(b + 1))
                        dve.tensor_tensor(dst[:, KC + b, :], x[:, b, :], dst[:, b, :],
                                          ALU.subtract).then_inc(k.lo.sem, 1)

        @block.scalar
        def _(act):
            act.wait_ge(k.step.sem, k.step.count(KC + 1))
            act.activation(scale, scale, ACT.Sqrt).then_inc(k.hi.sem, 1)
            act.wait_ge(k.step.sem, k.step.count(KC + 5))
            for b in range(KC):
                act.activation(x[:, b, :], x[:, b, :], ACT.Identity, scale=scale[:, b:b + 1],
                               bias=shift[:, b:b + 1]).then_inc(k.valued.sem, 1)

        @block.gpsimd
        def _(pool):
            for b in range(0, KC, 2) if dst is not None else ():
                pool.wait_ge(k.astep.sem, k.astep.count(b + 1))
                pool.tensor_tensor(dst[:, KC + b, :], x[:, b, :], dst[:, b, :], ALU.subtract).then_inc(k.aux.sem, 1)

    done(k, step=KC + 5, hi=1, valued=KC)
    if dst is not None:
        done(k, astep=KC, lo=KC // 2, aux=KC // 2)


def layer1_graph(k):
    ins = k.ins
    x, a, res = k.F(0), k.F(2), k.F32v(1)
    heads_out = k.big[1][:, :].rearrange("p (h t d) -> p h t d", t=4, d=DH)

    def attended_tile(dve, i, j, y, chain):
        return dve.tensor_copy(y.rearrange("p (h d) -> p h d", h=HEADS),
                               heads_out[:, bass.ts(i, HEADS), j, :])

    q_dram, k_dram, v_dram, m_dram = (ins[n] for n in ("q_dram", "k_dram", "v_dram", "m_dram"))
    top = k.small_top
    for layer in range(2):
        col = lambda n, width=KC: k.cols[:, ins["col_index"][n] + width * layer:][:, 0:width]
        wq = use_weight(k)
        bq = col("L1_gnn_bq")
        product_stage(k, lambda i, j: features_out(x, wq, j, i), lambda dve, i, j, ps, y, chain:
                      dve.tensor_scalar(y, ps, bq[:, j:j + 1], DH ** -0.5, ALU.add, ALU.mult), f_halves(k.F(1)))
        wk = use_weight(k)
        kf = k.F(2)
        product_stage(k, lambda i, j: features_out(x, wk, j, i), as_is, f_halves(kf), value_on="scalar",
                      copies=[(q_dram.rearrange("h (b p) n -> p (h b) n", p=P), k.F(1))])
        wv = use_weight(k)
        v = k.TH(3)

        def store_values(i):
            return [(v_dram[:, :, bass.ds(i * RING + j, 1), (1 - a_) * DH:(2 - a_) * DH].rearrange("h p s d -> p h (s d)"),
                     v[:, bass.ds(i * RING + j, 1), a_, :].rearrange("p s (h d) -> p (s h) d", h=HEADS))
                    for j in range(RING) for a_ in range(2)]

        product_stage(k, lambda i, j: tokens_out(x, wv, tile_of(i, j)), as_is, t_halves(v), value_on="scalar",
                      copies=[(k_dram.rearrange("h (b p) n -> p (h b) n", p=P), kf)], trip_store=store_values)
        edge_max_stage(k, q_dram, k_dram, top)
        edge_max_out_stage(k, top, m_dram)
        edge_attention_stage(k, q_dram, k_dram, v_dram, m_dram, heads_out)
        transpose_stage(k, attended_tile, a)
        wo = use_weight(k)
        bo = col("L1_gnn_bo")

        def attended(dve, i, j, ps, y, chain):
            chain(dve.scalar_tensor_tensor(y, ps, bo[:, j:j + 1], x[:, KC + j, bass.ts(i, CH)], ALU.add, ALU.add), 1)
            return dve.tensor_tensor(res[:, j, bass.ts(i, CH)], y, x[:, j, bass.ts(i, CH)], ALU.add)

        chunk_rows = lambda i, j: (i + j * NC, res[:, j, bass.ts(i, CH)])
        product_stage(k, lambda i, j: features_out(a, wo, j, i), attended, steps=2, stats=chunk_rows)
        batch_norm_stage(k, res, col("L1_gnn_g1"), col("L1_gnn_beta1"), EPS, x)
        w1 = use_weight(k)
        f1 = k.F(2)
        product_stage(k, lambda i, j: features_out(x, w1, 0, i), plus_col(col("L1_gnn_b1", 1), relu=True),
                      lambda i, j: (f1[:, 0, bass.ts(i, CH)], f1[:, KC, bass.ts(i, CH)]), width=1)
        w2 = use_weight(k)
        b2 = col("L1_gnn_b2")

        def fed(dve, i, j, ps, y, chain):
            r = res[:, j, bass.ts(i, CH)]
            return dve.scalar_tensor_tensor(r, ps, b2[:, j:j + 1], r, ALU.add, ALU.add)

        def from_f1(i, j):
            hi, lo = f1[:, 0, bass.ts(i, CH)], f1[:, KC, bass.ts(i, CH)]
            whi, wlo = (w2[:, h, 0, j * P:(j + 1) * P] for h in range(2))
            return [(whi, hi), (whi, lo), (wlo, hi)]

        product_stage(k, from_f1, fed, stats=chunk_rows)
        batch_norm_stage(k, res, col("L1_gnn_g2"), col("L1_gnn_beta2"), EPS, x if layer == 0 else None)
    t32 = k.T32(2)
    turn_to_tokens_stage(k, res, t32)
    moments_stage(k, t32, EPS, row_loads(k, "L1_gnn_ln_g", "L1_gnn_ln_b"))
    norm_add_stage(k, t32, k.rows[:, 0, :], k.rows[:, 1, :])


def turn_to_tokens_stage(k, src, dst):
    nc = k.nc
    with nc.Block() as block:

        @block.tensor
        def _(pe):
            for t in range(T):
                pe.wait_ge(k.valued.sem, k.valued.count(t + 1))
                for c in range(KC):
                    last = pe.transpose(k.bank[t % RING][:, c * P:(c + 1) * P], src[:, c, t * P:(t + 1) * P],
                                        k.identf[:, :])
                last.then_inc(k.full.sem, 1)

        @block.vector
        def _(dve):
            for t in range(T):
                dve.wait_ge(k.full.sem, k.full.count(t + 1))
                dve.tensor_copy(dst[:, t, :], k.bank[t % RING]).then_inc(k.valued.sem, 1)

    done(k, full=T, valued=T)



def weights_of(part):
    return {
        "L0_mix": ["L0_mix_Wq", "L0_mix_Wk", "L0_mix_Wv", "L0_mix_Wo", "L0_mix_W1", "L0_mix_W2"],
        "L0_gnn": ["L0_gnn_W_rel1", "L0_gnn_W_root1", "L0_gnn_W_lin1", "L0_gnn_W_rel2", "L0_gnn_W_root2",
                   "L0_gnn_W_lin2"],
        "L0_ffn": ["L0_ffn_Wr", "L0_ffn_W1", "L0_ffn_W2", "L0_ffn_W3"],
        "L1_mix": ["L1_mix_Wk", "L1_mix_Wv", "L1_mix_Wq", "L1_mix_W1", "L1_mix_W2"],
        "L2_gnn": ["L2_gnn_W1", "L2_gnn_W2"],
        "L2_mix": ["L2_mix_Wq", "L2_mix_Wk", "L2_mix_Wv", "L2_mix_out_w"],
        "L3_gnn": ["L3_gnn_W_l", "L3_gnn_W_r"],
        "L3_ffn": [f"L3_ffn_{n}{g}" for g in range(3) for n in ("gate", "up", "down")],
        "L3_mix": ["L3_mix_Wq", "L3_mix_Wk", "L3_mix_Wv", "L3_mix_proj", "L3_mix_Wo", "L3_mix_W1a", "L3_mix_W1b",
                   "L3_mix_W2a", "L3_mix_W2b"],
        "L1_gnn": [f"L1_gnn_{n}{l}" for l in range(2) for n in ("Wq", "Wk", "Wv", "Wo", "W1", "W2")],
        "L1_ffn": ["L1_ffn_W_router", "L1_ffn_W1", "L1_ffn_b2", "L1_ffn_W2"],
        "L2_ffn": ["L2_ffn_w1", "L2_ffn_w2"],
    }.get(part, [])


STAGES = {"graph": graph_stages,
          "L0_mix": layer0_mix, "L0_gnn": layer0_graph, "L0_ffn": layer0_experts,
          "L1_mix": layer1_mix, "L1_gnn": layer1_graph, "L1_ffn": layer1_experts,
          "L2_gnn": layer2_graph, "L2_mix": layer2_mix, "L2_ffn": layer2_experts,
          "L3_mix": layer3_mix, "L3_gnn": layer3_graph, "L3_ffn": layer3_ffn}

PARTS = ["graph",
         "norm", "L0_mix", "L0_gnn", "norm", "L0_ffn",
         "norm", "L1_mix", "L1_gnn", "norm", "L1_ffn",
         "norm", "L2_gnn", "L2_mix", "norm", "L2_ffn",
         "norm", "L3_mix", "L3_gnn", "norm", "L3_ffn"]

STATS_TAKEN = {"L0_gnn": 0, "L0_ffn": 0, "L1_ffn": 0, "L2_mix": 0, "L2_ffn": 1, "L3_gnn": 0}


def entry_copies(k, part):
    if part == "L2_ffn":
        return [*zip(assignments(k), (k.ins["expert_idx"], k.ins["expert_w"]))]
    rows = {"L0_mix": ("L0_mix_bk", "L0_mix_bv", "L0_mix_bo"), "L0_ffn": ("L0_ffn_br",), "L1_ffn": ("L1_ffn_b1",),
            "L2_gnn": ("L2_gnn_b1",)}
    return row_loads(k, *rows.get(part, ()))


def build(nc, ins, out, parts):
    with ExitStack() as ctx:
        k = Core(ctx, nc, ins)
        quantized = lambda n: None if not n.startswith("L3_ffn") else "before" if n == "L3_ffn_gate0" else "by trips"
        k.queue = [weight(ins[n], ins[n].shape[0] // P, quantized(n)) for p in parts for n in weights_of(p)]
        setup_stage(k)
        for n, part in enumerate(parts):
            if part == "norm":
                input_norm(k, STATS_TAKEN.get(parts[n - 1], T), entry_copies(k, parts[n + 1]))
            else:
                STAGES[part](k)
        with nc.Block() as block:

            @block.sync
            def _(sp):
                sp.dma_start(out.rearrange("(t p) d -> p t d", p=P), k.x[:, :, :]).then_inc(k.loaded.sem, 16)
                sp.wait_ge(k.loaded.sem, k.loaded.count(16))



ROWS = ["L0_mix_bk", "L0_mix_bv", "L0_mix_bo", "L0_mix_ln1_scale", "L0_mix_ln1_bias", "L0_mix_b2",
        "L0_mix_ln2_scale", "L0_mix_ln2_bias", "L0_gnn_b_lin2", "L0_ffn_br", "L1_ffn_b1", "L2_gnn_b1", "L2_mix_ln_gamma",
        "L2_mix_ln_beta", "L2_mix_bk", "L2_mix_bv", "L2_mix_out_b", "L3_gnn_gamma", "L3_gnn_beta", "L3_gnn_b_l", "L3_mix_bo", "L3_mix_ln0_g",
        "L3_mix_ln0_b", "L3_mix_b2", "L3_mix_ln1_g", "L3_mix_ln1_b", "L1_gnn_ln_g", "L1_gnn_ln_b"]
COLS = ["L0_mix_bq", "L0_mix_b1", "L0_gnn_b_rel1", "L0_gnn_b_lin1", "L0_gnn_b_rel2", "L2_mix_bq", "L3_mix_b1"] + [
    "L1_gnn_" + n for n in ("bq", "bo", "b1", "b2", "g1", "beta1", "g2", "beta2")]


def lay_out(inputs):
    a = {n: np.asarray(v) for n, v in inputs.items()}
    f32 = np.float32

    def wide(w):
        return np.concatenate([w, np.zeros((w.shape[0], P - w.shape[1]), f32)], 1)

    def tall(w):
        return np.concatenate([w, np.zeros((P - w.shape[0], w.shape[1]), f32)], 0)

    o = {"x": a["x"]}
    for n in ("Wq", "Wk", "Wv"):
        o["L0_mix_" + n] = a["L0_mix_" + n].reshape(D, D)
    o["L0_mix_Wo"] = a["L0_mix_Wo"].reshape(D, D)
    o["L0_mix_W1"] = wide(a["L0_mix_W1"])
    o["L0_mix_W2"] = tall(a["L0_mix_W2"])
    for n in ("rel1", "root1", "lin1", "rel2", "root2", "lin2"):
        o["L0_gnn_W_" + n] = a["L0_gnn_W_" + n].T

    def experts_in(w):
        return w.transpose(1, 0, 2).reshape(D, D)

    o["L0_ffn_Wr"] = a["L0_ffn_Wr"]
    o["L0_ffn_W1"], o["L0_ffn_W2"] = experts_in(a["L0_ffn_W1"]), experts_in(a["L0_ffn_W2"])
    o["L0_ffn_W3"] = a["L0_ffn_W3"].reshape(D, D)
    o["L1_ffn_W_router"] = a["L1_ffn_W_router"]
    o["L1_ffn_W1"], o["L1_ffn_W2"] = experts_in(a["L1_ffn_W1"]), a["L1_ffn_W2"].reshape(D, D)
    o["L1_ffn_b2"] = tall(a["L1_ffn_b2"])
    o["L2_ffn_w1"], o["L2_ffn_w2"] = experts_in(a["L2_ffn_w1"]), a["L2_ffn_w2"].reshape(D, D)
    o["expert_idx"], o["expert_w"] = a["L2_ffn_expert_indices"], a["L2_ffn_expert_weights"]

    for n in ("Wq", "Wk", "Wv", "W2"):
        o["L1_mix_" + n] = a["L1_mix_" + n].T
    o["L1_mix_W1"] = a["L1_mix_W1"]
    o["L2_gnn_W1"] = wide(a["L2_gnn_W1"])
    o["L2_gnn_W2"] = tall(np.concatenate([a["L2_gnn_W2"], a["L2_gnn_b2"][None]], 0))
    a["L2_gnn_b1"] = np.concatenate([a["L2_gnn_b1"], np.ones(1, f32)])
    for n, part in enumerate("qkv"):
        o["L2_mix_W" + part] = a["L2_mix_qkv_w"][n * D:(n + 1) * D].T
        a["L2_mix_b" + part] = a["L2_mix_qkv_b"][n * D:(n + 1) * D]
    o["L2_mix_out_w"] = a["L2_mix_out_w"].T
    for n in ("W_l", "W_r"):
        o["L3_gnn_" + n] = a["L3_gnn_" + n].T
    for g in range(3):
        f = slice(g * D, min(g * D + D, 1408))
        o[f"L3_ffn_gate{g}"], o[f"L3_ffn_up{g}"] = a["L3_ffn_w_gate"][f].T, a["L3_ffn_w_up"][f].T
        o[f"L3_ffn_down{g}"] = a["L3_ffn_w_down"][:, f].T

    for n in ("Wq", "Wk", "Wv", "Wo"):
        o["L3_mix_" + n] = a["L3_mix_" + n]
    o["L3_mix_W1a"], o["L3_mix_W1b"] = a["L3_mix_W1"][:, :D], a["L3_mix_W1"][:, D:]
    o["L3_mix_W2a"], o["L3_mix_W2b"] = a["L3_mix_W2"][:D], a["L3_mix_W2"][D:]
    pj = np.zeros((2, 2, 64, 266), f32)
    pj[0, 0] = pj[1, 1] = a["L3_mix_proj"].T
    o["L3_mix_proj"] = pj.reshape(2 * P, 266)

    for l in range(2):
        for n in ("Wq", "Wk", "Wv", "Wo"):
            o[f"L1_gnn_{n}{l}"] = a["L1_gnn_" + n][l].T
        o[f"L1_gnn_W1{l}"] = wide(a["L1_gnn_W1"][l].T)
        o[f"L1_gnn_W2{l}"] = tall(a["L1_gnn_W2"][l].T)
    a["L1_gnn_b1"] = np.concatenate([a["L1_gnn_b1"], np.zeros((2, 64), f32)], 1)

    def row(v):
        v = v.reshape(-1)
        return np.concatenate([v, np.zeros(D - v.size, f32)])

    def col(v):
        v = v.reshape(-1)
        v = np.concatenate([v, np.zeros(-v.size % P, f32)])
        return v.reshape(-1, P).T

    o["src"], o["dst"] = (a[n].reshape(E // P, P).T for n in ("src", "dst"))
    tile = np.arange(3)[None] * P + np.arange(P)[:, None]
    group = np.minimum(tile // TAKEN, GROUPS - 1)
    block = np.broadcast_to(np.arange(T)[None] * P, (P, T))
    o["edge_consts"] = np.concatenate([group, group - NOWHERE, block, block + P], 1).astype(f32)
    o["iota"] = np.arange(N)[None].astype(np.float16)
    o["rows"] = np.stack([row(a[n]) for n in ROWS])
    cols = [col(a[n]) for n in COLS]
    o["cols"] = np.concatenate(cols, 1)
    at = np.cumsum([0] + [c.shape[1] for c in cols])
    return {n: np.ascontiguousarray(v) for n, v in o.items()}, {n: int(at[i]) for i, n in enumerate(COLS)}


def program(nc, arrays, col_index, parts):
    ins = {n: nc.dram_tensor(f"in_{n}", a.shape, mybir.dt.from_np(a.dtype), kind="ExternalInput").ap()
           for n, a in arrays.items()}
    ins["col_index"] = col_index
    ins["row_index"] = {n: i for i, n in enumerate(ROWS)}
    for n, shape, dt in (("xn_dram", [T, P, D], F32), ("at_dram", [T, P, N], BF16),
                         ("a_dram", [T, P, N], BF16), ("q_dram", [2, D, N], BF16), ("k_dram", [2, D, N], BF16),
                         ("v_dram", [HEADS, P, T, 2 * DH], BF16), ("m_dram", [3, 8, N], BF16)):
        if n not in ins:
            ins[n] = nc.dram_tensor(n, shape, dt, kind="Internal").ap()
    out = nc.dram_tensor("out_0_dram", (N, D), F32, kind="ExternalOutput").ap()
    build(nc, ins, out, parts)


def kernel(**inputs):
    import concourse.bacc as bacc
    from concourse.bass_utils import run_bass_kernel_spmd

    arrays, col_index = lay_out(inputs)
    nc = bacc.Bacc("TRN2", target_bir_lowering=False, num_devices=1)
    program(nc, arrays, col_index, PARTS)
    inputs = {f"in_{n}": a for n, a in arrays.items()}
    return run_bass_kernel_spmd(nc, [inputs], core_ids=[0]).results[0]["out_0_dram"]
```
